# Optimizing a Trainium2 kernel written in Bass

```python
import numpy as np
import jax
import jax.numpy as jnp

def _softmax(x, axis=-1):
    return jax.nn.softmax(x, axis=axis)

def _gelu(x):
    return jax.nn.gelu(x, approximate=True)

def _silu(x):
    return jax.nn.silu(x)

def _sigmoid(x):
    return jax.nn.sigmoid(x)

def _layernorm(x, axis=-1, eps=1e-05):
    m = jnp.mean(x, axis=axis, keepdims=True)
    v = jnp.var(x, axis=axis, keepdims=True)
    return (x - m) / jnp.sqrt(v + eps)

def _scatter_add(tgt, idx, src, axis=0):
    return tgt.at[idx].add(src)

def _segment_sum(src, seg, n):
    return jax.ops.segment_sum(src, seg, n)
kernel_name = 'mk_flamingo_gated_d2_seqx_r4_ebb931'

def setup_inputs(seed: int=0):
    np.random.seed(seed)
    _w = jnp.asarray

    def _rec_inputs():
        import jax
        import jax.numpy as jnp
        _rk = jax.random.key(seed)
        x = -0.000125 + 0.9999 * jax.random.normal(jax.random.fold_in(_rk, 1), (4, 512, 512), jnp.float32)
        _lenS = 512 - jax.random.randint(jax.random.fold_in(_rk, 7), (4,), 0, max(1, 512 // 4) + 1, jnp.int32)
        _lenS2 = 512 - jax.random.randint(jax.random.fold_in(_rk, 8), (4,), 0, max(1, 512 // 4) + 1, jnp.int32)
        fside_BxS2xS2_0 = -3.05549e-07 + 0.0199987 * jax.random.normal(jax.random.fold_in(_rk, 11), (4, 512, 512), jnp.float32)
        _ctx_1024P = jax.random.normal(jax.random.fold_in(_rk, 12), (4, 16, 256), jnp.float32)
        _ctx_1024c = jax.random.dirichlet(jax.random.fold_in(_rk, 512), 0.3 * jnp.ones((16,), jnp.float32), (4, 512))
        _ctx_1024t = jnp.einsum('bsk,bkd->bsd', _ctx_1024c, _ctx_1024P)
        _ctx_1024t = _ctx_1024t * jax.lax.rsqrt(jnp.mean(jnp.square(_ctx_1024t)) + 1e-12) * 0.953939
        ctx_1024 = 6.82029e-06 + 0.0200006 * (_ctx_1024t + 0.3 * jax.random.normal(jax.random.fold_in(_rk, 612), (4, 512, 256), jnp.float32))
        _validS = jnp.arange(512)[None, :] < _lenS[:, None]
        _validS2 = jnp.arange(512)[None, :] < _lenS2[:, None]
        _causal = jnp.tril(jnp.ones((512, 512), dtype=bool))
        mask_BxS2_bf1 = jnp.ones((4, 512), dtype=bool)
        _g = jax.random.normal(jax.random.fold_in(_rk, 9001), (2, 2), jnp.float32)
        _g = jnp.sign(_g) * jnp.maximum(jnp.abs(_g), 1.0) + (_g == 0) * 1.0
        g_xattn = _g[0]
        g_ffn = _g[1]
        return (x, fside_BxS2xS2_0, ctx_1024, mask_BxS2_bf1, g_xattn, g_ffn)
    x, fside_BxS2xS2_0, ctx_1024, mask_BxS2_bf1, g_xattn, g_ffn = _rec_inputs()

    def _L0_xattn_setup():
        import jax, jax.numpy as jnp
        import numpy as np
        EPS = 1e-06
        QMAX = 127.0

        def _smooth_quant_linear(x, w):
            amax_x = jnp.max(jnp.abs(x), axis=0)
            amax_w = jnp.max(jnp.abs(w), axis=0)
            s = jnp.sqrt(jnp.maximum(amax_x, EPS) / jnp.maximum(amax_w, EPS))
            s = jnp.maximum(s, EPS)
            xs = x / s
            ws = w * s
            x_scale = jnp.maximum(jnp.max(jnp.abs(xs), axis=-1, keepdims=True), EPS) / QMAX
            w_scale = jnp.maximum(jnp.max(jnp.abs(ws), axis=-1, keepdims=True), EPS) / QMAX
            x_q = jnp.clip(jnp.round(xs / x_scale), -QMAX, QMAX)
            w_q = jnp.clip(jnp.round(ws / w_scale), -QMAX, QMAX)
            return x_q @ w_q.T * x_scale * w_scale.T

        def _expert_forward(xe, guw, dw):
            h = _smooth_quant_linear(xe, guw)
            gate, up = jnp.split(h, 2, axis=-1)
            a = jax.nn.silu(gate) * up
            return _smooth_quant_linear(a, dw)
        key = jax.random.key(seed)
        k1, k2, k3 = jax.random.split(key, 3)
        E, T, D, I = (8, 512, 512, 256)
        x = jax.random.normal(k1, (E, T, D), dtype=jnp.float32)
        gate_up_weight = jax.random.normal(k2, (E, 2 * I, D), dtype=jnp.float32) * 0.02
        down_weight = jax.random.normal(k3, (E, D, I), dtype=jnp.float32) * 0.02
        return {'x': x, 'gate_up_weight': gate_up_weight, 'down_weight': down_weight}
    _L0_xattn_all = _L0_xattn_setup()
    _L0_xattn_in = {k: v for k, v in _L0_xattn_all.items() if k in ()}
    del _L0_xattn_all

    def _L0_ffn_setup():
        import jax, jax.numpy as jnp
        import numpy as np
        B, S, D, H = (8, 1024, 512, 1280)

        def ternarize_weight(w):
            abs_mean = jnp.maximum(jnp.mean(jnp.abs(w)), 1e-05)
            thr = 0.7 * abs_mean
            one = jnp.ones((), dtype=w.dtype)
            q = jnp.where(w > thr, one, jnp.where(w < -thr, -one, jnp.zeros((), dtype=w.dtype)))
            return w + jax.lax.stop_gradient(q * abs_mean - w)
        key = jax.random.key(seed)
        k1, k2, k3 = jax.random.split(key, 3)
        x = jax.random.normal(k1, (B, S, D), dtype=jnp.float32)
        w_fc = jax.random.normal(k2, (H, D), dtype=jnp.float32) / np.sqrt(D).astype(np.float32)
        w_proj = jax.random.normal(k3, (D, H), dtype=jnp.float32) / np.sqrt(H).astype(np.float32)
        return {'x': x, 'w_fc': w_fc, 'w_proj': w_proj}
    _L0_ffn_all = _L0_ffn_setup()
    _L0_ffn_in = {k: v for k, v in _L0_ffn_all.items() if k in ('w_fc', 'w_proj')}
    del _L0_ffn_all

    def _L1_xattn_setup():
        import jax, jax.numpy as jnp
        import numpy as np
        N_HEADS = 16
        N_KV_HEADS = 8
        HEAD_DIM = 128
        D_TEXT = 512
        D_VISION = 256
        GROUPS = N_HEADS // N_KV_HEADS
        key = jax.random.key(seed)
        ks = jax.random.split(key, 6)
        B, T_text, T_vis = (4, 512, 144)
        text_hidden = jax.random.normal(ks[0], (B, T_text, D_TEXT), dtype=jnp.float32)
        vision_tokens = jax.random.normal(ks[1], (B, T_vis, D_VISION), dtype=jnp.float32)
        vision_mask = jnp.ones((B, T_vis), dtype=bool)
        s = 0.02
        Wq = jax.random.normal(ks[2], (D_TEXT, N_HEADS * HEAD_DIM), dtype=jnp.float32) * s
        Wk = jax.random.normal(ks[3], (D_VISION, N_KV_HEADS * HEAD_DIM), dtype=jnp.float32) * s
        Wv = jax.random.normal(ks[4], (D_VISION, N_KV_HEADS * HEAD_DIM), dtype=jnp.float32) * s
        Wo = jax.random.normal(ks[5], (N_HEADS * HEAD_DIM, D_TEXT), dtype=jnp.float32) * s
        return {'text_hidden': text_hidden, 'vision_tokens': vision_tokens, 'vision_mask': vision_mask, 'Wq': Wq, 'Wk': Wk, 'Wv': Wv, 'Wo': Wo}
    _L1_xattn_all = _L1_xattn_setup()
    _L1_xattn_in = {k: v for k, v in _L1_xattn_all.items() if k in ('Wq', 'Wk', 'Wv', 'Wo')}
    del _L1_xattn_all

    def _L1_ffn_setup():
        import jax, jax.numpy as jnp
        import numpy as np
        E = 8
        TOP_K = 2
        D = 512
        F_E = 2048 // E
        EPS = 1e-06
        SCALE = E / TOP_K
        key = jax.random.key(seed)
        ks = jax.random.split(key, 6)
        B, S = (2, 512)
        std = 0.02
        return {'hidden_states': jax.random.normal(ks[0], (B, S, D), jnp.float32), 'router_w': jax.random.normal(ks[1], (E, D), jnp.float32) * std, 'norm_w': jnp.ones((D,), jnp.float32), 'gate_w': jax.random.normal(ks[2], (E, D, F_E), jnp.float32) * std, 'up_w': jax.random.normal(ks[3], (E, D, F_E), jnp.float32) * std, 'down_w': jax.random.normal(ks[4], (E, F_E, D), jnp.float32) * std}
    _L1_ffn_all = _L1_ffn_setup()
    _L1_ffn_in = {k: v for k, v in _L1_ffn_all.items() if k in ('router_w', 'norm_w', 'gate_w', 'up_w', 'down_w')}
    del _L1_ffn_all
    return {'x': x, 'fside_BxS2xS2_0': fside_BxS2xS2_0, 'ctx_1024': ctx_1024, 'mask_BxS2_bf1': mask_BxS2_bf1, 'g_xattn': g_xattn, 'g_ffn': g_ffn, 'L0_ffn_w_fc': _L0_ffn_in['w_fc'], 'L0_ffn_w_proj': _L0_ffn_in['w_proj'], 'L1_xattn_Wq': _L1_xattn_in['Wq'], 'L1_xattn_Wk': _L1_xattn_in['Wk'], 'L1_xattn_Wv': _L1_xattn_in['Wv'], 'L1_xattn_Wo': _L1_xattn_in['Wo'], 'L1_ffn_router_w': _L1_ffn_in['router_w'], 'L1_ffn_norm_w': _L1_ffn_in['norm_w'], 'L1_ffn_gate_w': _L1_ffn_in['gate_w'], 'L1_ffn_up_w': _L1_ffn_in['up_w'], 'L1_ffn_down_w': _L1_ffn_in['down_w']}

def reference(x, fside_BxS2xS2_0, ctx_1024, mask_BxS2_bf1, g_xattn, g_ffn, L0_ffn_w_fc, L0_ffn_w_proj, L1_xattn_Wq, L1_xattn_Wk, L1_xattn_Wv, L1_xattn_Wo, L1_ffn_router_w, L1_ffn_norm_w, L1_ffn_gate_w, L1_ffn_up_w, L1_ffn_down_w):
    import jax
    import jax.numpy as jnp

    def _L0_xattn_ref(x, gate_up_weight, down_weight):
        import jax, jax.numpy as jnp
        import numpy as np
        EPS = 1e-06
        QMAX = 127.0

        def _smooth_quant_linear(x, w):
            amax_x = jnp.max(jnp.abs(x), axis=0)
            amax_w = jnp.max(jnp.abs(w), axis=0)
            s = jnp.sqrt(jnp.maximum(amax_x, EPS) / jnp.maximum(amax_w, EPS))
            s = jnp.maximum(s, EPS)
            xs = x / s
            ws = w * s
            x_scale = jnp.maximum(jnp.max(jnp.abs(xs), axis=-1, keepdims=True), EPS) / QMAX
            w_scale = jnp.maximum(jnp.max(jnp.abs(ws), axis=-1, keepdims=True), EPS) / QMAX
            x_q = jnp.clip(jnp.round(xs / x_scale), -QMAX, QMAX)
            w_q = jnp.clip(jnp.round(ws / w_scale), -QMAX, QMAX)
            return x_q @ w_q.T * x_scale * w_scale.T

        def _expert_forward(xe, guw, dw):
            h = _smooth_quant_linear(xe, guw)
            gate, up = jnp.split(h, 2, axis=-1)
            a = jax.nn.silu(gate) * up
            return _smooth_quant_linear(a, dw)
        return jax.vmap(_expert_forward)(x, gate_up_weight, down_weight)

    def _L0_ffn_ref(x, w_fc, w_proj):
        import jax, jax.numpy as jnp
        import numpy as np
        B, S, D, H = (8, 1024, 512, 1280)

        def ternarize_weight(w):
            abs_mean = jnp.maximum(jnp.mean(jnp.abs(w)), 1e-05)
            thr = 0.7 * abs_mean
            one = jnp.ones((), dtype=w.dtype)
            q = jnp.where(w > thr, one, jnp.where(w < -thr, -one, jnp.zeros((), dtype=w.dtype)))
            return w + jax.lax.stop_gradient(q * abs_mean - w)
        h = jnp.einsum('bsd,hd->bsh', x, ternarize_weight(w_fc))
        h = jnp.square(jax.nn.relu(h))
        return jnp.einsum('bsh,dh->bsd', h, ternarize_weight(w_proj))

    def _L1_xattn_ref(text_hidden, vision_tokens, vision_mask, Wq, Wk, Wv, Wo):
        import jax, jax.numpy as jnp
        import numpy as np
        N_HEADS = 16
        N_KV_HEADS = 8
        HEAD_DIM = 128
        D_TEXT = 512
        D_VISION = 256
        GROUPS = N_HEADS // N_KV_HEADS
        B, T_text, _ = text_hidden.shape
        T_vis = vision_tokens.shape[1]
        scale = jnp.float32(np.sqrt(HEAD_DIM))
        q = (text_hidden @ Wq).reshape(B, T_text, N_HEADS, HEAD_DIM).transpose(0, 2, 1, 3)
        k = (vision_tokens @ Wk).reshape(B, T_vis, N_KV_HEADS, HEAD_DIM).transpose(0, 2, 1, 3)
        v = (vision_tokens @ Wv).reshape(B, T_vis, N_KV_HEADS, HEAD_DIM).transpose(0, 2, 1, 3)
        k = jnp.repeat(k, GROUPS, axis=1)
        v = jnp.repeat(v, GROUPS, axis=1)
        scores = jnp.einsum('bhtd,bhsd->bhts', q, k) / scale
        mask = vision_mask[:, None, None, :]
        scores = jnp.where(mask, scores, -jnp.inf)
        attn = jax.nn.softmax(scores, axis=-1)
        attn = jnp.nan_to_num(attn, nan=0.0)
        out = jnp.einsum('bhts,bhsd->bhtd', attn, v)
        out = out.transpose(0, 2, 1, 3).reshape(B, T_text, N_HEADS * HEAD_DIM)
        return out @ Wo

    def _L1_ffn_ref(hidden_states, router_w, norm_w, gate_w, up_w, down_w):
        import jax, jax.numpy as jnp
        import numpy as np
        E = 8
        TOP_K = 2
        D = 512
        F_E = 2048 // E
        EPS = 1e-06
        SCALE = E / TOP_K
        B, S, Dm = hidden_states.shape
        T = B * S
        flat = hidden_states.reshape(T, Dm)
        xf = flat.astype(jnp.float32)
        var = jnp.mean(xf * xf, axis=-1, keepdims=True)
        router_in = norm_w * (xf * jax.lax.rsqrt(var + EPS)).astype(flat.dtype)
        logits = router_in @ router_w.T
        probs = jax.nn.softmax(logits, axis=-1)
        topw, topi = jax.lax.top_k(probs, TOP_K)
        topw = topw / jnp.sum(topw, axis=-1, keepdims=True)
        cw = jnp.zeros((T, E), flat.dtype).at[jnp.arange(T)[:, None], topi].add(topw)
        g = jnp.einsum('td,edf->tef', flat, gate_w)
        u = jnp.einsum('td,edf->tef', flat, up_w)
        a = jax.nn.silu(g) * u
        expert_out = jnp.einsum('tef,efd->ted', a, down_w)
        y = jnp.einsum('ted,te->td', expert_out, cw) * SCALE
        return y.reshape(B, S, Dm)
    x = x + jnp.tanh(g_xattn[0]) * _L0_xattn_ref(_layernorm(x, axis=-1), fside_BxS2xS2_0, ctx_1024)
    x = x + jnp.tanh(g_ffn[0]) * _L0_ffn_ref(_layernorm(x, axis=-1), L0_ffn_w_fc, L0_ffn_w_proj)
    x = x + jnp.tanh(g_xattn[1]) * _L1_xattn_ref(_layernorm(x, axis=-1), ctx_1024, mask_BxS2_bf1, L1_xattn_Wq, L1_xattn_Wk, L1_xattn_Wv, L1_xattn_Wo)
    x = x + jnp.tanh(g_ffn[1]) * _L1_ffn_ref(_layernorm(x, axis=-1), L1_ffn_router_w, L1_ffn_norm_w, L1_ffn_gate_w, L1_ffn_up_w, L1_ffn_down_w)
    return x

_drawn_inputs = setup_inputs


def setup_inputs(seed=0):
    import zlib

    import numpy as np

    out = dict(_drawn_inputs(seed))
    spreads = {'g_ffn': (-1.0, 0.6), 'L1_ffn_norm_w': (1.0, 0.6)}
    factors = {'fside_BxS2xS2_0': 3.619,
     'ctx_1024': 3.595,
     'L1_xattn_Wq': 8.0,
     'L1_xattn_Wk': 8.0,
     'L1_xattn_Wv': 8.0,
     'L1_xattn_Wo': 8.0}
    for name, (base, spread) in spreads.items():
        noise = np.random.default_rng([zlib.crc32(name.encode()), seed]).standard_normal(out[name].shape)
        drawn = base * np.exp(spread * noise) if base else spread * noise
        out[name] = jnp.asarray(drawn.astype(out[name].dtype))
    for name, factor in factors.items():
        out[name] = (out[name] * factor).astype(out[name].dtype)
    return out
```

```python
import concourse.bass as bass
from concourse import mybir
from contextlib import ExitStack

FP32 = mybir.dt.float32
FP32R = mybir.dt.float32r
BF16 = mybir.dt.bfloat16
U8 = mybir.dt.uint8
U32 = mybir.dt.uint32
I32 = mybir.dt.int32
ALU = mybir.AluOpType
ACT = mybir.ActivationFunctionType
AX = mybir.AxisListType

P = 128
B, S, D = 4, 512, 512
TT = S // P
DT = D // P
DC = 256
CT = DC // P
IH = DC
HF = 1280
HT = HF // P
NH, NG, DH = 16, 8, 128
NE, FE = 8, 256
FT = FE // P
LN_EPS = 1e-5
Q_EPS = 1e-6
QMAX = 127.0
MAGIC = 1.5 * 2.0 ** 23
MASKED = 1e30
SCALE = float(DH) ** -0.5
MOE_SCALE = 4.0
NPC = 2 * B * TT
ROWS = 256
NTILE = (2 * B * S + NE * (ROWS - 1)) // ROWS
LEAD = 1


class Chain:

    def __init__(self, eng, sem, base):
        self.eng, self.sem, self.base, self.n = eng, sem, base, 0

    def link(self, ins, past=None):
        self.n += 1
        ins.then_inc(self.sem, 1)
        if past is None:
            self.eng.wait_ge(self.sem, self.base + self.n)
        else:
            wait_alone(self.eng, self.sem, self.base + self.n, past)


def wait_alone(eng, sem, value, passed):
    eng.wait_ge(sem, value)
    eng.sem_inc(passed, 1)


def flamingo_gated_kernel(nc, x, fside, ctx_in, mask, g_xattn, g_ffn, w_fc, w_proj,
                          wq, wk, wv, wo, router_w, norm_w, gate_w, up_w, down_w, out, stop="D"):
    V, A, G, T = nc.vector, nc.scalar, nc.gpsimd, nc.tensor
    persistent = ExitStack()
    sems = ExitStack()

    def sem(name):
        return sems.enter_context(nc.semaphore(name))

    def buf(scope, name, shape, dt):
        return scope.enter_context(nc.sbuf_tensor(name, shape, dt))

    xt = buf(persistent, "x_tok", [P, B * TT, D], FP32)
    ident = buf(persistent, "ident", [P, P], FP32)
    identb = buf(persistent, "identb", [P, P], BF16)
    ones = buf(persistent, "ones", [P, P], FP32)
    eps_ln = buf(persistent, "eps_ln", [P, 1], FP32)
    eps_q = buf(persistent, "eps_q", [P, 1], FP32)
    gates_raw = buf(persistent, "gates_raw", [P, 4], FP32)
    gates = buf(persistent, "gates", [P, 4], FP32)
    stats = buf(persistent, "stats", [P, TT, 6], FP32)
    mv = buf(persistent, "mean_var", [P, TT, 2], FP32)
    std = buf(persistent, "std", [P, TT], FP32)
    rstd = buf(persistent, "rstd", [P, TT], FP32)
    xn = buf(persistent, "x_normed", [P, TT, D], FP32)
    ps = persistent.enter_context(nc.psum_tensor("ps", [P, 8, 512], FP32))
    psb = ps[:, :, :].rearrange("p k n -> p (k n)").bitcast(BF16)
    bank_bf = [psb[:, 1024 * k:1024 * (k + 1)] for k in range(8)]

    ab = ExitStack()
    t_fc = buf(ab, "ternary_fc_T", [P, DT, HF], FP32R)
    t_pr = buf(ab, "ternary_proj_T", [P, HT, D], FP32R)
    wabs = buf(ab, "wabs", [P, 2], FP32)
    wmean = buf(ab, "wmean", [P, 2], FP32)
    wthr = buf(ab, "wthr", [P, 2], FP32)
    wnthr = buf(ab, "wnthr", [P, 2], FP32)
    b_shift = buf(ab, "b_norm_shift", [P, TT], FP32)
    h_scale = buf(ab, "h_scale", [P, 1], FP32)
    y_scale = buf(ab, "y_scale", [P, 1], FP32)

    xa = buf(ab, "a_x_normed", [P, TT, D], FP32)
    w1 = buf(ab, "gate_up", [P, TT, D], FP32)
    w2 = buf(ab, "down", [P, TT, DC], FP32)
    ws = buf(ab, "w_smoothed", [P, TT, D], FP32)
    a_stats = buf(ab, "a_stats", [P, TT, 6], FP32)
    a_mv = buf(ab, "a_mean_var", [P, TT, 2], FP32)
    a_std = buf(ab, "a_std", [P, TT], FP32)
    a_rstd = buf(ab, "a_rstd", [P, TT], FP32)
    a_fine = buf(ab, "a_std_refined", [P, TT], FP32)
    cmax = buf(ab, "colmax", [P, 2 * D], FP32)
    cmax2 = buf(ab, "colmax2", [P, 2 * DC], FP32)
    amax = buf(ab, "amax", [P, 8], FP32)
    winv = buf(ab, "w_amax_inv", [P, DT], FP32)
    ratio = buf(ab, "smooth_ratio", [P, DT], FP32)
    smooth = buf(ab, "smooth", [P, DT], FP32)
    refine = buf(ab, "smooth_refined", [P, DT], FP32)
    smooth_inv = buf(ab, "smooth_inv", [P, DT], FP32)
    diag_s = buf(ab, "diag_smooth", [P, DT, P], FP32)
    diag_i = buf(ab, "diag_smooth_inv", [P, DT, P], FP32)
    diag_w = buf(ab, "diag_w_scale", [P, TT, P], FP32)
    s_row = buf(ab, "smooth_row", [P, D], FP32)
    rowmax = buf(ab, "rowmax", [P, TT], FP32)
    xsc = buf(ab, "x_scale", [P, TT], FP32)
    xrq = buf(ab, "x_scale_inv", [P, TT], FP32)
    wrowmax = buf(ab, "w_rowmax", [P, TT], FP32)
    wsc = buf(ab, "w_scale", [P, TT], FP32)
    wrq = buf(ab, "w_scale_inv", [P, TT], FP32)
    wsc_row = buf(ab, "w_scale_row", [P, S], FP32)
    qx = buf(ab, "qx", [P, TT, D], BF16)
    qw = buf(ab, "qw", [P, TT, D], BF16)
    qxT = buf(ab, "qxT", [P, DT, S], BF16)
    qwT = buf(ab, "qwT", [P, DT, S], BF16)
    hh = buf(ab, "h", [P, TT, D], FP32)

    bxh = buf(ab, "b_xT_hi", [P, DT, S], FP32R)
    bxl = buf(ab, "b_xT_lo", [P, DT, S], FP32R)

    pt = ExitStack()
    ternary_raw = buf(pt, "ternary_raw", [P, 5120], FP32)
    ternary_bf = buf(pt, "ternary_values", [P, 5120], BF16)
    pt.close()
    pb = ExitStack()
    relu = [buf(pb, f"relu{i}", [P, S], FP32) for i in range(2)]
    sq = [buf(pb, f"relu_sq{i}", [P, S], FP32) for i in range(2)]
    sqh = [buf(pb, f"relu_sq_hi{i}", [P, S], FP32R) for i in range(2)]
    sql = [buf(pb, f"relu_sq_lo{i}", [P, S], FP32R) for i in range(2)]
    pb.close()
    ab.close()

    pc = ExitStack()
    xTh = buf(pc, "xT_hi", [P, 2, DT, S], FP32R)
    xTl = buf(pc, "xT_lo", [P, 2, DT, S], FP32R)
    ctx_raw = buf(pc, "ctx_raw", [P, 2, TT, DC], FP32)
    cTh = buf(pc, "ctxT_hi", [P, 2, CT, S], FP32R)
    cTl = buf(pc, "ctxT_lo", [P, 2, CT, S], FP32R)
    mask_u8 = buf(pc, "mask_u8", [P, 2, S], U8)
    pen = buf(pc, "penalty", [P, 2, S], FP32)
    valid = buf(pc, "any_valid", [P, 2], FP32)
    y_gate = buf(pc, "y_gate", [P, 2], FP32)
    wq_raw = buf(pc, "wq_raw", [P, DT, 2 * DH], FP32)
    wk_raw = buf(pc, "wk_raw", [P, CT, DH], FP32)
    wv_raw = buf(pc, "wv_raw", [P, CT, DH], FP32)
    wo_raw = buf(pc, "wo_raw", [P, 2, D], FP32)
    wqh = buf(pc, "wq_hi", [P, DT, 2 * DH], FP32R)
    wql = buf(pc, "wq_lo", [P, DT, 2 * DH], FP32R)
    wkh = buf(pc, "wk_hi", [P, CT, DH], FP32R)
    wkl = buf(pc, "wk_lo", [P, CT, DH], FP32R)
    wvh = buf(pc, "wv_hi", [P, CT, DH], FP32R)
    wvl = buf(pc, "wv_lo", [P, CT, DH], FP32R)
    woh = buf(pc, "wo_hi", [P, 2, D], FP32R)
    wol = buf(pc, "wo_lo", [P, 2, D], FP32R)
    kh = [buf(pc, f"kT_hi{i}", [P, S], FP32R) for i in range(2)]
    kl = [buf(pc, f"kT_lo{i}", [P, S], FP32R) for i in range(2)]
    vT = buf(pc, "vT", [P, S], FP32)
    vh = [buf(pc, f"v_hi{i}", [P, TT, DH], FP32R) for i in range(2)]
    vl = [buf(pc, f"v_lo{i}", [P, TT, DH], FP32R) for i in range(2)]
    qh = [buf(pc, f"qT_hi{i}", [P, S], FP32R) for i in range(2)]
    ql = [buf(pc, f"qT_lo{i}", [P, S], FP32R) for i in range(2)]
    sm = [buf(pc, f"masked_scores{i}", [P, S], FP32) for i in range(TT)]
    smax = [buf(pc, f"score_max{i}", [P, TT], FP32) for i in range(2)]
    nbias = [buf(pc, f"neg_max{i}", [P, TT], FP32) for i in range(2)]
    rsum = [buf(pc, f"row_sum{i}", [P, TT], FP32) for i in range(2)]
    rinv = [buf(pc, f"row_sum_inv{i}", [P, TT], FP32) for i in range(2)]
    pr = [buf(pc, f"probs{i}", [P, TT, S], FP32) for i in range(2)]
    pTh = buf(pc, "probsT_hi", [P, TT, S], FP32R)
    pTl = buf(pc, "probsT_lo", [P, TT, S], FP32R)
    oh = [buf(pc, f"oT_hi{i}", [P, S], FP32R) for i in range(2)]
    ol = [buf(pc, f"oT_lo{i}", [P, S], FP32R) for i in range(2)]
    pc.close()

    pd = ExitStack()
    g_raw = buf(pd, "gate_raw", [P, NE, DT, FE], FP32)
    u_raw = buf(pd, "up_raw", [P, NE, DT, FE], FP32)
    d_raw = buf(pd, "down_raw", [P, NE, FT, D], FP32)
    combine = buf(pd, "combine", [P, 2, B * TT], FP32)
    pos_i = buf(pd, "position", [P, 2, B * TT], I32)
    row_tok = buf(pd, "row_token", [P, 2 * NTILE], I32)
    tile_e = buf(pd, "tile_expert", [1, NTILE], I32)
    xg = xn[:, :, :].rearrange("p (i h) d -> p i h d", i=2)
    pr_ = ExitStack()
    dxh = buf(pr_, "d_xT_hi", [P, DT, S], FP32R)
    dxl = buf(pr_, "d_xT_lo", [P, DT, S], FP32R)
    rw_raw = buf(pr_, "router_raw", [NE, D], FP32)
    nw_raw = buf(pr_, "norm_raw", [NE, D], FP32)
    rw = buf(pr_, "router_scaled", [NE, D], FP32)
    rwh = buf(pr_, "router_hi", [P, DT, NE], FP32R)
    rwl = buf(pr_, "router_lo", [P, DT, NE], FP32R)
    junk = buf(pr_, "junk", [P, D], FP32)
    ssq = buf(pr_, "sum_sq", [P, TT], FP32)
    rms = buf(pr_, "rms", [P, TT], FP32)
    rms_inv = buf(pr_, "rms_inv", [P, TT], FP32)
    lgT = buf(pr_, "logitsT", [NE, S], FP32)
    lg = buf(pr_, "logits", [P, TT, NE], FP32)
    lmax = buf(pr_, "logit_max", [P, TT], FP32)
    pe_ = buf(pr_, "router_exp", [P, TT, NE], FP32)
    top = buf(pr_, "top8", [P, TT, 8], FP32)
    topi = buf(pr_, "top8_index", [P, TT, 8], U32)
    topf = buf(pr_, "top8_index_f", [P, TT, 8], FP32)
    den = buf(pr_, "top2_sum", [P, TT], FP32)
    topw = buf(pr_, "top_weight", [P, TT, 2], FP32)
    iota_e = buf(pr_, "iota_e", [P, NE], FP32)
    iota_l = buf(pr_, "iota_lane", [P, P], FP32)
    iota_p = buf(pr_, "iota_partition", [P, 1], FP32)
    iota_j = buf(pr_, "iota_token_tile", [P, 2, B * TT], FP32)
    before = buf(pr_, "before", [P, P], BF16)
    onesb = buf(pr_, "onesb", [P, P], BF16)
    chosen = buf(pr_, "chosen", [P, 2, B * TT, NE], BF16)
    total = buf(pr_, "total", [P, NE, NPC], FP32)
    scan = buf(pr_, "scan", [P, NE, NPC], FP32)
    keep = buf(pr_, "keep", [P, NE, NPC], FP32)
    tiles = buf(pr_, "tiles", [P, NE], FP32)
    tiles_to = buf(pr_, "tiles_to", [P, NE], FP32)
    first = buf(pr_, "first_row", [P, NE], FP32)
    posm = buf(pr_, "position_by_expert", [P, NPC, NE], FP32)
    pos = buf(pr_, "position_f", [P, NPC], FP32)
    posq = buf(pr_, "position_tile", [P, NPC], FP32)
    posr = buf(pr_, "position_lane", [P, NPC], FP32)
    hot_r = buf(pr_, "lane_onehot", [P, NPC, P], BF16)
    hot_q = buf(pr_, "tile_onehot", [P, NPC, 2, 2 * NTILE], BF16)
    texp = buf(pr_, "tile_compare", [1, NTILE, NE], FP32)
    texf = buf(pr_, "tile_expert_f", [1, NTILE], FP32)
    rtok = buf(pr_, "row_token_f", [P, 2 * NTILE], FP32)
    pr_.close()
    pm = ExitStack()
    gwh = [buf(pm, f"gate_hi{i}", [P, DT, FE], FP32R) for i in range(2)]
    gwl = [buf(pm, f"gate_lo{i}", [P, DT, FE], FP32R) for i in range(2)]
    uwh = [buf(pm, f"up_hi{i}", [P, DT, FE], FP32R) for i in range(2)]
    uwl = [buf(pm, f"up_lo{i}", [P, DT, FE], FP32R) for i in range(2)]
    dwh = buf(pm, "down_hi", [P, FT, D], FP32R)
    dwl = buf(pm, "down_lo", [P, FT, D], FP32R)
    gxh = buf(pm, "rowsT_hi", [P, DT, ROWS], FP32R)
    gxl = buf(pm, "rowsT_lo", [P, DT, ROWS], FP32R)
    sg = buf(pm, "silu", [P, FT * ROWS], FP32)
    au = buf(pm, "gated", [P, FT * ROWS], FP32)
    auh = [buf(pm, f"gated_hi{i}", [P, FT, ROWS], FP32R) for i in range(2)]
    aul = [buf(pm, f"gated_lo{i}", [P, FT, ROWS], FP32R) for i in range(2)]
    yrow = [buf(pm, f"expert_rows{i}", [P, D], FP32) for i in range(2)]
    icur = [buf(pm, f"gather_index{i}", [P, 2], I32) for i in range(2)]
    pm.close()
    pf = ExitStack()
    back = [[buf(pf, f"back{i}{c}", [P, D], FP32) for c in range(2)] for i in range(4)]
    pcur = [buf(pf, f"back_index{i}", [P, 2], I32) for i in range(4)]
    pf.close()
    pd.close()
    normed_rows = nc.dram_tensor("normed_rows", (B * S, D), FP32).ap()
    expert_rows = nc.dram_tensor("expert_rows", (NTILE * ROWS, D), FP32).ap()

    s_const = sem("const")
    s_constb = sem("const_vector")
    s_gates_in = sem("gates_in")
    s_gates = sem("gates_tanh")
    s_passed = sem("waits_passed")
    c_dve = sem("chain_vector")
    c_act = sem("chain_scalar")
    c_pool = sem("chain_gpsimd")
    s_var = sem("variance")
    s_std = sem("std")
    s_xin = sem("x_in")
    s_w1in = sem("gate_up_in")
    s_w2in = sem("down_in")
    s_tw_in = sem("ternary_raw_in")
    s_wabs = sem("ternary_abs_sums")
    s_wtot = sem("ternary_totals")
    s_tern = sem("ternary_values")
    s_ternT = sem("ternary_transposed")
    s_ternE = sem("ternary_evicted")
    c_head = sem("chain_vector_head")
    c_main = sem("chain_vector_main")
    s_avar = sem("a_variance")
    s_astd = sem("a_std")
    s_cm = sem("colmax")
    s_cm2 = sem("colmax2")
    s_cmT = sem("colmax_transposed")
    s_ratio = sem("smooth_ratio")
    s_sqrt = sem("smooth_sqrt")
    s_dg = sem("smooth_diagonals")
    s_rows = sem("smooth_rows")
    s_srow = sem("smooth_row_evicted")
    s_ws1 = sem("gate_up_smoothed")
    s_ws2 = sem("down_smoothed")
    s_wrq = sem("w_scale_inverse")
    s_wmg = sem("w_rounded")
    s_qx = sem("x_quantized")
    s_qw = sem("w_quantized")
    s_qxT = sem("x_quantized_transposed")
    s_qwT = sem("w_quantized_transposed")
    s_qxE = sem("x_quantized_evicted")
    s_qwE = sem("w_quantized_evicted")
    s_bc = sem("w_scale_broadcast")
    s_bcE = sem("w_scale_evicted")
    s_mm = sem("quantized_product")
    s_h = sem("product_dequantized")
    s_silu = sem("a_silu")
    s_xadd = sem("a_added")
    s_bnb = sem("b_norm_factors")
    s_bxn = sem("b_normed")
    s_bxt = sem("b_transposed")
    s_bhi = sem("b_xT_hi")
    s_blo = sem("b_xT_lo")
    s_hps = sem("b_hidden")
    s_relu = sem("b_relu")
    s_sq = sem("b_square")
    s_sqh = sem("b_square_hi")
    s_sql = sem("b_square_lo")
    s_yuse = sem("b_square_used")
    s_by = sem("b_product")
    s_bdone = sem("b_added")
    s_cin = sem("c_inputs")
    s_cxn = sem("c_normed")
    s_cxt = sem("c_transposed")
    s_cxh = sem("c_xT_hi")
    s_cxl = sem("c_xT_lo")
    s_cct = sem("c_ctx_transposed")
    s_cch = sem("c_ctxT_hi")
    s_ccl = sem("c_ctxT_lo")
    s_w1raw = sem("c_qkv_weights_in")
    s_w2raw = sem("c_out_weights_in")
    s_w1 = sem("c_qkv_weights_split")
    s_w2 = sem("c_out_weights_split")
    s_kv = sem("c_kv_product")
    s_kh = sem("c_k_hi")
    s_kl = sem("c_k_lo")
    s_vT = sem("c_vT")
    s_vt = sem("c_v_transposed")
    s_vh = sem("c_v_hi")
    s_vl = sem("c_v_lo")
    s_q = sem("c_q_product")
    s_qh = sem("c_q_hi")
    s_ql = sem("c_q_lo")
    s_s = sem("c_scores")
    s_max = [sem(f"c_score_max{i}") for i in range(2)]
    s_nb = sem("c_neg_max")
    s_exp = [sem(f"c_exp{i}") for i in range(TT)]
    s_rinv = sem("c_row_sum_inv")
    s_pn = sem("c_probs_normed")
    s_pt = sem("c_probs_transposed")
    s_pth = sem("c_probsT_hi")
    s_ptl = [sem(f"c_probsT_lo{i}") for i in range(2)]
    s_o = sem("c_attended")
    s_oh = sem("c_oT_hi")
    s_ol = sem("c_oT_lo")
    s_y = sem("c_out_product")
    s_yadd = [sem(f"c_added{i}") for i in range(2)]
    s_din = sem("d_router_in")
    s_rw = sem("d_router_split")
    s_rws = sem("d_router_scaled")
    s_rwT = sem("d_router_transposed")
    s_iota = sem("d_iota")
    s_dxn = sem("d_normed")
    s_ssq = sem("d_sum_sq")
    s_rms = sem("d_rms")
    s_dxt = sem("d_transposed")
    s_dxh = sem("d_xT_hi")
    s_dxl = sem("d_xT_lo")
    s_lgT = sem("d_logitsT")
    s_lgTE = sem("d_logitsT_evicted")
    s_lg = sem("d_logits")
    s_lc = sem("d_logits_centred")
    s_lexp = sem("d_router_exp")
    s_cw = sem("d_chosen")
    s_xst = sem("d_normed_stored")
    s_wraw = sem("d_weights_in")
    s_cnt = sem("d_counts")
    s_hot = sem("d_onehots")
    s_inverted = sem("d_inverted")
    s_plan = sem("d_plan")
    s_icur = sem("d_gather_index")
    s_gat = [sem(f"d_gathered{i}") for i in range(2)]
    s_guhi = sem("d_gate_up_hi")
    s_gulo = sem("d_gate_up_lo")
    s_dhi = sem("d_down_hi")
    s_dns = sem("d_down_split")
    s_gT = sem("d_rows_transposed")
    s_gxh = sem("d_rowsT_hi")
    s_gxl = sem("d_rowsT_lo")
    s_gu = sem("d_gate_up_product")
    s_sg = sem("d_silu")
    s_au = sem("d_gated")
    s_auh = sem("d_gated_hi")
    s_aul = sem("d_gated_lo")
    s_dy = sem("d_product")
    s_yrow = [sem(f"d_rows_evicted{i}") for i in range(2)]
    s_yst = [sem(f"d_rows_stored{i}") for i in range(2)]
    s_pcur = sem("d_back_index")
    s_back = [sem(f"d_back{i}") for i in range(4)]
    s_dadd = sem("d_added")
    s_out = sem("stored")

    xv = x.rearrange("b (n p) d -> (b n) p d", p=P)
    fv = fside.rearrange("b (n p) d -> (b n) p d", p=P)
    cv = ctx_in.rearrange("b (n p) d -> (b n) p d", p=P)
    ov = out.rearrange("b (n p) d -> (b n) p d", p=P)

    block = persistent.enter_context(nc.Block())
    LN_B, LN_C, LN_D = 0, B, 2 * B
    upto = {"A": 1, "B": 2, "C": 3, "D": 4}[stop]

    HEAD_LINKS, MAIN_LINKS, TAIL_LINKS = 15, 26, 7

    F32R_AS_F32 = lambda ap: ap.bitcast(FP32)

    @block.sync
    def _(sp):
        for c, src in enumerate((g_xattn, g_ffn)):
            sp.dma_start(gates_raw[:, 2 * c:2 * c + 2], src.partition_broadcast(P)).then_inc(s_gates_in, 16)
        def load_first(b, first=False):
            if not first:
                sp.wait_ge(s_xin, 16 * b)
            sp.dma_start(xt[:, bass.ds(b * TT, TT), :],
                         xv[bass.ds(b * TT, TT), :, :].rearrange("n p d -> p n d")).then_inc(s_xin, 16)
            sp.wait_ge(s_ws1, LEAD + b)
            sp.dma_start(w1[:, :, :], fv[bass.ds(b * TT, TT), :, :].rearrange("n p d -> p n d")).then_inc(s_w1in, 16)

        def load_second(b):
            sp.wait_ge(s_ws2, LEAD + b)
            sp.dma_start(w2[:, :, :], cv[bass.ds(b * TT, TT), :, :].rearrange("n p d -> p n d")).then_inc(s_w2in, 16)

        load_first(0, first=True)
        load_second(0)
        sp.dma_start(ternary_raw[:, :].rearrange("p (n d) -> p n d", d=D),
                     w_fc.rearrange("(n p) d -> p n d", p=P)).then_inc(s_tw_in, 16)
        load_first(1)
        sp.wait_ge(s_tern, 1)
        sp.dma_start(ternary_raw[:, :].rearrange("p (n d) -> p n d", d=HF),
                     w_proj.rearrange("(n p) d -> p n d", p=P)).then_inc(s_tw_in, 16)
        load_second(1)
        with sp.Fori(2, B) as b:
            load_first(b)
            load_second(b)
        if upto >= 3:
            sp.wait_ge(s_bdone, LEAD + B)

            def load_group(grp, g):
                sp.wait_ge(s_w1, LEAD + grp)
                sp.dma_start(wq_raw[:, :, :], wq.rearrange("(n p) (g c) -> g p n c", p=P, g=NG)[bass.ds(g, 1), :, :, :].rearrange("g p n c -> (g p) n c")).then_inc(s_w1raw, 16)
                sp.dma_start(wk_raw[:, :, :], wk.rearrange("(n p) (g c) -> g p n c", p=P, g=NG)[bass.ds(g, 1), :, :, :].rearrange("g p n c -> (g p) n c")).then_inc(s_w1raw, 16)
                sp.dma_start(wv_raw[:, :, :], wv.rearrange("(n p) (g c) -> g p n c", p=P, g=NG)[bass.ds(g, 1), :, :, :].rearrange("g p n c -> (g p) n c")).then_inc(s_w1raw, 16)
                sp.wait_ge(s_w2, LEAD + grp)
                sp.dma_start(wo_raw[:, :, :], wo.rearrange("(g n p) d -> g p n d", p=P, g=NG)[bass.ds(g, 1), :, :, :].rearrange("g p n d -> (g p) n d")).then_inc(s_w2raw, 16)

            with sp.Fori(0, 2) as bp:
                sp.wait_ge(s_ccl, LEAD + 4 * bp)
                for bl in range(2):
                    sp.dma_start(ctx_raw[:, bl, :, :],
                                 cv[bass.ds((bp * 2 + bl) * TT, TT), :, :].rearrange("n p d -> p n d")).then_inc(s_cin, 16)
                    sp.dma_start(mask_u8[:, bl, :],
                                 mask[bass.ds(bp * 2 + bl, 1), :].broadcast_to([P, S])).then_inc(s_cin, 16)
                with sp.Fori(0, NG) as g:
                    load_group(bp * NG + g, g)
        if upto >= 4:
            sp.wait_ge(s_yadd[1], LEAD + 2 * 2 * NG * 2)
            sp.dma_start(nw_raw[:, :], norm_w.partition_broadcast(NE)).then_inc(s_din, 16)
            sp.dma_start(rw_raw[:, :], router_w).then_inc(s_din, 16)
            with sp.Fori(0, NE) as e:
                for dst, src in ((g_raw, gate_w), (u_raw, up_w), (d_raw, down_w)):
                    sp.dma_start(dst[:, bass.ds(e, 1), :, :].rearrange("p e n f -> p (e n) f"),
                                 src.rearrange("e (n p) f -> e p n f", p=P)[bass.ds(e, 1), :, :, :].rearrange("e p n f -> p (e n) f")).then_inc(s_wraw, 16)
            with sp.Fori(0, B) as b:
                sp.wait_ge(s_dxn, b + 1)
                sp.dma_start(normed_rows[bass.ds(b * S, S), :].rearrange("(n p) d -> p n d", p=P), xn[:, :, :]).then_inc(s_xst, 16)

            with sp.Fori(0, NTILE) as t:
                for h in range(2):
                    sp.wait_ge(s_yrow[h], LEAD + t + 1)
                    sp.dma_start(expert_rows[bass.ds(t * ROWS + h * P, P), :], yrow[h][:, :]).then_inc(s_yst[h], 16)
            with sp.Fori(0, B) as b:
                sp.wait_ge(s_dadd, TT * b + TT)
                sp.dma_start(ov[bass.ds(b * TT, TT), :, :].rearrange("n p d -> p n d"),
                             xt[:, bass.ds(b * TT, TT), :]).then_inc(s_out, 16)
            sp.wait_ge(s_out, 16 * B)
        elif upto == 3:
            sp.wait_ge(s_yadd[1], LEAD + 2 * 2 * NG * 2)
        else:
            sp.wait_ge(s_bdone, LEAD + B)
        if upto < 4:
            sp.dma_start(ov.rearrange("n p d -> p n d"), xt[:, :, :]).then_inc(s_out, 16)
            sp.wait_ge(s_out, 16)

    @block.gpsimd
    def _(pool):
        for last_use in (s_ws1, s_ws2, s_bdone, s_h, s_cmT, s_blo, s_relu, s_w1, s_w2, s_ccl, s_q, s_y, s_cxt, s_dxt, s_ssq, s_cxl, s_dxl, s_ql, s_ol,
                         s_yuse, *s_exp, *s_max, *s_ptl, *s_yadd, *s_yrow):
            pool.sem_inc(last_use, LEAD)
        for last_use in (s_xst, *s_yst):
            pool.sem_inc(last_use, 16 * LEAD)
        G.memset(ident[:, :], 0.0).then_inc(c_pool, 1)
        G.memset(ones[:, :], 1.0)
        pool.wait_ge(c_pool, 1)
        G.affine_select(out=ident[:, :], in_=ident[:, :], compare_op=ALU.not_equal, fill=1.0, base=0,
                        pattern=[[-1, P]], channel_multiplier=1).then_inc(s_const, 1)
        def smoothed(b, k):
            width = (D, DC)[k]
            wait_alone(pool, s_srow, 2 * b + k + 1, s_passed)
            wait_alone(pool, (s_w1in, s_w2in)[k], 16 * b + 16, s_passed)
            G.tensor_tensor(ws[:, :, 0:width], (w1, w2)[k][:, :, :],
                            s_row[:, None, 0:width].broadcast_to([P, TT, width]), ALU.mult).then_inc((s_ws1, s_ws2)[k], 1)

        def rounded(b, k):
            width = (D, DC)[k]
            wait_alone(pool, s_wrq, 2 * b + k + 1, s_passed)
            for j in range(TT):
                ins = G.tensor_scalar(ws[:, j, 0:width], ws[:, j, 0:width], wrq[:, j:j + 1], MAGIC, ALU.mult, ALU.add)
            ins.then_inc(s_wmg, 1)

        def add_product(b):
            for j in range(TT):
                wait_alone(pool, s_h, LEAD + 8 * b + TT + j + 1, s_passed)
                xj = xt[:, bass.ds(b * TT + j, 1), :].rearrange("p o d -> p (o d)")
                G.tensor_tensor(xj, xj, hh[:, j, :], ALU.add).then_inc(s_xadd, 1)

        def square_lo(b, j):
            i = j % 2
            wait_alone(pool, s_sqh, b * HT + j + 1, s_passed)
            G.tensor_tensor(sql[i][:, :], sq[i][:, :], F32R_AS_F32(sqh[i][:, :]), ALU.subtract).then_inc(s_sql, 1)

        def iteration(b, main, feed):
            def slot(j):
                if feed:
                    square_lo(b - 1, j)

            if main:
                smoothed(b, 0)
            slot(0)
            if main:
                rounded(b, 0)
            slot(1)
            slot(2)
            slot(3)
            slot(4)
            slot(5)
            if main:
                smoothed(b, 1)
            slot(6)
            slot(7)
            if main:
                rounded(b, 1)
            slot(8)
            if main:
                add_product(b)
            slot(9)

        iteration(0, True, False)
        with pool.Fori(1, B) as b:
            iteration(b, True, True)
        iteration(B, False, True)
        if upto >= 3:
            CP = 4

            def split(hi, lo, raw, last=None):
                G.tensor_scalar(hi, raw, 1.0, 1.0, ALU.mult, ALU.mult).then_inc(c_pool, 1)
                split.n += 1
                wait_alone(pool, c_pool, split.base + split.n, s_passed)
                ins = G.tensor_tensor(lo, raw, F32R_AS_F32(hi), ALU.subtract)
                if last is not None:
                    ins.then_inc(last, 1)

            def split_qkv(grp):
                split.base, split.n = 1 + grp * 4, 0
                wait_alone(pool, s_w1raw, 48 * grp + 48, s_passed)
                wait_alone(pool, s_q, LEAD + grp * 4, s_passed)
                split(wkh[:, :, :], wkl[:, :, :], wk_raw[:, :, :])
                split(wvh[:, :, :], wvl[:, :, :], wv_raw[:, :, :])
                split(wqh[:, :, :], wql[:, :, :], wq_raw[:, :, :], s_w1)

            def split_out(grp):
                split.base, split.n = 1 + grp * 4 + 3, 0
                wait_alone(pool, s_w2raw, 16 * grp + 16, s_passed)
                wait_alone(pool, s_y, LEAD + grp * 8, s_passed)
                split(woh[:, :, :], wol[:, :, :], wo_raw[:, :, :], s_w2)

            def normalize(n, h):
                for i in range(TT):
                    wait_alone(pool, s_rinv, n * TT + i + 1, s_passed)
                    ins = G.tensor_scalar(pr[h][:, i, :], pr[h][:, i, :], rinv[h][:, i:i + 1], 1.0, ALU.mult, ALU.mult)
                ins.then_inc(s_pn, 1)

            def group(n0, grp, last):
                normalize(n0 + 1, 1)
                normalize(n0 + 2, 0)
                if not last:
                    split_qkv(grp + 1)
                normalize(n0 + 3, 1)
                if not last:
                    normalize(n0 + 4, 0)
                    split_out(grp + 1)

            with pool.Fori(0, 2) as bp:
                split_qkv(bp * NG)
                split_out(bp * NG)
                normalize(bp * (4 * NG), 0)
                with pool.Fori(0, NG - 1) as g:
                    group(bp * (4 * NG) + g * 4, bp * NG + g, False)
                group(bp * (4 * NG) + 4 * (NG - 1), bp * NG + (NG - 1), True)
        if upto >= 4:
            pool.wait_ge(s_yadd[1], LEAD + 2 * 2 * NG * 2)
            small = dict(allow_small_or_imprecise_dtypes=True)
            G.iota(iota_e[:, :], pattern=[[1, NE]], base=0, channel_multiplier=0, **small)
            G.iota(iota_l[:, :], pattern=[[1, P]], base=0, channel_multiplier=0, **small)
            G.iota(iota_p[:, :], pattern=[[0, 1]], base=0, channel_multiplier=1, **small)
            G.iota(iota_j[:, :, :], pattern=[[0, 2], [1, B * TT]], base=0, channel_multiplier=0, **small)
            G.memset(onesb[:, :], 1.0)
            G.memset(keep[:, :, :], 1.0)
            G.memset(before[:, :], 1.0).then_inc(c_pool, 1)
            DP = 1 + 2 * NG * 4 + 1
            pool.wait_ge(c_pool, DP)
            G.memset(keep[:, :, 0:1], 0.0)
            G.affine_select(out=before[:, :], in_=before[:, :], compare_op=ALU.is_gt, fill=0.0, base=0,
                            pattern=[[1, P]], channel_multiplier=-1).then_inc(s_iota, 1)

            def gather(t, i, k, early=False):
                if not early:
                    wait_alone(pool, s_gat[i], 32 * k, s_passed)
                    wait_alone(pool, s_gT, 2 * t - 2, s_passed)
                G.tensor_copy(icur[i][:, :], row_tok[:, bass.ds(2 * t, 2)]).then_inc(s_icur, 1)
                wait_alone(pool, s_icur, t + 1, s_passed)
                for h in range(2):
                    G.indirect_dma_start(xg[:, i, h, :], None, normed_rows,
                                         bass.IndirectOffsetOnAxis(ap=icur[i][:, h:h + 1], axis=0),
                                         bounds_check=B * S - 1).then_inc(s_gat[i], 16)

            def split_down(t):
                e = pool.value_load(tile_e[0:1, bass.ds(t, 1)], min_val=0, max_val=NE - 1)
                wait_alone(pool, s_dhi, t + 1, s_passed)
                G.tensor_tensor(dwl[:, :, :].rearrange("p n d -> p (n d)"),
                                d_raw[:, bass.ds(e, 1), :, :].rearrange("p e n d -> p (e n d)"),
                                F32R_AS_F32(dwh[:, :, :].rearrange("p n d -> p (n d)")), ALU.subtract).then_inc(s_dns, 1)

            pool.wait_ge(s_plan, 1)
            pool.wait_ge(s_xst, 16 * LEAD + 16 * B)
            gather(0, 0, 0, early=True)
            gather(1, 1, 0, early=True)
            pool.wait_ge(s_wraw, 16 * 3 * NE)
            gather(2, 0, 1)
            split_down(0)
            with pool.Fori(0, (NTILE - 3) // 2) as pair:
                for i in range(2):
                    gather(pair * 2 + i + 3, (i + 1) % 2, pair + (i + 3) // 2)
                    split_down(pair * 2 + i + 1)
            for t in range(NTILE - 2, NTILE):
                split_down(t)
            for h in range(2):
                pool.wait_ge(s_yst[h], 16 * LEAD + 16 * NTILE)
            with pool.Fori(0, B) as b:
                for i in range(TT):
                    wait_alone(pool, s_pcur, b * TT + i + 1, s_passed)
                    for c in range(2):
                        G.indirect_dma_start(back[i][c][:, :], None, expert_rows,
                                             bass.IndirectOffsetOnAxis(ap=pcur[i][:, c:c + 1], axis=0),
                                             bounds_check=NTILE * ROWS - 1).then_inc(s_back[i], 16)

    @block.scalar
    def _(act):
        act.wait_ge(s_gates_in, 32)
        A.activation(gates[:, :], gates_raw[:, :], ACT.Tanh).then_inc(s_gates, 1)
        act.wait_ge(s_constb, 1)

        def ln_std(n):
            act.wait_ge(s_var, n + 1)
            A.activation(std[:, :], mv[:, :, 1], ACT.Sqrt, bias=eps_ln[:, :]).then_inc(s_std, 1)

        def a_std_of(b):
            act.wait_ge(s_avar, b + 1)
            A.activation(a_std[:, :], a_mv[:, :, 1], ACT.Sqrt, bias=eps_ln[:, :]).then_inc(s_astd, 1)

        def smooth_root(b, k):
            n = (DT, CT)[k]
            act.wait_ge(s_ratio, 2 * b + k + 1)
            A.activation(smooth[:, 0:n], ratio[:, 0:n], ACT.Sqrt).then_inc(s_sqrt, 1)

        def evict_row(b, k):
            act.wait_ge(s_rows, 2 * b + k + 1)
            if k == 0:
                A.activation(s_row[:, :], ps[:, 2, :], ACT.Copy).then_inc(s_srow, 1)
            else:
                A.activation(s_row[:, 0:DC], ps[:, 3, 0:DC], ACT.Copy).then_inc(s_srow, 1)

        def evict_x(b, k):
            act.wait_ge(s_qxT, 2 * b + k + 1)
            n = (DT, CT)[k]
            A.activation(qxT[:, 0:n, :].rearrange("p n s -> p (n s)"), psb[:, 2048:2048 + n * S], ACT.Copy).then_inc(s_qxE, 1)

        def evict_w(b, k):
            act.wait_ge(s_qwT, 2 * b + k + 1)
            n, c = (DT, CT)[k], (2048, 3072)[k]
            A.activation(qwT[:, 0:n, :].rearrange("p n s -> p (n s)"), psb[:, c:c + n * S], ACT.Copy).then_inc(s_qwE, 1)

        def evict_scale(b, k):
            act.wait_ge(s_bc, 2 * b + k + 1)
            A.activation(wsc_row[:, :], ps[:, 2, :], ACT.Copy).then_inc(s_bcE, 1)

        def a_silu(b):
            act.wait_ge(s_h, LEAD + 8 * b + TT)
            A.activation(hh[:, :, 0:IH], hh[:, :, 0:IH], ACT.Silu).then_inc(s_silu, 1)

        def normed(b):
            act.wait_ge(s_bnb, b + 1)
            for j in range(TT):
                ins = A.activation(xn[:, j, :], xt[:, bass.ds(b * TT + j, 1), :].rearrange("p o d -> p (o d)"),
                                   ACT.Identity, bias=b_shift[:, j:j + 1], scale=rstd[:, j:j + 1])
            ins.then_inc(s_bxn, 1)

        def turned_hi(b):
            for t in range(DT):
                act.wait_ge(s_bxt, b * DT + t + 1)
                A.activation(bxh[:, t, :], ps[:, t % 2, :], ACT.Copy).then_inc(s_bhi, 1)

        def squares(b, j):
            i, k = j % 2, b * HT + j
            act.wait_ge(s_hps, k + 1)
            A.activation(relu[i][:, :], ps[:, i, :], ACT.Relu, scale=h_scale[:, :]).then_inc(s_relu, 1)
            act.wait_ge(s_relu, LEAD + k + 1)
            if j >= 2:
                act.wait_ge(s_yuse, LEAD + k - 1)
            else:
                act.wait_ge(s_yuse, LEAD + b * HT)
            A.activation(sq[i][:, :], relu[i][:, :], ACT.Square).then_inc(s_sq, 1)
            act.wait_ge(s_sq, k + 1)
            A.activation(sqh[i][:, :], sq[i][:, :], ACT.Copy).then_inc(s_sqh, 1)

        def ternary_abs(m):
            act.wait_ge(s_tw_in, 16 * m + 16)
            if m:
                act.wait_ge(s_ternT, DT)
            A.activation(ternary_bf[:, :], ternary_raw[:, :], ACT.Abs, accum_out=wabs[:, m:m + 1]).then_inc(s_wabs, 1)

        def ternary_out(m):
            dst, n_in, n_out = ((t_fc, HT, DT), (t_pr, DT, HT))[m]
            for o in range(n_out):
                k = m * DT + o
                act.wait_ge(s_ternT, k + 1)
                A.activation(dst[:, o, :], psb[:, 4096 + 2048 * (k % 2):4096 + 2048 * (k % 2) + n_in * P], ACT.Copy).then_inc(s_ternE, 1)

        def iteration(b, main, feed, head, tern=False):
            def slot(j):
                if feed:
                    squares(b - 1, j)

            slot(0)
            if tern:
                ternary_abs(0)
            slot(1)
            if main:
                evict_x(b, 0)
            slot(2)
            if main:
                evict_w(b, 0)
                evict_scale(b, 0)
            slot(3)
            if main:
                a_silu(b)
            if tern:
                ternary_out(0)
            slot(4)
            if main:
                smooth_root(b, 1)
            if head:
                a_std_of(b + 1)
            if tern:
                ternary_abs(1)
            slot(5)
            slot(6)
            if main:
                evict_row(b, 1)
            slot(7)
            slot(8)
            if main:
                evict_x(b, 1)
                evict_w(b, 1)
                evict_scale(b, 1)
            slot(9)
            if head:
                smooth_root(b + 1, 0)
            if main:
                ln_std(LN_B + b)
            if head:
                evict_row(b + 1, 0)
            if main:
                normed(b)
                turned_hi(b)
            if tern:
                ternary_out(1)

        a_std_of(0)
        smooth_root(0, 0)
        evict_row(0, 0)
        iteration(0, True, False, True, tern=True)
        with act.Fori(1, B - 1) as b:
            iteration(b, True, True, True)
        iteration(B - 1, True, True, False)
        iteration(B, False, True, False)
        if upto >= 3:
            def exps(n, i, h):
                act.wait_ge(s_nb, n * TT + i + 1)
                A.activation(pr[h][:, i, :], sm[i][:, :], ACT.Exp, bias=nbias[h][:, i:i + 1], scale=SCALE,
                             accum_out=rsum[h][:, i:i + 1]).then_inc(s_exp[i], 1)

            def evict_k(m, bl):
                act.wait_ge(s_kv, 2 * m + 1)
                A.activation(kh[bl][:, :], ps[:, 6, :], ACT.Copy).then_inc(s_kh, 1)
                act.wait_ge(s_kv, 2 * m + 2)
                A.activation(vT[:, :], ps[:, 7, :], ACT.Copy).then_inc(s_vT, 1)

            def evict_v(m, bl):
                act.wait_ge(s_vt, m + 1)
                A.activation(vh[bl][:, :, :].rearrange("p n d -> p (n d)"), ps[:, 7, :], ACT.Copy).then_inc(s_vh, 1)

            def evict_q(n, h):
                act.wait_ge(s_q, LEAD + n + 1)
                A.activation(qh[h][:, :], ps[:, 4, :], ACT.Copy).then_inc(s_qh, 1)

            def group(n0, m0, last):
                for u in range(4):
                    n, h = n0 + u, u % 2
                    for i in range(TT):
                        act.wait_ge(s_pt, n * TT + i + 1)
                        A.activation(pTh[:, i, :], ps[:, 2 + i % 2, :], ACT.Copy).then_inc(s_pth, 1)
                        if not (last and u == 3):
                            exps(n + 1, i, 1 - h)
                    more_q = not (last and u >= 2)
                    if h == 0 and more_q:
                        evict_q(n + 2, h)
                        evict_k(m0 + u // 2 + 1, (u // 2 + 1) % 2)
                    act.wait_ge(s_o, n + 1)
                    A.activation(oh[h][:, :], ps[:, 5, :], ACT.Copy).then_inc(s_oh, 1)
                    if h == 0 and more_q:
                        evict_v(m0 + u // 2 + 1, (u // 2 + 1) % 2)
                    if h == 1 and more_q:
                        evict_q(n + 2, h)

            with act.Fori(0, 2) as bp:
                for bl in range(2):
                    ln_std(LN_C + bp * 2 + bl)
                    for t in range(DT):
                        act.wait_ge(s_cxt, LEAD + (bp * 2 + bl) * DT + t + 1)
                        A.activation(xTh[:, bl, t, :], ps[:, t, :], ACT.Copy).then_inc(s_cxh, 1)
                    for t in range(CT):
                        act.wait_ge(s_cct, (bp * 2 + bl) * CT + t + 1)
                        A.activation(cTh[:, bl, t, :], ps[:, 4 + t, :], ACT.Copy).then_inc(s_cch, 1)
                n0, m0 = bp * (4 * NG), bp * (2 * NG)
                evict_k(m0, 0)
                evict_v(m0, 0)
                evict_q(n0, 0)
                for i in range(TT):
                    exps(n0, i, 0)
                evict_q(n0 + 1, 1)
                with act.Fori(0, NG - 1) as g:
                    group(n0 + g * 4, m0 + g * 2, False)
                group(n0 + 4 * (NG - 1), m0 + 2 * (NG - 1), True)
        if upto >= 4:
            with act.Fori(0, B) as b:
                ln_std(LN_D + b)
                act.wait_ge(s_dxn, b + 1)
                for i in range(TT):
                    if i:
                        act.wait_ge(c_act, b * (TT - 1) + i)
                    ins = A.activation(junk[:, :], xn[:, i, :], ACT.Square, accum_out=ssq[:, i:i + 1])
                    ins.then_inc(c_act if i < TT - 1 else s_ssq, 1)
                act.wait_ge(s_ssq, LEAD + b + 1)
                A.activation(rms[:, :], ssq[:, :], ACT.Sqrt, bias=eps_q[:, :], scale=1.0 / D).then_inc(s_rms, 1)
                for t in range(DT):
                    act.wait_ge(s_dxt, LEAD + b * DT + t + 1)
                    A.activation(dxh[:, t, :], ps[:, t, :], ACT.Copy).then_inc(s_dxh, 1)
                act.wait_ge(s_lgT, b + 1)
                A.activation(lgT[:, :], ps[0:NE, 4, :], ACT.Copy).then_inc(s_lgTE, 1)
                act.wait_ge(s_lc, b + 1)
                A.activation(pe_[:, :, :], lg[:, :, :], ACT.Exp).then_inc(s_lexp, 1)

            def hi_gate_up(t, i, early=False):
                e = act.value_load(tile_e[0:1, bass.ds(t, 1)], min_val=0, max_val=NE - 1)
                if not early:
                    act.wait_ge(s_gu, 2 * t - 2)
                for dst, src in ((gwh[i], g_raw), (uwh[i], u_raw)):
                    A.activation(dst[:, :, :].rearrange("p n f -> p (n f)"),
                                 src[:, bass.ds(e, 1), :, :].rearrange("p e n f -> p (e n f)"), ACT.Copy).then_inc(s_guhi, 1)

            def hi_down(t, early=False):
                e = act.value_load(tile_e[0:1, bass.ds(t, 1)], min_val=0, max_val=NE - 1)
                if not early:
                    act.wait_ge(s_dy, 2 * t)
                A.activation(dwh[:, :, :].rearrange("p n d -> p (n d)"),
                             d_raw[:, bass.ds(e, 1), :, :].rearrange("p e n d -> p (e n d)"), ACT.Copy).then_inc(s_dhi, 1)

            def hi_rows(t):
                for k in range(2):
                    act.wait_ge(s_gT, 2 * t + k + 1)
                    A.activation(gxh[:, 2 * k:2 * k + 2, :].rearrange("p n r -> p (n r)"), ps[:, k, :], ACT.Copy).then_inc(s_gxh, 1)

            def silu(t, i):
                act.wait_ge(s_gu, 2 * t + 1)
                A.activation(sg[:, :], ps[:, 2 + 4 * i, :], ACT.Silu).then_inc(s_sg, 1)

            def hi_gated(t, i):
                act.wait_ge(s_au, t + 1)
                A.activation(auh[i][:, :, :].rearrange("p f r -> p (f r)"), au[:, :], ACT.Copy).then_inc(s_auh, 1)

            def rows_out(t):
                for h in range(2):
                    act.wait_ge(s_dy, 2 * t + h + 1)
                    act.wait_ge(s_yst[h], 16 * LEAD + 16 * t)
                    A.activation(yrow[h][:, :], ps[:, 4 + h, :], ACT.Copy).then_inc(s_yrow[h], 1)

            act.wait_ge(s_plan, 1)
            act.wait_ge(s_wraw, 16 * 3 * NE)
            hi_gate_up(0, 0, early=True)
            hi_rows(0)
            hi_gate_up(1, 1, early=True)
            silu(0, 0)
            hi_rows(1)
            hi_gated(0, 0)
            hi_gate_up(2, 0)
            hi_down(0, early=True)

            def slot(t, i):
                silu(t + 1, 1 - i)
                hi_rows(t + 2)
                hi_gated(t + 1, 1 - i)
                hi_gate_up(t + 3, 1 - i)
                rows_out(t)
                hi_down(t + 1)

            with act.Fori(0, (NTILE - 3) // 2) as pair:
                for i in range(2):
                    slot(pair * 2 + i, i)
            t = NTILE - 3
            silu(t + 1, 1)
            hi_rows(t + 2)
            hi_gated(t + 1, 1)
            rows_out(t)
            hi_down(t + 1)
            silu(t + 2, 0)
            hi_gated(t + 2, 0)
            rows_out(t + 1)
            hi_down(t + 2)
            rows_out(t + 2)

    @block.vector
    def _(dve):
        chain0 = Chain(dve, c_dve, 0)
        V.memset(eps_ln[:, :], LN_EPS)
        V.memset(eps_q[:, :], Q_EPS)
        dve.wait_ge(s_const, 1)
        V.tensor_copy(identb[:, :], ident[:, :]).then_inc(s_constb, 1)

        def norm_stats(ch, tile0, added=None):
            for j in range(TT):
                if added is not None:
                    wait_alone(dve, s_xadd, added + j + 1, s_passed)
                ins = V.bn_stats(stats[:, j, :], xt[:, bass.ds(tile0 + j, 1), :].rearrange("p o d -> p (o d)"))
            ch.link(ins, s_passed)
            for j in range(TT):
                ins = V.bn_aggr(mv[:, j, :], stats[:, j, :])
            ins.then_inc(s_var, 1)

        def norm_apply(ch, tile0, n, done):
            dve.wait_ge(s_std, n + 1)
            ch.link(V.reciprocal(rstd[:, :], std[:, :]))
            for j in range(TT):
                ins = V.tensor_scalar(xn[:, j, :], xt[:, bass.ds(tile0 + j, 1), :].rearrange("p o d -> p (o d)"),
                                      mv[:, j, 0:1], rstd[:, j:j + 1], ALU.subtract, ALU.mult)
            ins.then_inc(done, 1)

        def norm_factors(ch, b):
            dve.wait_ge(s_std, LN_B + b + 1)
            ch.link(V.reciprocal(rstd[:, :], std[:, :]))
            V.scalar_tensor_tensor(b_shift[:, :], mv[:, :, 0], -1.0, rstd[:, :], ALU.mult, ALU.mult).then_inc(s_bnb, 1)

        def layer_norm(ch, tile0, n, done):
            norm_stats(ch, tile0)
            norm_apply(ch, tile0, n, done)

        def head_stats(ch, b):
            wait_alone(dve, s_xin, 16 * b + 16, s_passed)
            for j in range(TT):
                ins = V.bn_stats(a_stats[:, j, :], xt[:, bass.ds(b * TT + j, 1), :].rearrange("p o d -> p (o d)"))
            ch.link(ins, s_passed)
            for j in range(TT):
                ins = V.bn_aggr(a_mv[:, j, :], a_stats[:, j, :])
            ins.then_inc(s_avar, 1)

        def head_norm(ch, b):
            dve.wait_ge(s_astd, b + 1)
            ch.link(V.reciprocal(a_rstd[:, :], a_std[:, :]))
            ch.link(V.scalar_tensor_tensor(a_fine[:, :], a_mv[:, :, 1], LN_EPS, a_rstd[:, :], ALU.add, ALU.mult))
            ch.link(V.tensor_tensor(a_fine[:, :], a_fine[:, :], a_std[:, :], ALU.add))
            ch.link(V.tensor_scalar(a_fine[:, :], a_fine[:, :], 0.5, None, ALU.mult))
            ch.link(V.reciprocal(a_rstd[:, :], a_fine[:, :]))
            for j in range(TT):
                ins = V.tensor_scalar(xa[:, j, :], xt[:, bass.ds(b * TT + j, 1), :].rearrange("p o d -> p (o d)"),
                                      a_mv[:, j, 0:1], a_rstd[:, j:j + 1], ALU.subtract, ALU.mult)
            ch.link(ins)

        def head_colmax_w(b, first=False):
            if not first:
                dve.wait_ge(s_cmT, LEAD + 2 * b - 1)
            wait_alone(dve, s_w1in, 16 * b + 16, s_passed)
            V.tensor_reduce(cmax[:, 0:D], w1[:, :, :].rearrange("p n d -> p d n"), AX.X,
                            ALU.max, apply_absolute_value=True).then_inc(s_cm, 1)

        def down_colmax(b):
            wait_alone(dve, s_w2in, 16 * b + 16, s_passed)
            V.tensor_reduce(cmax2[:, 0:DC], w2[:, :, :].rearrange("p n d -> p d n"), AX.X,
                            ALU.max, apply_absolute_value=True)

        def head_colmax_x(ch, b):
            V.tensor_reduce(cmax[:, D:], xa[:, :, :].rearrange("p n d -> p d n"), AX.X,
                            ALU.max, apply_absolute_value=True).then_inc(s_cm, 1)

        def smooth_ratio(ch, b, k):
            n = (DT, CT)[k]
            dve.wait_ge(s_cmT, LEAD + 2 * b + k + 1)
            ch.link(V.tensor_reduce(amax[:, 0:2 * n], ps[:, 2:4, :].rearrange("p k (n c) -> p (k n) c", c=P)[:, 0:2 * n, :],
                                    AX.X, ALU.max, apply_absolute_value=True))
            ch.link(V.tensor_scalar(amax[:, 0:2 * n], amax[:, 0:2 * n], Q_EPS, None, ALU.max))
            ch.link(V.reciprocal(winv[:, 0:n], amax[:, 0:n]))
            V.tensor_tensor(ratio[:, 0:n], amax[:, n:2 * n], winv[:, 0:n], ALU.mult).then_inc(s_ratio, 1)

        def smooth_diagonals(ch, b, k):
            n = (DT, CT)[k]
            dve.wait_ge(s_sqrt, 2 * b + k + 1)
            ch.link(V.reciprocal(refine[:, 0:n], smooth[:, 0:n]))
            ch.link(V.tensor_tensor(refine[:, 0:n], refine[:, 0:n], ratio[:, 0:n], ALU.mult))
            ch.link(V.tensor_tensor(smooth[:, 0:n], smooth[:, 0:n], refine[:, 0:n], ALU.add))
            ch.link(V.tensor_scalar(smooth[:, 0:n], smooth[:, 0:n], 0.5, Q_EPS, ALU.mult, ALU.max))
            ch.link(V.reciprocal(smooth_inv[:, 0:n], smooth[:, 0:n]))
            eye = ident[:, None, :].broadcast_to([P, n, P])
            V.tensor_tensor(diag_s[:, 0:n, :], eye, smooth[:, 0:n, None].broadcast_to([P, n, P]), ALU.mult)
            V.tensor_tensor(diag_i[:, 0:n, :], eye, smooth_inv[:, 0:n, None].broadcast_to([P, n, P]),
                            ALU.mult).then_inc(s_dg, 1)

        def quantize_x(ch, b, k, x_):
            for j in range(TT):
                ins = V.tensor_scalar(x_[:, j, :], x_[:, j, :], xrq[:, j:j + 1], MAGIC, ALU.mult, ALU.add)
            ch.link(ins)

        def smooth_x(ch, b, k, x_):
            width = (D, DC)[k]
            inv_row = (ps[:, 3, None, :], ps[:, 2, None, 0:DC])[k]
            wait_alone(dve, s_rows, 2 * b + k + 1, s_passed)
            ch.link(V.tensor_tensor(x_, x_, inv_row.broadcast_to([P, TT, width]), ALU.mult))
            ch.link(V.tensor_reduce(rowmax[:, :], x_, AX.X, ALU.max, apply_absolute_value=True))
            ch.link(V.tensor_scalar(xsc[:, :], rowmax[:, :], Q_EPS, 1.0 / QMAX, ALU.max, ALU.mult))
            ch.link(V.reciprocal(xrq[:, :], xsc[:, :]))

        def integers_x(k, x_):
            V.tensor_scalar(qx[:, :, 0:(D, DC)[k]], x_, -MAGIC, QMAX, ALU.add, ALU.min).then_inc(s_qx, 1)

        def scale_w(ch, b, k):
            width = (D, DC)[k]
            wait_alone(dve, (s_ws1, s_ws2)[k], LEAD + b + 1, s_passed)
            ch.link(V.tensor_reduce(wrowmax[:, :], ws[:, :, 0:width], AX.X, ALU.max, apply_absolute_value=True))
            ch.link(V.tensor_scalar(wsc[:, :], wrowmax[:, :], Q_EPS, 1.0 / QMAX, ALU.max, ALU.mult))
            V.reciprocal(wrq[:, :], wsc[:, :]).then_inc(s_wrq, 1)

        def scale_diagonal():
            V.tensor_tensor(diag_w[:, :, :], ident[:, None, :].broadcast_to([P, TT, P]),
                            wsc[:, :, None].broadcast_to([P, TT, P]), ALU.mult)

        def quantize_w(b, k):
            width = (D, DC)[k]
            dve.wait_ge(s_wmg, 2 * b + k + 1)
            V.tensor_scalar(qw[:, :, 0:width], ws[:, :, 0:width], -MAGIC, QMAX, ALU.add, ALU.min).then_inc(s_qw, 1)

        def dequantize(b, k):
            dve.wait_ge(s_bcE, 2 * b + k + 1)
            for j in range(TT):
                dve.wait_ge(s_mm, 8 * b + k * TT + j + 1)
                V.scalar_tensor_tensor(hh[:, j, :], ps[:, 3 - j % 2, :], xsc[:, j:j + 1], wsc_row[:, :],
                                       ALU.mult, ALU.mult).then_inc(s_h, 1)

        def gated_product(ch, b):
            dve.wait_ge(s_silu, b + 1)
            ch.link(V.tensor_tensor(hh[:, :, 0:IH], hh[:, :, 0:IH], hh[:, :, IH:], ALU.mult))
            V.tensor_reduce(cmax2[:, DC:], hh[:, :, 0:IH].rearrange("p n d -> p d n"), AX.X,
                            ALU.max, apply_absolute_value=True).then_inc(s_cm2, 1)

        def turned_lo(b):
            for t in range(DT):
                dve.wait_ge(s_bhi, b * DT + t + 1)
                V.tensor_tensor(bxl[:, t, :], ps[:, t % 2, :], F32R_AS_F32(bxh[:, t, :]), ALU.subtract).then_inc(s_blo, 1)

        def add_feed(b):
            dve.wait_ge(s_by, b + 1)
            for j in range(TT):
                xj = xt[:, bass.ds(b * TT + j, 1), :].rearrange("p o d -> p (o d)")
                ins = V.scalar_tensor_tensor(xj, ps[:, 4 + j, :], y_scale[:, :], xj, ALU.mult, ALU.add)
            ins.then_inc(s_bdone, 1)

        def ternary_threshold(m):
            ch = Chain(dve, c_dve, m * 4)
            dve.wait_ge(s_wtot, m + 1)
            ch.link(V.tensor_scalar(wmean[:, m:m + 1], ps[:, 7, m:m + 1], 1.0 / (HF * D), 1e-5, ALU.mult, ALU.max))
            ch.link(V.tensor_scalar(wthr[:, m:m + 1], wmean[:, m:m + 1], 0.7, None, ALU.mult))
            ch.link(V.tensor_scalar(wnthr[:, m:m + 1], wthr[:, m:m + 1], -1.0, None, ALU.mult))

        def ternary(m):
            ch = Chain(dve, c_dve, m * 4 + 3)
            ch.link(V.tensor_scalar(ternary_bf[:, :], ternary_raw[:, :], wnthr[:, m:m + 1], None, ALU.is_lt))
            V.scalar_tensor_tensor(ternary_bf[:, :], ternary_raw[:, :], wthr[:, m:m + 1], ternary_bf[:, :],
                                   ALU.is_gt, ALU.subtract).then_inc(s_tern, 1)

        def iteration(b, main, feed, ahead, tern=False):
            if main:
                ch = Chain(dve, c_main, b * MAIN_LINKS)
                hd = Chain(dve, c_head, (b + 1) * HEAD_LINKS)
                ch.n = TAIL_LINKS
                integers_x(0, xa[:, :, :])
                if tern:
                    ternary_threshold(0)
                scale_diagonal()
                if ahead:
                    head_stats(hd, b + 1)
                quantize_w(b, 0)
                if ahead:
                    head_colmax_w(b + 1)
                if tern:
                    ternary(0)
                dequantize(b, 0)
                down_colmax(b)
                gated_product(ch, b)
                smooth_ratio(ch, b, 1)
                smooth_diagonals(ch, b, 1)
                if ahead:
                    head_norm(hd, b + 1)
                if tern:
                    ternary_threshold(1)
                smooth_x(ch, b, 1, hh[:, :, 0:DC])
                quantize_x(ch, b, 1, hh[:, :, 0:DC])
                scale_w(ch, b, 1)
                integers_x(1, hh[:, :, 0:DC])
                scale_diagonal()
                ch.link(V.tensor_scalar(xsc[:, :], xsc[:, :], gates[:, 0:1], None, ALU.mult))
                quantize_w(b, 1)
                if ahead:
                    head_colmax_x(hd, b + 1)
                dequantize(b, 1)
                if ahead:
                    smooth_ratio(hd, b + 1, 0)
                norm_stats(ch, b * TT, added=b * TT)
                if ahead:
                    smooth_diagonals(hd, b + 1, 0)
                    assert hd.n == HEAD_LINKS, hd.n
                norm_factors(ch, b)
                if tern:
                    ternary(1)
                    V.tensor_copy(h_scale[:, :], wmean[:, 0:1])
                    V.tensor_scalar(y_scale[:, :], wmean[:, 1:2], gates[:, 2:3], None, ALU.mult)
                assert ch.n == MAIN_LINKS, ch.n
                if ahead:
                    ch = Chain(dve, c_main, (b + 1) * MAIN_LINKS)
                    smooth_x(ch, b + 1, 0, xa[:, :, :])
                turned_lo(b)
                if ahead:
                    quantize_x(ch, b + 1, 0, xa[:, :, :])
                    scale_w(ch, b + 1, 0)
                    assert ch.n == TAIL_LINKS, ch.n
            if feed:
                add_feed(b - 1)

        dve.wait_ge(s_gates, 1)
        hd = Chain(dve, c_head, 0)
        head_stats(hd, 0)
        head_colmax_w(0, first=True)
        head_norm(hd, 0)
        head_colmax_x(hd, 0)
        smooth_ratio(hd, 0, 0)
        smooth_diagonals(hd, 0, 0)
        ch = Chain(dve, c_main, 0)
        smooth_x(ch, 0, 0, xa[:, :, :])
        quantize_x(ch, 0, 0, xa[:, :, :])
        scale_w(ch, 0, 0)
        iteration(0, True, False, True, tern=True)
        with dve.Fori(1, B - 1) as b:
            iteration(b, True, True, True)
        iteration(B - 1, True, True, False)
        iteration(B, False, True, False)
        dve.wait_ge(s_bdone, LEAD + B)
        base = 8

        if upto >= 3:
            def row_max(n, i, h, bl):
                dve.wait_ge(s_exp[i], LEAD + n)
                wait_alone(dve, s_s, n * TT + i + 1, s_passed)
                V.tensor_tensor_reduce(out=sm[i][:, :], in0=ps[:, i % 2, :], in1=pen[:, bl, :], scale=1.0,
                                       scalar=-3.0e38, op0=ALU.add, op1=ALU.max,
                                       accum_out=smax[h][:, i:i + 1]).then_inc(s_max[i % 2], 1)
                dve.wait_ge(s_max[i % 2], LEAD + n * 2 + i // 2 + 1)
                V.tensor_scalar(nbias[h][:, i:i + 1], smax[h][:, i:i + 1], -SCALE, None, ALU.mult).then_inc(s_nb, 1)

            def lo_k(m, bl):
                dve.wait_ge(s_kh, m + 1)
                V.tensor_tensor(kl[bl][:, :], ps[:, 6, :], F32R_AS_F32(kh[bl][:, :]), ALU.subtract).then_inc(s_kl, 1)

            def lo_v(m, bl):
                dve.wait_ge(s_vh, m + 1)
                V.tensor_tensor(vl[bl][:, :, :].rearrange("p n d -> p (n d)"), ps[:, 7, :],
                                F32R_AS_F32(vh[bl][:, :, :].rearrange("p n d -> p (n d)")), ALU.subtract).then_inc(s_vl, 1)

            def lo_q(n, h):
                dve.wait_ge(s_qh, n + 1)
                V.tensor_tensor(ql[h][:, :], ps[:, 4, :], F32R_AS_F32(qh[h][:, :]), ALU.subtract).then_inc(s_ql, 1)

            def inverse_sum(n, i, h):
                dve.wait_ge(s_exp[i], LEAD + n + 1)
                V.reciprocal(rinv[h][:, i:i + 1], rsum[h][:, i:i + 1]).then_inc(s_rinv, 1)

            def group(bp, n0, m0, last):
                for u in range(4):
                    n, bl, h = n0 + u, u // 2, u % 2
                    more_s, more_q = not (last and u == 3), not (last and u >= 2)
                    for i in range(TT):
                        if more_s:
                            row_max(n + 1, i, 1 - h, ((u + 1) // 2) % 2)
                        dve.wait_ge(s_pth, n * TT + i + 1)
                        V.tensor_tensor(pTl[:, i, :], ps[:, 2 + i % 2, :], F32R_AS_F32(pTh[:, i, :]),
                                        ALU.subtract).then_inc(s_ptl[i % 2], 1)
                        if more_s and i:
                            inverse_sum(n + 1, i - 1, 1 - h)
                    if more_s:
                        inverse_sum(n + 1, TT - 1, 1 - h)
                    if h == 0 and more_q:
                        lo_q(n + 2, h)
                        lo_k(m0 + u // 2 + 1, (u // 2 + 1) % 2)
                    dve.wait_ge(s_oh, n + 1)
                    V.tensor_tensor(ol[h][:, :], ps[:, 5, :], F32R_AS_F32(oh[h][:, :]), ALU.subtract).then_inc(s_ol, 1)
                    if h == 0 and more_q:
                        lo_v(m0 + u // 2 + 1, (u // 2 + 1) % 2)
                    if h == 1 and more_q:
                        lo_q(n + 2, h)
                    if h == 1:
                        m = m0 + bl
                        for j in range(TT):
                            dve.wait_ge(s_y, LEAD + m * TT + j + 1)
                            xj = xt[:, bass.ds((bp * 2 + bl) * TT + j, 1), :].rearrange("p o d -> p (o d)")
                            V.scalar_tensor_tensor(xj, ps[:, 6 + j % 2, :], y_gate[:, bl:bl + 1], xj,
                                                   ALU.mult, ALU.add).then_inc(s_yadd[j % 2], 1)
                        dve.wait_ge(s_yadd[1], LEAD + m * 2 + 2)

            with dve.Fori(0, 2) as bp:
                ch = Chain(dve, c_dve, base + bp * 7)
                for bl in range(2):
                    b = bp * 2 + bl
                    dve.wait_ge(s_cxt, LEAD + b * DT)
                    layer_norm(ch, b * TT, LN_C + b, s_cxn)
                    for t in range(DT):
                        dve.wait_ge(s_cxh, b * DT + t + 1)
                        V.tensor_tensor(xTl[:, bl, t, :], ps[:, t, :], F32R_AS_F32(xTh[:, bl, t, :]),
                                        ALU.subtract).then_inc(s_cxl, 1)
                    for t in range(CT):
                        dve.wait_ge(s_cch, b * CT + t + 1)
                        V.tensor_tensor(cTl[:, bl, t, :], ps[:, 4 + t, :], F32R_AS_F32(cTh[:, bl, t, :]),
                                        ALU.subtract).then_inc(s_ccl, 1)
                dve.wait_ge(s_cin, bp * 64 + 64)
                ch.link(V.tensor_scalar(pen[:, :, :], mask_u8[:, :, :], MASKED, -MASKED, ALU.mult, ALU.add))
                ch.link(V.tensor_reduce(valid[:, :], mask_u8[:, :, :], AX.X, ALU.max))
                ch.link(V.tensor_scalar(y_gate[:, :], valid[:, :], gates[:, 1:2], None, ALU.mult))
                n0, m0 = bp * (4 * NG), bp * (2 * NG)
                lo_k(m0, 0)
                lo_v(m0, 0)
                lo_q(n0, 0)
                for i in range(TT):
                    row_max(n0, i, 0, 0)
                for i in range(TT):
                    inverse_sum(n0, i, 0)
                lo_q(n0 + 1, 1)
                with dve.Fori(0, NG - 1) as g:
                    group(bp, n0 + g * 4, m0 + g * 2, False)
                group(bp, n0 + 4 * (NG - 1), m0 + 2 * (NG - 1), True)
            assert ch.n == 7, ch.n
            base += 14

        if upto >= 4:
            ch = Chain(dve, c_dve, base)
            dve.wait_ge(s_din, 32)
            V.tensor_tensor(rw[:, :], rw_raw[:, :], nw_raw[:, :], ALU.mult).then_inc(s_rws, 1)
            dve.wait_ge(s_rwT, 1)
            rwT = ps[:, 5, 0:DT * NE].rearrange("p (n e) -> p n e", e=NE)
            ch.link(V.tensor_copy(rwh[:, :, :], rwT))
            V.tensor_tensor(rwl[:, :, :], rwT, F32R_AS_F32(rwh[:, :, :]), ALU.subtract).then_inc(s_rw, 1)
            base += 1
            dve.wait_ge(s_iota, 1)
            with dve.Fori(0, B) as b:
                ch = Chain(dve, c_dve, base + b * 10)
                dve.wait_ge(s_dxt, LEAD + b * DT)
                dve.wait_ge(s_ssq, LEAD + b)
                dve.wait_ge(s_xst, 16 * LEAD + 16 * b)
                layer_norm(ch, b * TT, LN_D + b, s_dxn)
                for t in range(DT):
                    dve.wait_ge(s_dxh, b * DT + t + 1)
                    V.tensor_tensor(dxl[:, t, :], ps[:, t, :], F32R_AS_F32(dxh[:, t, :]),
                                    ALU.subtract).then_inc(s_dxl, 1)
                dve.wait_ge(s_rms, b + 1)
                ch.link(V.reciprocal(rms_inv[:, :], rms[:, :]))
                dve.wait_ge(s_lg, b + 1)
                ch.link(V.tensor_tensor(lg[:, :, :], ps[:, 5, 0:TT * NE].rearrange("p (n e) -> p n e", e=NE),
                                        rms_inv[:, :, None].broadcast_to([P, TT, NE]), ALU.mult))
                ch.link(V.tensor_reduce(lmax[:, :], lg[:, :, :], AX.X, ALU.max))
                V.tensor_tensor(lg[:, :, :], lg[:, :, :], lmax[:, :, None].broadcast_to([P, TT, NE]),
                                ALU.subtract).then_inc(s_lc, 1)
                wait_alone(dve, s_lexp, b + 1, s_passed)
                for i in range(TT):
                    ins = V.max(top[:, i, :], pe_[:, i, :])
                ch.link(ins, s_passed)
                for i in range(TT):
                    ins = V.max_index(topi[:, i, :], top[:, i, :], pe_[:, i, :])
                ch.link(V.tensor_tensor(den[:, :], top[:, :, 0], top[:, :, 1], ALU.add))
                ch.link(V.tensor_copy(topf[:, :, :], topi[:, :, :]))
                ch.link(V.reciprocal(den[:, :], den[:, :]))
                ch.link(V.tensor_tensor(topw[:, :, :], top[:, :, 0:2], den[:, :, None].broadcast_to([P, TT, 2]), ALU.mult))
                for c in range(2):
                    V.tensor_tensor(chosen[:, c, bass.ds(b * TT, TT), :], iota_e[:, None, :].broadcast_to([P, TT, NE]),
                                    topf[:, :, c:c + 1].broadcast_to([P, TT, NE]), ALU.is_equal)
                for c in range(2):
                    ins = V.tensor_scalar(combine[:, c, bass.ds(b * TT, TT)], topw[:, :, c], gates[:, 3:4], MOE_SCALE,
                                          ALU.mult, ALU.mult)
                ins.then_inc(s_cw, 1)
                dve.wait_ge(s_cw, b + 1)
            assert ch.n == 10, ch.n
            ch = Chain(dve, c_dve, base + B * 10)

            dve.wait_ge(s_cnt, 1)
            flat = lambda ap: ap.rearrange("p e k -> p (e k)")
            ch.link(V.tensor_copy(total[:, :, :], ps[:, 1, 0:NPC * NE].rearrange("p (k e) -> p e k", e=NE)))
            ch.link(V.tensor_tensor_scan(flat(scan[:, :, :]), flat(keep[:, :, :]), flat(total[:, :, :]), 0.0,
                                         ALU.mult, ALU.add))
            ch.link(V.tensor_scalar(tiles[:, :], scan[:, :, NPC - 1], 1.0 / ROWS, (ROWS - 1.0) / ROWS - 0.498,
                                    ALU.mult, ALU.add))
            ch.link(V.tensor_scalar(tiles[:, :], tiles[:, :], MAGIC, -MAGIC, ALU.add, ALU.add))
            ch.link(V.tensor_tensor_scan(tiles_to[:, :], ones[:, 0:NE], tiles[:, :], 0.0, ALU.mult, ALU.add))
            ch.link(V.tensor_tensor(first[:, :], tiles_to[:, :], tiles[:, :], ALU.subtract))
            ch.link(V.tensor_scalar(first[:, :], first[:, :], float(ROWS), None, ALU.mult))
            ch.link(V.tensor_tensor(scan[:, :, :], scan[:, :, :], total[:, :, :], ALU.subtract))
            ch.link(V.tensor_tensor(scan[:, :, :], scan[:, :, :], first[:, :, None].broadcast_to([P, NE, NPC]), ALU.add))
            ch.link(V.tensor_tensor(posm[:, :, :], ps[:, 0, 0:NPC * NE].rearrange("p (k e) -> p k e", e=NE),
                                    scan[:, :, :].rearrange("p e k -> p k e"), ALU.add))
            ch.link(V.tensor_tensor(posm[:, :, :], posm[:, :, :], chosen[:, :, :, :].rearrange("p c j e -> p (c j) e"),
                                    ALU.mult))
            ch.link(V.tensor_reduce(pos[:, :], posm[:, :, :], AX.X, ALU.add))
            V.tensor_copy(pos_i[:, :, :].rearrange("p c j -> p (c j)"), pos[:, :])
            ch.link(V.tensor_scalar(posq[:, :], pos[:, :], 1.0 / P, -0.498, ALU.mult, ALU.add))
            ch.link(V.tensor_scalar(posq[:, :], posq[:, :], MAGIC, -MAGIC, ALU.add, ALU.add))
            ch.link(V.scalar_tensor_tensor(posr[:, :], posq[:, :], -float(P), pos[:, :], ALU.mult, ALU.add))
            V.tensor_tensor(hot_r[:, :, :], iota_l[:, None, :].broadcast_to([P, NPC, P]),
                            posr[:, :, None].broadcast_to([P, NPC, P]), ALU.is_equal)
            ch.link(V.tensor_tensor(hot_q[:, :, 0, :], iota_l[:, None, 0:2 * NTILE].broadcast_to([P, NPC, 2 * NTILE]),
                                    posq[:, :, None].broadcast_to([P, NPC, 2 * NTILE]), ALU.is_equal))
            ch.link(V.tensor_scalar(hot_q[:, :, 1, :], hot_q[:, :, 0, :], iota_p[:, :], None, ALU.mult))
            V.tensor_tensor(hot_q[:, :, 0, :], hot_q[:, :, 0, :],
                            iota_j[:, :, :].rearrange("p c j -> p (c j)")[:, :, None].broadcast_to([P, NPC, 2 * NTILE]),
                            ALU.mult).then_inc(s_hot, 1)
            ch.link(V.tensor_tensor(texp[:, :, :], tiles_to[0:1, None, :].broadcast_to([1, NTILE, NE]),
                                    iota_l[0:1, 0:NTILE, None].broadcast_to([1, NTILE, NE]), ALU.is_le))
            ch.link(V.tensor_reduce(texf[:, :], texp[:, :, :], AX.X, ALU.add))
            V.tensor_scalar(tile_e[:, :], texf[:, :], NE - 1.0, None, ALU.min)
            dve.wait_ge(s_inverted, 1)
            ch.link(V.tensor_scalar(rtok[:, :], ps[:, 2, 0:2 * NTILE], float(P), None, ALU.mult))
            V.tensor_tensor(row_tok[:, :], rtok[:, :], ps[:, 2, 2 * NTILE:4 * NTILE], ALU.add).then_inc(s_plan, 1)
            dve.wait_ge(s_plan, 1)
            base += B * 10 + ch.n

            def lo_gate_up(t, i):
                e = dve.value_load(tile_e[0:1, bass.ds(t, 1)], min_val=0, max_val=NE - 1)
                for k, (hi, lo, src) in enumerate(((gwh[i], gwl[i], g_raw), (uwh[i], uwl[i], u_raw))):
                    dve.wait_ge(s_guhi, 2 * t + k + 1)
                    V.tensor_tensor(lo[:, :, :].rearrange("p n f -> p (n f)"),
                                    src[:, bass.ds(e, 1), :, :].rearrange("p e n f -> p (e n f)"),
                                    F32R_AS_F32(hi[:, :, :].rearrange("p n f -> p (n f)")), ALU.subtract).then_inc(s_gulo, 1)

            def lo_rows(t):
                for k in range(2):
                    dve.wait_ge(s_gxh, 2 * t + k + 1)
                    part = slice(2 * k, 2 * k + 2)
                    V.tensor_tensor(gxl[:, part, :].rearrange("p n r -> p (n r)"), ps[:, k, :],
                                    F32R_AS_F32(gxh[:, part, :].rearrange("p n r -> p (n r)")), ALU.subtract).then_inc(s_gxl, 1)

            def gated(t, i, first=False):
                if not first:
                    dve.wait_ge(s_aul, t)
                dve.wait_ge(s_sg, t + 1)
                dve.wait_ge(s_gu, 2 * t + 2)
                V.tensor_tensor(au[:, :], ps[:, 3 + 4 * i, :], sg[:, :], ALU.mult).then_inc(s_au, 1)

            def lo_gated(t, i):
                dve.wait_ge(s_auh, t + 1)
                V.tensor_tensor(aul[i][:, :, :].rearrange("p f r -> p (f r)"), au[:, :],
                                F32R_AS_F32(auh[i][:, :, :].rearrange("p f r -> p (f r)")), ALU.subtract).then_inc(s_aul, 1)

            lo_gate_up(0, 0)
            lo_rows(0)
            lo_gate_up(1, 1)
            gated(0, 0, first=True)
            lo_rows(1)
            lo_gated(0, 0)
            lo_gate_up(2, 0)
            with dve.Fori(0, (NTILE - 3) // 2) as pair:
                for i in range(2):
                    t = pair * 2 + i
                    gated(t + 1, 1 - i)
                    lo_rows(t + 2)
                    lo_gated(t + 1, 1 - i)
                    lo_gate_up(t + 3, 1 - i)
            t = NTILE - 3
            gated(t + 1, 1)
            lo_rows(t + 2)
            lo_gated(t + 1, 1)
            gated(t + 2, 0)
            lo_gated(t + 2, 0)

            def back_index(b, i):
                V.tensor_copy(pcur[i][:, :], pos_i[:, :, bass.ds(b * TT + i, 1)].rearrange("p c j -> p (c j)")).then_inc(s_pcur, 1)

            def add_rows(b, i, base):
                dve.wait_ge(s_back[i], 32 * b + 32)
                xj = xt[:, bass.ds(b * TT + i, 1), :].rearrange("p o d -> p (o d)")
                for c in range(2):
                    ins = V.scalar_tensor_tensor(xj, back[i][c][:, :], combine[:, c, bass.ds(b * TT + i, 1)], xj,
                                                 ALU.mult, ALU.add)
                    if c == 0:
                        ins.then_inc(c_dve, 1)
                        dve.wait_ge(c_dve, base + b * TT + i + 1)
                ins.then_inc(s_dadd, 1)

            for h in range(2):
                dve.wait_ge(s_yst[h], 16 * LEAD + 16 * NTILE)
            for i in range(TT):
                back_index(0, i)
            with dve.Fori(0, B - 1) as b:
                for i in range(TT):
                    add_rows(b, i, base)
                    back_index(b + 1, i)
            for i in range(TT):
                add_rows(B - 1, i, base)

    @block.tensor
    def _(pe):
        pe.wait_ge(s_constb, 1)
        pe.wait_ge(s_const, 1)

        def turn_colmax(b, k):
            pe.wait_ge((s_cm, s_cm2)[k], (2 * b + 2, b + 1)[k])
            if k == 0:
                pe.wait_ge(s_h, LEAD + 8 * b)
            for c in range((2 * DT, 2 * CT)[k]):
                src = (cmax, cmax2)[k]
                mm = T.transpose(ps[:, 2 + c // 4, (c % 4) * P:(c % 4 + 1) * P], src[:, c * P:(c + 1) * P], ident[:, :])
            mm.then_inc(s_cmT, 1)

        def smooth_rows(b, k):
            pe.wait_ge(s_dg, 2 * b + k + 1)
            n = (DT, CT)[k]
            T.matmul(ps[:, (2, 3)[k], 0:n * P], ones[:, :], diag_s[:, 0:n, :].rearrange("p n c -> p (n c)"), start=True, stop=True)
            T.matmul(ps[:, (3, 2)[k], 0:n * P], ones[:, :], diag_i[:, 0:n, :].rearrange("p n c -> p (n c)"),
                     start=True, stop=True).then_inc(s_rows, 1)

        def transpose_q(src, base_col, n_out, done):
            for o in range(n_out):
                for j in range(TT):
                    c = base_col + o * S + j * P
                    mm = T.transpose(psb[:, c:c + P], src[:, j, o * P:(o + 1) * P], identb[:, :])
            mm.then_inc(done, 1)

        def turn_qx(b, k):
            pe.wait_ge(s_qx, 2 * b + k + 1)
            pe.wait_ge(s_srow, 2 * b + k + 1)
            transpose_q(qx, 2048, (DT, CT)[k], s_qxT)

        def turn_qw(b, k):
            pe.wait_ge(s_qw, 2 * b + k + 1)
            if k == 0:
                pe.wait_ge(s_qxE, 2 * b + 1)
            transpose_q(qw, (2048, 3072)[k], (DT, CT)[k], s_qwT)

        def scale_row(b, k):
            pe.wait_ge(s_qwE if k == 0 else s_qxE, 2 * b + k + 1)
            T.matmul(ps[:, 2, :], ones[:, :], diag_w[:, :, :].rearrange("p n c -> p (n c)"), start=True, stop=True).then_inc(s_bc, 1)

        def product(b, k):
            pe.wait_ge(s_qwE, 2 * b + k + 1)
            for j in range(TT):
                if j == 1:
                    pe.wait_ge(s_bcE, 2 * b + k + 1)
                elif j >= 2:
                    pe.wait_ge(s_h, LEAD + 8 * b + k * TT + j - 1)
                n_in = (DT, CT)[k]
                for t in range(n_in):
                    mm = T.matmul(ps[:, 3 - j % 2, :], qxT[:, t, j * P:(j + 1) * P], qwT[:, t, :],
                                  start=(t == 0), stop=(t == n_in - 1))
                mm.then_inc(s_mm, 1)

        def ternary_total(m):
            pe.wait_ge(s_wabs, m + 1)
            T.matmul(ps[:, 7, m:m + 1], ones[:, :], wabs[:, m:m + 1], start=True, stop=True).then_inc(s_wtot, 1)

        def turn_ternary(m):
            pe.wait_ge(s_tern, m + 1)
            n_in, n_out = ((HT, DT), (DT, HT))[m]
            src = ternary_bf[:, :].rearrange("p (n d) -> p n d", n=n_in)
            for o in range(n_out):
                k = m * DT + o
                if k >= 2:
                    pe.wait_ge(s_ternE, k - 1)
                for j in range(n_in):
                    c = 4096 + 2048 * (k % 2) + j * P
                    mm = T.transpose(psb[:, c:c + P], src[:, j, o * P:(o + 1) * P], identb[:, :])
                mm.then_inc(s_ternT, 1)

        def transpose_x(done, first, free, freed):
            for t in range(DT):
                if free is not None:
                    pe.wait_ge(free, freed)
                for j in range(TT):
                    mm = T.transpose(ps[:, t, j * P:(j + 1) * P], xn[:, j, t * P:(t + 1) * P], ident[:, :])
                mm.then_inc(done, 1)

        def three(bank, ah, al, bh, bl_, first, last):
            T.matmul(bank, ah, bh, start=first, stop=False)
            T.matmul(bank, ah, bl_, start=False, stop=False)
            return T.matmul(bank, al, bh, start=False, stop=last)

        def hidden(b, j):
            i = j % 2
            if j < 2:
                pe.wait_ge(s_blo, LEAD + b * DT + DT)
            else:
                pe.wait_ge(s_relu, LEAD + b * HT + j - 1)
            for t in range(DT):
                for part in (bxh, bxl):
                    mm = T.matmul(ps[:, i, :], t_fc[:, t, j * P:(j + 1) * P], part[:, t, :],
                                  start=(t == 0 and part is bxh), stop=(t == DT - 1 and part is bxl))
            mm.then_inc(s_hps, 1)

        def project(b, j):
            i = j % 2
            if j == 0:
                pe.wait_ge(s_bdone, LEAD + b)
            pe.wait_ge(s_sql, b * HT + j + 1)
            for k in range(TT):
                for part in (sqh[i], sql[i]):
                    mm = T.matmul(ps[:, 4 + k, :], part[:, k * P:(k + 1) * P], t_pr[:, j, :],
                                  start=(j == 0 and part is sqh[i]), stop=(j == HT - 1 and part is sql[i]))
            mm.then_inc(s_yuse, 1)

        def turn_normed(b):
            pe.wait_ge(s_bxn, b + 1)
            pe.wait_ge(s_relu, LEAD + b * HT)
            for t in range(DT):
                if t >= 2:
                    pe.wait_ge(s_blo, LEAD + b * DT + t - 1)
                for j in range(TT):
                    mm = T.transpose(ps[:, t % 2, j * P:(j + 1) * P], xn[:, j, t * P:(t + 1) * P], ident[:, :])
                mm.then_inc(s_bxt, 1)

        def iteration(b, main, feed, ahead, tern=False):
            def slot(j):
                if feed:
                    if j >= 2:
                        project(b - 1, j - 2)
                    hidden(b - 1, j)

            slot(0)
            if tern:
                ternary_total(0)
            slot(1)
            if main:
                turn_qx(b, 0)
            slot(2)
            if main:
                turn_qw(b, 0)
            slot(3)
            if main:
                scale_row(b, 0)
            if main:
                product(b, 0)
            if tern:
                turn_ternary(0)
            slot(4)
            if main:
                turn_colmax(b, 1)
            slot(5)
            slot(6)
            if main:
                smooth_rows(b, 1)
            if tern:
                ternary_total(1)
            slot(7)
            slot(8)
            if main:
                turn_qx(b, 1)
                turn_qw(b, 1)
                scale_row(b, 1)
            if main:
                product(b, 1)
            if feed:
                project(b - 1, HT - 3)
            if ahead:
                turn_colmax(b + 1, 0)
            if feed:
                hidden(b - 1, HT - 1)
                project(b - 1, HT - 2)
                project(b - 1, HT - 1)
                pe.wait_ge(s_yuse, LEAD + b * HT)
                pe.nop().then_inc(s_by, 1)
            if ahead:
                smooth_rows(b + 1, 0)
            if main:
                turn_normed(b)
            if tern:
                turn_ternary(1)

        turn_colmax(0, 0)
        smooth_rows(0, 0)
        iteration(0, True, False, True, tern=True)
        with pe.Fori(1, B - 1) as b:
            iteration(b, True, True, True)
        iteration(B - 1, True, True, False)
        iteration(B, False, True, False)

        if upto >= 3:
            def kv(grp, m, bl):
                pe.wait_ge(s_w1, LEAD + grp + 1)
                for t in range(CT):
                    mm = three(ps[:, 6, :], wkh[:, t, :], wkl[:, t, :], cTh[:, bl, t, :], cTl[:, bl, t, :],
                               t == 0, t == CT - 1)
                mm.then_inc(s_kv, 1)
                for t in range(CT):
                    mm = three(ps[:, 7, :], wvh[:, t, :], wvl[:, t, :], cTh[:, bl, t, :], cTl[:, bl, t, :],
                               t == 0, t == CT - 1)
                mm.then_inc(s_kv, 1)

            def v_turn(m):
                pe.wait_ge(s_vT, m + 1)
                for j in range(TT):
                    mm = T.transpose(ps[:, 7, j * P:(j + 1) * P], vT[:, j * P:(j + 1) * P], ident[:, :])
                mm.then_inc(s_vt, 1)

            def query_part(n, t, h, bl):
                if t == 0:
                    pe.wait_ge(s_ql, LEAD + n)
                mm = three(ps[:, 4, :], wqh[:, t, h * DH:(h + 1) * DH], wql[:, t, h * DH:(h + 1) * DH],
                           xTh[:, bl, t, :], xTl[:, bl, t, :], t == 0, t == DT - 1)
                if t == DT - 1:
                    mm.then_inc(s_q, 1)

            def query(n, h, bl):
                for t in range(DT):
                    query_part(n, t, h, bl)

            def scores(n, i, h, bl):
                if i == 0:
                    pe.wait_ge(s_ql, LEAD + n + 1)
                pe.wait_ge(s_max[i % 2], LEAD + n * 2 + i // 2)
                three(ps[:, i % 2, :], qh[h][:, i * P:(i + 1) * P], ql[h][:, i * P:(i + 1) * P],
                      kh[bl][:, :], kl[bl][:, :], True, True).then_inc(s_s, 1)

            def turn(n, i, h):
                pe.wait_ge(s_ptl[i % 2], LEAD + n * 2 + i // 2)
                for j in range(TT):
                    mm = T.transpose(ps[:, 2 + i % 2, j * P:(j + 1) * P], pr[h][:, j, i * P:(i + 1) * P], ident[:, :])
                mm.then_inc(s_pt, 1)

            def attend_part(n, i, h, bl):
                if i == 0:
                    pe.wait_ge(s_ol, LEAD + n)
                pe.wait_ge(s_ptl[i % 2], LEAD + n * 2 + i // 2 + 1)
                mm = three(ps[:, 5, :], vh[bl][:, i, :], vl[bl][:, i, :], pTh[:, i, :], pTl[:, i, :],
                           i == 0, i == TT - 1)
                if i == TT - 1:
                    mm.then_inc(s_o, 1)

            def project_out(grp, n, m):
                pe.wait_ge(s_w2, LEAD + grp + 1)
                pe.wait_ge(s_ol, LEAD + n + 1)
                for j in range(TT):
                    if j < 2:
                        pe.wait_ge(s_vl, m + 1)
                    else:
                        pe.wait_ge(s_yadd[j % 2], LEAD + m * 2 + j // 2)
                    for h in range(2):
                        mm = three(ps[:, 6 + j % 2, :], oh[h][:, j * P:(j + 1) * P], ol[h][:, j * P:(j + 1) * P],
                                   woh[:, h, :], wol[:, h, :], h == 0, h == 1)
                    mm.then_inc(s_y, 1)

            def group(grp, n0, m0, last):
                for u in range(4):
                    n, bl, h = n0 + u, u // 2, u % 2
                    pe.wait_ge(s_pn, n + 1)
                    nbl = ((u + 1) // 2) % 2
                    more_s, more_q = not (last and u == 3), not (last and u >= 2)
                    if u == 2 and more_q:
                        pe.wait_ge(s_w1, LEAD + grp + 2)
                    if h == 1 and more_s:
                        pe.wait_ge(s_kl, m0 + bl + 2)
                    for i in range(TT):
                        if more_s:
                            scores(n + 1, i, 1 - h, nbl)
                        turn(n, i, h)
                        if h == 0 and more_q:
                            query_part(n + 2, i, h, 1 - bl)
                        if h == 1 and i >= 2:
                            attend_part(n, i - 2, h, bl)
                    if h == 0:
                        if more_q:
                            m = m0 + u // 2 + 1
                            pe.wait_ge(s_yadd[1], LEAD + m * 2 - 2)
                            kv(grp if u == 0 else grp + 1, m, (u // 2 + 1) % 2)
                        pe.wait_ge(s_vl, m0 + bl + 1)
                        for i in range(TT):
                            attend_part(n, i, h, bl)
                        if more_q:
                            v_turn(m)
                    else:
                        attend_part(n, 2, h, bl)
                        attend_part(n, 3, h, bl)
                        if more_q:
                            query(n + 2, h, 1 - bl)
                        project_out(grp, n, m0 + bl)

            with pe.Fori(0, 2) as bp:
                for bl in range(2):
                    b = bp * 2 + bl
                    pe.wait_ge(s_cxn, b + 1)
                    transpose_x(s_cxt, None, s_cxl, b * DT)
                    pe.wait_ge(s_cin, bp * 64 + 64)
                    pe.wait_ge(s_ccl, LEAD + b * CT)
                    for t in range(CT):
                        for j in range(TT):
                            mm = T.transpose(ps[:, 4 + t, j * P:(j + 1) * P], ctx_raw[:, bl, j, t * P:(t + 1) * P], ident[:, :])
                        mm.then_inc(s_cct, 1)
                grp, n0, m0 = bp * NG, bp * (4 * NG), bp * (2 * NG)
                pe.wait_ge(s_ccl, LEAD + bp * (2 * CT) + 2 * CT)
                pe.wait_ge(s_cxl, LEAD + bp * (2 * DT) + 2 * DT)
                kv(grp, m0, 0)
                query(n0, 0, 0)
                v_turn(m0)
                pe.wait_ge(s_kl, m0 + 1)
                for i in range(TT):
                    scores(n0, i, 0, 0)
                query(n0 + 1, 1, 0)
                with pe.Fori(0, NG - 1) as g:
                    group(grp + g, n0 + g * 4, m0 + g * 2, False)
                group(grp + (NG - 1), n0 + 4 * (NG - 1), m0 + 2 * (NG - 1), True)

        if upto >= 4:
            pe.wait_ge(s_rws, 1)
            for t in range(DT):
                mm = T.transpose(ps[:, 5, t * NE:(t + 1) * NE], rw[:, t * P:(t + 1) * P], ident[0:NE, 0:NE])
            mm.then_inc(s_rwT, 1)
            pe.wait_ge(s_rw, 1)
            with pe.Fori(0, B) as b:
                pe.wait_ge(s_dxn, b + 1)
                transpose_x(s_dxt, None, s_dxl, b * DT)
                pe.wait_ge(s_dxl, LEAD + b * DT + DT)
                for t in range(DT):
                    mm = three(ps[0:NE, 4, :], rwh[:, t, :], rwl[:, t, :], dxh[:, t, :], dxl[:, t, :], t == 0, t == DT - 1)
                mm.then_inc(s_lgT, 1)
                wait_alone(pe, s_lgTE, b + 1, s_passed)
                for j in range(TT):
                    mm = T.transpose(ps[:, 5, j * NE:(j + 1) * NE], lgT[:, j * P:(j + 1) * P], ident[0:NE, 0:NE])
                mm.then_inc(s_lg, 1)

            pe.wait_ge(s_cw, B)
            pe.wait_ge(s_iota, 1)
            picks = chosen[:, :, :, :].rearrange("p c j e -> p (c j e)")
            T.matmul(ps[:, 0, 0:NPC * NE], before[:, :], picks, start=True, stop=True)
            T.matmul(ps[:, 1, 0:NPC * NE], onesb[:, :], picks, start=True, stop=True).then_inc(s_cnt, 1)
            pe.wait_ge(s_hot, 1)
            for k in range(NPC):
                mm = T.matmul(ps[:, 2, 0:4 * NTILE], hot_r[:, k, :], hot_q[:, k, :, :].rearrange("p c q -> p (c q)"),
                              start=(k == 0), stop=(k == NPC - 1))
            mm.then_inc(s_inverted, 1)

            def turn_rows(t, i, k, early=False):
                pe.wait_ge(s_gat[i], 32 * k + 32)
                if not early:
                    pe.wait_ge(s_gxl, 2 * t)
                for d in range(DT):
                    for h in range(2):
                        mm = T.transpose(ps[:, d // 2, (d % 2) * ROWS + h * P:(d % 2) * ROWS + (h + 1) * P],
                                         xg[:, i, h, d * P:(d + 1) * P], ident[:, :])
                    if d % 2:
                        mm.then_inc(s_gT, 1)

            def gate_up(t, i):
                pe.wait_ge(s_gxl, 2 * t + 2)
                for k, (hi, lo) in enumerate(((gwh[i], gwl[i]), (uwh[i], uwl[i]))):
                    pe.wait_ge(s_gulo, 2 * t + k + 1)
                    for f in range(FT):
                        for d in range(DT):
                            mm = three(ps[:, 2 + 4 * i + k, f * ROWS:(f + 1) * ROWS], hi[:, d, f * P:(f + 1) * P],
                                       lo[:, d, f * P:(f + 1) * P], gxh[:, d, :], gxl[:, d, :], d == 0, d == DT - 1)
                    mm.then_inc(s_gu, 1)

            def down(t, i):
                pe.wait_ge(s_aul, t + 1)
                pe.wait_ge(s_dns, t + 1)
                for h in range(2):
                    pe.wait_ge(s_yrow[h], LEAD + t)
                    for f in range(FT):
                        mm = three(ps[:, 4 + h, :], auh[i][:, f, h * P:(h + 1) * P], aul[i][:, f, h * P:(h + 1) * P],
                                   dwh[:, f, :], dwl[:, f, :], f == 0, f == FT - 1)
                    mm.then_inc(s_dy, 1)

            turn_rows(0, 0, 0, early=True)
            gate_up(0, 0)
            turn_rows(1, 1, 0)
            with pe.Fori(0, (NTILE - 3) // 2) as pair:
                for i in range(2):
                    t = pair * 2 + i
                    gate_up(t + 1, 1 - i)
                    turn_rows(t + 2, i, pair + 1)
                    down(t, i)
            t = NTILE - 3
            gate_up(t + 1, 1)
            turn_rows(t + 2, 0, (t + 2) // 2)
            down(t, 0)
            gate_up(t + 2, 0)
            down(t + 1, 1)
            down(t + 2, 0)

    persistent.close()
    sems.close()


_INS = ['x', 'fside_BxS2xS2_0', 'ctx_1024', 'mask_BxS2_bf1', 'g_xattn', 'g_ffn', 'L0_ffn_w_fc', 'L0_ffn_w_proj',
        'L1_xattn_Wq', 'L1_xattn_Wk', 'L1_xattn_Wv', 'L1_xattn_Wo', 'L1_ffn_router_w', 'L1_ffn_norm_w',
        'L1_ffn_gate_w', 'L1_ffn_up_w', 'L1_ffn_down_w']
STOP = "D"


def kernel(**inputs):
    import numpy as _np
    import concourse.bacc as _bacc
    from concourse import mybir as _mybir
    from concourse.bass_utils import run_bass_kernel_spmd as _run

    nc = _bacc.Bacc("TRN2", target_bir_lowering=False, num_devices=1)
    arrays, args = {}, []
    for name in _INS:
        a = _np.ascontiguousarray(inputs[name])
        if a.dtype == _np.bool_:
            a = a.view(_np.uint8)
        arrays[f"in_{name}"] = a
        args.append(nc.dram_tensor(f"in_{name}", a.shape, _mybir.dt.from_np(a.dtype), kind="ExternalInput").ap())
    args.append(nc.dram_tensor("out_y", (B, S, D), FP32, kind="ExternalOutput").ap())
    flamingo_gated_kernel(nc, *args, stop=STOP)
    r = _run(nc, [arrays], core_ids=[0])
    return r.results[0]["out_y"]
```

```python
import concourse.bass as bass
from concourse import mybir
from contextlib import ExitStack

FP32 = mybir.dt.float32
FP32R = mybir.dt.float32r
BF16 = mybir.dt.bfloat16
U8 = mybir.dt.uint8
U32 = mybir.dt.uint32
I32 = mybir.dt.int32
ALU = mybir.AluOpType
ACT = mybir.ActivationFunctionType
AX = mybir.AxisListType

P = 128
B, S, D = 4, 512, 512
TT = S // P
DT = D // P
DC = 256
CT = DC // P
IH = DC
HF = 1280
HT = HF // P
NH, NG, DH = 16, 8, 128
NE, FE = 8, 256
FT = FE // P
LN_EPS = 1e-5
Q_EPS = 1e-6
QMAX = 127.0
MAGIC = 1.5 * 2.0 ** 23
MASKED = 2.0 ** 100
SCALE = float(DH) ** -0.5
MOE_SCALE = 4.0
NPC = 2 * B * TT
ROWS = 256
NTILE = (2 * B * S + NE * (ROWS - 1)) // ROWS
LEAD = 1


class Chain:

    def __init__(self, eng, sem, base):
        self.eng, self.sem, self.base, self.n = eng, sem, base, 0

    def link(self, ins, past=None):
        self.n += 1
        ins.then_inc(self.sem, 1)
        if past is None:
            self.eng.wait_ge(self.sem, self.base + self.n)
        else:
            wait_alone(self.eng, self.sem, self.base + self.n, past)


def wait_alone(eng, sem, value, passed):
    eng.wait_ge(sem, value)
    eng.sem_inc(passed, 1)


def flamingo_gated_kernel(nc, x, fside, ctx_in, mask, g_xattn, g_ffn, w_fc, w_proj,
                          wq, wk, wv, wo, router_w, norm_w, gate_w, up_w, down_w, out):
    V, A, G, T = nc.vector, nc.scalar, nc.gpsimd, nc.tensor
    persistent = ExitStack()
    sems = ExitStack()

    def sem(name):
        return sems.enter_context(nc.semaphore(name))

    def buf(scope, name, shape, dt):
        return scope.enter_context(nc.sbuf_tensor(name, shape, dt))

    xt = buf(persistent, "x_tok", [P, B * TT, D], FP32)
    ident = buf(persistent, "ident", [P, P], FP32)
    identb = buf(persistent, "identb", [P, P], BF16)
    ones = buf(persistent, "ones", [P, P], FP32)
    eps_ln = buf(persistent, "eps_ln", [P, 1], FP32)
    eps_q = buf(persistent, "eps_q", [P, 1], FP32)
    gates_raw = buf(persistent, "gates_raw", [P, 4], FP32)
    gates = buf(persistent, "gates", [P, 4], FP32)
    stats = buf(persistent, "stats", [P, TT, 6], FP32)
    mv = buf(persistent, "mean_var", [P, TT, 2], FP32)
    std = buf(persistent, "std", [P, TT], FP32)
    rstd = buf(persistent, "rstd", [P, TT], FP32)
    xn = buf(persistent, "x_normed", [P, TT, D], FP32)
    ps = persistent.enter_context(nc.psum_tensor("ps", [P, 8, 512], FP32))
    psb = ps[:, :, :].rearrange("p k n -> p (k n)").bitcast(BF16)

    ab = ExitStack()
    t_fc = buf(ab, "ternary_fc_T", [P, DT, HF], FP32R)
    t_pr = buf(ab, "ternary_proj_T", [P, HT, D], FP32R)
    wabs = buf(ab, "wabs", [P, 2], FP32)
    wmean = buf(ab, "wmean", [P, 2], FP32)
    wthr = buf(ab, "wthr", [P, 2], FP32)
    wnthr = buf(ab, "wnthr", [P, 2], FP32)
    b_shift = buf(ab, "b_norm_shift", [P, TT], FP32)
    h_scale = buf(ab, "h_scale", [P, 1], FP32)
    y_scale = buf(ab, "y_scale", [P, 1], FP32)

    xa = buf(ab, "a_x_normed", [P, TT, D], FP32)
    w1 = buf(ab, "gate_up", [P, TT, D], FP32)
    w2 = buf(ab, "down", [P, TT, DC], FP32)
    ws = buf(ab, "w_smoothed", [P, TT, D], FP32)
    a_stats = buf(ab, "a_stats", [P, TT, 6], FP32)
    a_mv = buf(ab, "a_mean_var", [P, TT, 2], FP32)
    a_std = buf(ab, "a_std", [P, TT], FP32)
    a_rstd = buf(ab, "a_rstd", [P, TT], FP32)
    a_fine = buf(ab, "a_std_refined", [P, TT], FP32)
    cmax = buf(ab, "colmax", [P, 2 * D], FP32)
    cmax2 = buf(ab, "colmax2", [P, 2 * DC], FP32)
    amax = buf(ab, "amax", [P, 8], FP32)
    winv = buf(ab, "w_amax_inv", [P, DT], FP32)
    ratio = buf(ab, "smooth_ratio", [P, DT], FP32)
    smooth = buf(ab, "smooth", [P, DT], FP32)
    refine = buf(ab, "smooth_refined", [P, DT], FP32)
    smooth_inv = buf(ab, "smooth_inv", [P, DT], FP32)
    diag_s = buf(ab, "diag_smooth", [P, DT, P], FP32)
    diag_i = buf(ab, "diag_smooth_inv", [P, DT, P], FP32)
    diag_w = buf(ab, "diag_w_scale", [P, TT, P], FP32)
    s_row = buf(ab, "smooth_row", [P, D], FP32)
    rowmax = buf(ab, "rowmax", [P, TT], FP32)
    xsc = buf(ab, "x_scale", [P, TT], FP32)
    xrq = buf(ab, "x_scale_inv", [P, TT], FP32)
    wrowmax = buf(ab, "w_rowmax", [P, TT], FP32)
    wsc = buf(ab, "w_scale", [P, TT], FP32)
    wrq = buf(ab, "w_scale_inv", [P, TT], FP32)
    wsc_row = buf(ab, "w_scale_row", [P, S], FP32)
    qx = buf(ab, "qx", [P, TT, D], BF16)
    qw = buf(ab, "qw", [P, TT, D], BF16)
    qxT = buf(ab, "qxT", [P, DT, S], BF16)
    qwT = buf(ab, "qwT", [P, DT, S], BF16)
    hh = buf(ab, "h", [P, TT, D], FP32)

    bxh = buf(ab, "b_xT_hi", [P, DT, S], FP32R)
    bxl = buf(ab, "b_xT_lo", [P, DT, S], FP32R)

    pt = ExitStack()
    ternary_raw = buf(pt, "ternary_raw", [P, 5120], FP32)
    ternary_bf = buf(pt, "ternary_values", [P, 5120], BF16)
    pt.close()
    pb = ExitStack()
    relu = [buf(pb, f"relu{i}", [P, S], FP32) for i in range(2)]
    sq = [buf(pb, f"relu_sq{i}", [P, S], FP32) for i in range(2)]
    sqh = [buf(pb, f"relu_sq_hi{i}", [P, S], FP32R) for i in range(2)]
    sql = [buf(pb, f"relu_sq_lo{i}", [P, S], FP32R) for i in range(2)]
    pb.close()
    ab.close()

    pc = ExitStack()
    pr = [buf(pc, f"probs{i}", [P, TT, S], FP32) for i in range(2)]
    pTh = buf(pc, "probsT_hi", [P, TT, S], FP32R)
    pTl = buf(pc, "probsT_lo", [P, TT, S], FP32R)
    sm = [buf(pc, f"masked_scores{i}", [P, S], FP32) for i in range(TT)]
    smax = [buf(pc, f"score_max{i}", [P, TT], FP32) for i in range(2)]
    nbias = [buf(pc, f"neg_max{i}", [P, TT], FP32) for i in range(2)]
    rsum = [buf(pc, f"row_sum{i}", [P, TT], FP32) for i in range(2)]
    rinv = [buf(pc, f"row_sum_inv{i}", [P, TT], FP32) for i in range(2)]
    xTh = buf(pc, "xT_hi", [P, 2, DT, S], FP32R)
    xTl = buf(pc, "xT_lo", [P, 2, DT, S], FP32R)
    ctx_raw = buf(pc, "ctx_raw", [P, 2, TT, DC], FP32)
    cTh = buf(pc, "ctxT_hi", [P, 2, CT, S], FP32R)
    cTl = buf(pc, "ctxT_lo", [P, 2, CT, S], FP32R)
    mask_u8 = buf(pc, "mask_u8", [P, 2, S], U8)
    pen = buf(pc, "penalty", [P, 2, S], FP32)
    valid = buf(pc, "any_valid", [P, 2], FP32)
    y_gate = buf(pc, "y_gate", [P, 2], FP32)
    kh = [buf(pc, f"kT_hi{i}", [P, S], FP32R) for i in range(2)]
    kl = [buf(pc, f"kT_lo{i}", [P, S], FP32R) for i in range(2)]
    vT = buf(pc, "vT", [P, S], FP32)
    vh = [buf(pc, f"v_hi{i}", [P, TT, DH], FP32R) for i in range(2)]
    vl = [buf(pc, f"v_lo{i}", [P, TT, DH], FP32R) for i in range(2)]
    qh = [buf(pc, f"qT_hi{i}", [P, S], FP32R) for i in range(2)]
    ql = [buf(pc, f"qT_lo{i}", [P, S], FP32R) for i in range(2)]
    oh = [buf(pc, f"oT_hi{i}", [P, S], FP32R) for i in range(2)]
    ol = [buf(pc, f"oT_lo{i}", [P, S], FP32R) for i in range(2)]
    woh = buf(pc, "wo_hi", [P, 2, D], FP32R)
    wol = buf(pc, "wo_lo", [P, 2, D], FP32R)
    wq_raw = buf(pc, "wq_raw", [P, DT, 2 * DH], FP32)
    wk_raw = buf(pc, "wk_raw", [P, CT, DH], FP32)
    wv_raw = buf(pc, "wv_raw", [P, CT, DH], FP32)
    wo_raw = buf(pc, "wo_raw", [P, 2, D], FP32)
    wqh = buf(pc, "wq_hi", [P, DT, 2 * DH], FP32R)
    wql = buf(pc, "wq_lo", [P, DT, 2 * DH], FP32R)
    wkh = buf(pc, "wk_hi", [P, CT, DH], FP32R)
    wkl = buf(pc, "wk_lo", [P, CT, DH], FP32R)
    wvh = buf(pc, "wv_hi", [P, CT, DH], FP32R)
    wvl = buf(pc, "wv_lo", [P, CT, DH], FP32R)
    pc.close()

    pd = ExitStack()
    g_raw = buf(pd, "gate_raw", [P, NE, DT, FE], FP32)
    u_raw = buf(pd, "up_raw", [P, NE, DT, FE], FP32)
    d_raw = buf(pd, "down_raw", [P, NE, FT, D], FP32)
    combine = buf(pd, "combine", [P, 2, B * TT], FP32)
    pos_i = buf(pd, "position", [P, 2, B * TT], I32)
    row_tok = buf(pd, "row_token", [P, 2 * NTILE], I32)
    tile_e = buf(pd, "tile_expert", [1, NTILE], I32)
    xg = xn[:, :, :].rearrange("p (i h) d -> p i h d", i=2)
    pr_ = ExitStack()
    dxn = buf(pr_, "d_x_normed", [P, B * TT, D], FP32)
    rw_raw = buf(pr_, "router_raw", [NE, D], FP32)
    nw_raw = buf(pr_, "norm_raw", [NE, D], FP32)
    rw = buf(pr_, "router_scaled", [NE, D], FP32)
    rwh = buf(pr_, "router_hi", [P, DT, NE], FP32R)
    rwl = buf(pr_, "router_lo", [P, DT, NE], FP32R)
    ssq = buf(pr_, "sum_sq", [P, B * TT], FP32)
    rms = buf(pr_, "rms", [P, B * TT], FP32)
    rms_inv = buf(pr_, "rms_inv", [P, B * TT], FP32)
    lgT = buf(pr_, "logitsT", [NE, S], FP32)
    lg = buf(pr_, "logits", [P, B * TT, NE], FP32)
    lmax = buf(pr_, "logit_max", [P, B * TT], FP32)
    pe_ = buf(pr_, "router_exp", [P, B * TT, NE], FP32)
    top = buf(pr_, "top8", [P, B * TT, 8], FP32)
    topi = buf(pr_, "top8_index", [P, B * TT, 8], U32)
    topf = buf(pr_, "top8_index_f", [P, B * TT, 8], FP32)
    den = buf(pr_, "top2_sum", [P, B * TT], FP32)
    topw = buf(pr_, "top_weight", [P, B * TT, 2], FP32)
    iota_e = buf(pr_, "iota_e", [P, NE], FP32)
    iota_l = buf(pr_, "iota_lane", [P, P], FP32)
    iota_b = buf(pr_, "iota_lane_bf16", [P, P], BF16)
    iota_p = buf(pr_, "iota_partition", [P, 1], FP32)
    iota_j = buf(pr_, "iota_token_tile", [P, 2, B * TT], FP32)
    before = buf(pr_, "before", [P, P], BF16)
    onesb = buf(pr_, "onesb", [P, P], BF16)
    chosen = buf(pr_, "chosen", [P, 2, B * TT, NE], BF16)
    total = buf(pr_, "total", [P, NE, NPC], FP32)
    scan = buf(pr_, "scan", [P, NE, NPC], FP32)
    keep = buf(pr_, "keep", [P, NE, NPC], FP32)
    tiles = buf(pr_, "tiles", [P, NE], FP32)
    tiles_to = buf(pr_, "tiles_to", [P, NE], FP32)
    first = buf(pr_, "first_row", [P, NE], FP32)
    posm = buf(pr_, "position_by_expert", [P, NPC, NE], FP32)
    pos = buf(pr_, "position_f", [P, NPC], FP32)
    posq = buf(pr_, "position_tile", [P, NPC], FP32)
    posqb = buf(pr_, "position_tile_bf16", [P, NPC], BF16)
    posrb = buf(pr_, "position_lane_bf16", [P, NPC], BF16)
    texp = buf(pr_, "tile_compare", [1, NTILE, NE], FP32)
    texf = buf(pr_, "tile_expert_f", [1, NTILE], FP32)
    rtok = buf(pr_, "row_token_f", [P, 2 * NTILE], FP32)
    px = ExitStack()
    dxh = buf(px, "d_xT_hi", [P, DT, S], FP32R)
    dxl = buf(px, "d_xT_lo", [P, DT, S], FP32R)
    px.close()
    ph = ExitStack()
    hot_r = buf(ph, "lane_onehot", [P, NPC, P], BF16)
    hot_q = buf(ph, "tile_onehot", [P, NPC, 2, 2 * NTILE], BF16)
    ph.close()
    pr_.close()
    pm = ExitStack()
    gwh = [buf(pm, f"gate_hi{i}", [P, DT, FE], FP32R) for i in range(2)]
    gwl = [buf(pm, f"gate_lo{i}", [P, DT, FE], FP32R) for i in range(2)]
    uwh = [buf(pm, f"up_hi{i}", [P, DT, FE], FP32R) for i in range(2)]
    uwl = [buf(pm, f"up_lo{i}", [P, DT, FE], FP32R) for i in range(2)]
    dwh = buf(pm, "down_hi", [P, FT, D], FP32R)
    dwl = buf(pm, "down_lo", [P, FT, D], FP32R)
    gxh = buf(pm, "rowsT_hi", [P, DT, ROWS], FP32R)
    gxl = buf(pm, "rowsT_lo", [P, DT, ROWS], FP32R)
    sg = buf(pm, "silu", [P, FT * ROWS], FP32)
    au = buf(pm, "gated", [P, FT * ROWS], FP32)
    auh = [buf(pm, f"gated_hi{i}", [P, FT, ROWS], FP32R) for i in range(2)]
    aul = [buf(pm, f"gated_lo{i}", [P, FT, ROWS], FP32R) for i in range(2)]
    yrow = [buf(pm, f"expert_rows{i}", [P, D], FP32) for i in range(2)]
    icur = [buf(pm, f"gather_index{i}", [P, 2], I32) for i in range(2)]
    pm.close()
    pf = ExitStack()
    back = [[buf(pf, f"back{i}{c}", [P, D], FP32) for c in range(2)] for i in range(4)]
    pcur = [buf(pf, f"back_index{i}", [P, 2], I32) for i in range(4)]
    pf.close()
    pd.close()
    normed_rows = nc.dram_tensor("normed_rows", (B * S, D), FP32).ap()
    expert_rows = nc.dram_tensor("expert_rows", (NTILE * ROWS, D), FP32).ap()

    s_const = sem("const")
    s_constb = sem("const_vector")
    s_gates_in = sem("gates_in")
    s_gates = sem("gates_tanh")
    s_passed = sem("waits_passed")
    c_dve = sem("chain_vector")
    c_pool = sem("chain_gpsimd")
    s_var = sem("variance")
    s_std = sem("std")
    s_xin = sem("x_in")
    s_w1in = sem("gate_up_in")
    s_w2in = sem("down_in")
    s_tw_in = sem("ternary_raw_in")
    s_wabs = sem("ternary_abs_sums")
    s_wtot = sem("ternary_totals")
    s_tern = sem("ternary_values")
    s_ternT = sem("ternary_transposed")
    s_ternE = sem("ternary_evicted")
    c_head = sem("chain_vector_head")
    c_main = sem("chain_vector_main")
    s_avar = sem("a_variance")
    s_astd = sem("a_std")
    s_cm = sem("colmax")
    s_cm2 = sem("colmax2")
    s_cmT = sem("colmax_transposed")
    s_ratio = sem("smooth_ratio")
    s_sqrt = sem("smooth_sqrt")
    s_dg = sem("smooth_diagonals")
    s_rows = sem("smooth_rows")
    s_srow = sem("smooth_row_evicted")
    s_ws1 = sem("gate_up_smoothed")
    s_ws2 = sem("down_smoothed")
    s_wrq = sem("w_scale_inverse")
    s_wmg = sem("w_rounded")
    s_qx = sem("x_quantized")
    s_qw = sem("w_quantized")
    s_qxT = sem("x_quantized_transposed")
    s_qwT = sem("w_quantized_transposed")
    s_qxE = sem("x_quantized_evicted")
    s_qwE = sem("w_quantized_evicted")
    s_bc = sem("w_scale_broadcast")
    s_bcE = sem("w_scale_evicted")
    s_mm = sem("quantized_product")
    s_h = sem("product_dequantized")
    s_silu = sem("a_silu")
    s_xadd = sem("a_added")
    s_bnb = sem("b_norm_factors")
    s_bxn = sem("b_normed")
    s_bxt = sem("b_transposed")
    s_bhi = sem("b_xT_hi")
    s_blo = sem("b_xT_lo")
    s_hps = sem("b_hidden")
    s_relu = sem("b_relu")
    s_sq = sem("b_square")
    s_sqh = sem("b_square_hi")
    s_sql = sem("b_square_lo")
    s_yuse = sem("b_square_used")
    s_by = sem("b_product")
    s_bdone = sem("b_added")
    s_cin = sem("c_inputs")
    s_cxn = sem("c_normed")
    s_min = sem("c_masks_in")
    s_pen = sem("c_penalty")
    s_ct = sem("c_turned")
    s_ch = sem("c_turned_hi")
    s_cl = sem("c_turned_lo")
    s_w1raw = sem("c_qkv_weights_in")
    s_w2raw = sem("c_out_weights_in")
    s_w1 = sem("c_qkv_weights_split")
    s_w2 = sem("c_out_weights_split")
    s_kv = sem("c_kv_product")
    s_kh = sem("c_k_hi")
    s_kl = sem("c_k_lo")
    s_vT = sem("c_vT")
    s_vt = sem("c_v_transposed")
    s_vh = sem("c_v_hi")
    s_vl = sem("c_v_lo")
    s_q = sem("c_q_product")
    s_qh = sem("c_q_hi")
    s_ql = sem("c_q_lo")
    s_s = sem("c_scores")
    s_max = [sem(f"c_score_max{i}") for i in range(2)]
    s_nb = sem("c_neg_max")
    s_exp = [sem(f"c_exp{i}") for i in range(TT)]
    s_rinv = sem("c_row_sum_inv")
    s_pn = sem("c_probs_normed")
    s_pt = sem("c_probs_transposed")
    s_pth = sem("c_probsT_hi")
    s_ptl = [sem(f"c_probsT_lo{i}") for i in range(2)]
    s_o = sem("c_attended")
    s_oh = sem("c_oT_hi")
    s_ol = sem("c_oT_lo")
    s_y = sem("c_out_product")
    s_yadd = [sem(f"c_added{i}") for i in range(2)]
    s_din = sem("d_router_in")
    s_rw = sem("d_router_split")
    s_rws = sem("d_router_scaled")
    s_rwT = sem("d_router_transposed")
    s_iota = sem("d_iota")
    s_dxn = sem("d_normed")
    s_ssq = sem("d_sum_sq")
    s_rms = sem("d_rms")
    s_dxt = sem("d_transposed")
    s_dxh = sem("d_xT_hi")
    s_dxl = sem("d_xT_lo")
    s_lgT = sem("d_logitsT")
    s_lgTE = sem("d_logitsT_evicted")
    s_lg = sem("d_logits")
    s_lc = sem("d_logits_centred")
    s_lexp = sem("d_router_exp")
    s_cw = sem("d_chosen")
    s_xst = sem("d_normed_stored")
    s_wraw = sem("d_weights_in")
    s_cnt = sem("d_counts")
    s_hot = sem("d_onehots")
    s_inverted = sem("d_inverted")
    s_plan = sem("d_plan")
    s_icur = sem("d_gather_index")
    s_gat = [sem(f"d_gathered{i}") for i in range(2)]
    s_guhi = sem("d_gate_up_hi")
    s_gulo = sem("d_gate_up_lo")
    s_dhi = sem("d_down_hi")
    s_dns = sem("d_down_split")
    s_gT = sem("d_rows_transposed")
    s_gxh = sem("d_rowsT_hi")
    s_gxl = sem("d_rowsT_lo")
    s_gu = sem("d_gate_up_product")
    s_sg = sem("d_silu")
    s_au = sem("d_gated")
    s_auh = sem("d_gated_hi")
    s_aul = sem("d_gated_lo")
    s_dy = sem("d_product")
    s_yrow = [sem(f"d_rows_evicted{i}") for i in range(2)]
    s_yst = [sem(f"d_rows_stored{i}") for i in range(2)]
    s_pcur = sem("d_back_index")
    s_back = [sem(f"d_back{i}") for i in range(4)]
    s_dadd = sem("d_added")
    s_out = sem("stored")

    xv = x.rearrange("b (n p) d -> (b n) p d", p=P)
    fv = fside.rearrange("b (n p) d -> (b n) p d", p=P)
    cv = ctx_in.rearrange("b (n p) d -> (b n) p d", p=P)
    ov = out.rearrange("b (n p) d -> (b n) p d", p=P)

    block = persistent.enter_context(nc.Block())
    LN_B, LN_C, LN_D = 0, B, 2 * B

    CN = DT + CT
    NEXT = {2: {3: (0,), TT: (1, 2, 3, 4, 5)}, 3: {1: (0,), 2: (1,), 3: (2, 3), TT: (4, 5)}}
    NEXT_BANKS = (4, 6, 7)
    FIRST = {1: (0, 1), 2: (2, 3), 3: (4, 5), 6: (6, 7), 7: (8, 9), 8: (10, 11)}
    FIRST_BANKS = (2, 3)
    HEAD_LINKS, MAIN_LINKS, TAIL_LINKS = 15, 26, 7

    F32R_AS_F32 = lambda ap: ap.bitcast(FP32)

    @block.sync
    def _(sp):
        for c, src in enumerate((g_xattn, g_ffn)):
            sp.dma_start(gates_raw[:, 2 * c:2 * c + 2], src.partition_broadcast(P)).then_inc(s_gates_in, 16)
        def load_first(b, first=False):
            if not first:
                sp.wait_ge(s_xin, 16 * b)
            sp.dma_start(xt[:, bass.ds(b * TT, TT), :],
                         xv[bass.ds(b * TT, TT), :, :].rearrange("n p d -> p n d")).then_inc(s_xin, 16)
            sp.wait_ge(s_ws1, LEAD + b)
            sp.dma_start(w1[:, :, :], fv[bass.ds(b * TT, TT), :, :].rearrange("n p d -> p n d")).then_inc(s_w1in, 16)

        def load_second(b):
            sp.wait_ge(s_ws2, LEAD + b)
            sp.dma_start(w2[:, :, :], cv[bass.ds(b * TT, TT), :, :].rearrange("n p d -> p n d")).then_inc(s_w2in, 16)

        load_first(0, first=True)
        load_second(0)
        sp.dma_start(ternary_raw[:, :].rearrange("p (n d) -> p n d", d=D),
                     w_fc.rearrange("(n p) d -> p n d", p=P)).then_inc(s_tw_in, 16)
        load_first(1)
        sp.wait_ge(s_tern, 1)
        sp.dma_start(ternary_raw[:, :].rearrange("p (n d) -> p n d", d=HF),
                     w_proj.rearrange("(n p) d -> p n d", p=P)).then_inc(s_tw_in, 16)
        load_second(1)
        with sp.Fori(2, B) as b:
            load_first(b)
            load_second(b)
        sp.wait_ge(s_bxn, B)

        def load_group(grp, g):
            sp.wait_ge(s_w1, LEAD + grp)
            for dst, w in ((wq_raw, wq), (wk_raw, wk), (wv_raw, wv)):
                src = w.rearrange("(n p) (g c) -> g p n c", p=P, g=NG)[bass.ds(g, 1), :, :, :]
                sp.dma_start(dst[:, :, :], src.rearrange("g p n c -> (g p) n c")).then_inc(s_w1raw, 16)
            sp.wait_ge(s_w2, LEAD + grp)
            src = wo.rearrange("(g n p) d -> g p n d", p=P, g=NG)[bass.ds(g, 1), :, :, :]
            sp.dma_start(wo_raw[:, :, :], src.rearrange("g p n d -> (g p) n d")).then_inc(s_w2raw, 16)

        for bp in range(2):
            if bp:
                sp.wait_ge(s_cl, 2 * CN)
                sp.wait_ge(s_pen, 1)
            for bl in range(2):
                b = bp * 2 + bl
                sp.dma_start(ctx_raw[:, bl, :, :],
                             cv[b * TT:(b + 1) * TT, :, :].rearrange("n p d -> p n d")).then_inc(s_cin, 16)
                sp.dma_start(mask_u8[:, bl, :], mask[b:b + 1, :].broadcast_to([P, S])).then_inc(s_min, 16)
            with sp.Fori(0, NG) as g:
                load_group(bp * NG + g, g)
        sp.wait_ge(s_yadd[1], LEAD + 2 * 2 * NG * 2)
        sp.dma_start(nw_raw[:, :], norm_w.partition_broadcast(NE)).then_inc(s_din, 16)
        sp.dma_start(rw_raw[:, :], router_w).then_inc(s_din, 16)
        with sp.Fori(0, B) as b:
            for i in range(NE // B):
                e = b * (NE // B) + i
                for dst, src in ((g_raw, gate_w), (u_raw, up_w), (d_raw, down_w)):
                    of_e = src.rearrange("e (n p) f -> e p n f", p=P)[bass.ds(e, 1), :, :, :]
                    sp.dma_start(dst[:, bass.ds(e, 1), :, :].rearrange("p e n f -> p (e n) f"),
                                 of_e.rearrange("e p n f -> p (e n) f")).then_inc(s_wraw, 16)
            sp.wait_ge(s_dxn, b + 1)
            sp.dma_start(normed_rows[bass.ds(b * S, S), :].rearrange("(n p) d -> p n d", p=P),
                         dxn[:, bass.ds(b * TT, TT), :]).then_inc(s_xst, 16)

        with sp.Fori(0, NTILE) as t:
            for h in range(2):
                sp.wait_ge(s_yrow[h], LEAD + t + 1)
                sp.dma_start(expert_rows[bass.ds(t * ROWS + h * P, P), :], yrow[h][:, :]).then_inc(s_yst[h], 16)
        with sp.Fori(0, B) as b:
            sp.wait_ge(s_dadd, TT * b + TT)
            sp.dma_start(ov[bass.ds(b * TT, TT), :, :].rearrange("n p d -> p n d"),
                         xt[:, bass.ds(b * TT, TT), :]).then_inc(s_out, 16)
        sp.wait_ge(s_out, 16 * B)

    @block.gpsimd
    def _(pool):
        for last_use in (s_ws1, s_ws2, s_bdone, s_h, s_cmT, s_blo, s_relu, s_yuse, s_w1, s_w2, s_q, s_y, s_ql, s_ol,
                         s_dxt, s_dxl, s_ssq, *s_exp, *s_max, *s_ptl, *s_yadd, *s_yrow):
            pool.sem_inc(last_use, LEAD)
        for last_use in (s_xst, *s_yst):
            pool.sem_inc(last_use, 16 * LEAD)
        G.memset(ident[:, :], 0.0).then_inc(c_pool, 1)
        G.memset(ones[:, :], 1.0)
        pool.wait_ge(c_pool, 1)
        G.affine_select(out=ident[:, :], in_=ident[:, :], compare_op=ALU.not_equal, fill=1.0, base=0,
                        pattern=[[-1, P]], channel_multiplier=1).then_inc(s_const, 1)
        def split(grp, part, hi, lo, raw, last=None):
            G.tensor_scalar(hi[:, :, :], raw[:, :, :], 1.0, 1.0, ALU.mult, ALU.mult).then_inc(c_pool, 1)
            wait_alone(pool, c_pool, 1 + grp * 4 + part + 1, s_passed)
            ins = G.tensor_tensor(lo[:, :, :], raw[:, :, :], F32R_AS_F32(hi[:, :, :]), ALU.subtract)
            if last is not None:
                ins.then_inc(last, 1)

        def split_k(grp):
            wait_alone(pool, s_w1raw, 48 * grp + 48, s_passed)
            wait_alone(pool, s_q, LEAD + grp * 4, s_passed)
            split(grp, 0, wkh, wkl, wk_raw)

        def split_v(grp):
            split(grp, 1, wvh, wvl, wv_raw)

        def split_q(grp):
            split(grp, 2, wqh, wql, wq_raw, s_w1)

        def split_out(grp):
            wait_alone(pool, s_w2raw, 16 * grp + 16, s_passed)
            wait_alone(pool, s_y, LEAD + grp * 8, s_passed)
            split(grp, 3, woh, wol, wo_raw, s_w2)

        def smoothed(b, k):
            width = (D, DC)[k]
            wait_alone(pool, s_srow, 2 * b + k + 1, s_passed)
            wait_alone(pool, (s_w1in, s_w2in)[k], 16 * b + 16, s_passed)
            G.tensor_tensor(ws[:, :, 0:width], (w1, w2)[k][:, :, :],
                            s_row[:, None, 0:width].broadcast_to([P, TT, width]), ALU.mult).then_inc((s_ws1, s_ws2)[k], 1)

        def rounded(b, k):
            width = (D, DC)[k]
            wait_alone(pool, s_wrq, 2 * b + k + 1, s_passed)
            for j in range(TT):
                ins = G.tensor_scalar(ws[:, j, 0:width], ws[:, j, 0:width], wrq[:, j:j + 1], MAGIC, ALU.mult, ALU.add)
            ins.then_inc(s_wmg, 1)

        def add_product(b):
            for j in range(TT):
                wait_alone(pool, s_h, LEAD + 8 * b + TT + j + 1, s_passed)
                xj = xt[:, bass.ds(b * TT + j, 1), :].rearrange("p o d -> p (o d)")
                G.tensor_tensor(xj, xj, hh[:, j, :], ALU.add).then_inc(s_xadd, 1)

        def square_lo(b, j):
            i = j % 2
            wait_alone(pool, s_sqh, b * HT + j + 1, s_passed)
            G.tensor_tensor(sql[i][:, :], sq[i][:, :], F32R_AS_F32(sqh[i][:, :]), ALU.subtract).then_inc(s_sql, 1)

        def iteration(b, main, feed, first_c=False):
            def slot(j):
                if feed:
                    square_lo(b - 1, j)

            if main:
                smoothed(b, 0)
            slot(0)
            if main:
                rounded(b, 0)
            slot(1)
            slot(2)
            slot(3)
            slot(4)
            slot(5)
            if first_c:
                split_k(0)
            if main:
                smoothed(b, 1)
            slot(6)
            if first_c:
                split_v(0)
            slot(7)
            if first_c:
                split_q(0)
            if main:
                rounded(b, 1)
            slot(8)
            if main:
                add_product(b)
            slot(9)

        iteration(0, True, False)
        with pool.Fori(1, B) as b:
            iteration(b, True, True)
        iteration(B, False, True, first_c=True)
        def normalize(n, h):
            for i in range(TT):
                wait_alone(pool, s_rinv, n * TT + i + 1, s_passed)
                ins = G.tensor_scalar(pr[h][:, i, :], pr[h][:, i, :], rinv[h][:, i:i + 1], 1.0, ALU.mult, ALU.mult)
            ins.then_inc(s_pn, 1)

        def group(n0, grp, last):
            normalize(n0 + 1, 1)
            normalize(n0 + 2, 0)
            if last is not None:
                split_k(grp + 1)
                split_v(grp + 1)
                split_q(grp + 1)
            normalize(n0 + 3, 1)
            if last is False:
                normalize(n0 + 4, 0)
            if last is not None:
                split_out(grp + 1)

        for bp in range(2):
            if bp == 0:
                pool.wait_ge(s_bdone, LEAD + B)
                split_out(0)
            normalize(bp * (4 * NG), 0)
            with pool.Fori(0, NG - 1) as g:
                group(bp * (4 * NG) + g * 4, bp * NG + g, False)
            group(bp * (4 * NG) + 4 * (NG - 1), bp * NG + (NG - 1), True if bp == 0 else None)
        pool.wait_ge(s_yadd[1], LEAD + 2 * 2 * NG * 2)
        small = dict(allow_small_or_imprecise_dtypes=True)
        G.iota(iota_e[:, :], pattern=[[1, NE]], base=0, channel_multiplier=0, **small)
        G.iota(iota_l[:, :], pattern=[[1, P]], base=0, channel_multiplier=0, **small)
        G.iota(iota_p[:, :], pattern=[[0, 1]], base=0, channel_multiplier=1, **small)
        G.iota(iota_j[:, :, :], pattern=[[0, 2], [1, B * TT]], base=0, channel_multiplier=0, **small)
        G.memset(onesb[:, :], 1.0)
        G.memset(keep[:, :, :], 1.0)
        G.memset(before[:, :], 1.0).then_inc(c_pool, 1)
        DP = 1 + 2 * NG * 4 + 1
        pool.wait_ge(c_pool, DP)
        G.memset(keep[:, :, 0:1], 0.0)
        G.affine_select(out=before[:, :], in_=before[:, :], compare_op=ALU.is_gt, fill=0.0, base=0,
                        pattern=[[1, P]], channel_multiplier=-1).then_inc(s_iota, 1)

        def gather(t, i, k, early=False):
            if not early:
                wait_alone(pool, s_gat[i], 32 * k, s_passed)
                wait_alone(pool, s_gT, 2 * t - 2, s_passed)
            G.tensor_copy(icur[i][:, :], row_tok[:, bass.ds(2 * t, 2)]).then_inc(s_icur, 1)
            wait_alone(pool, s_icur, t + 1, s_passed)
            for h in range(2):
                G.indirect_dma_start(xg[:, i, h, :], None, normed_rows,
                                     bass.IndirectOffsetOnAxis(ap=icur[i][:, h:h + 1], axis=0),
                                     bounds_check=B * S - 1).then_inc(s_gat[i], 16)

        def split_down(t):
            e = pool.value_load(tile_e[0:1, bass.ds(t, 1)], min_val=0, max_val=NE - 1)
            wait_alone(pool, s_dhi, t + 1, s_passed)
            G.tensor_tensor(dwl[:, :, :].rearrange("p n d -> p (n d)"),
                            d_raw[:, bass.ds(e, 1), :, :].rearrange("p e n d -> p (e n d)"),
                            F32R_AS_F32(dwh[:, :, :].rearrange("p n d -> p (n d)")), ALU.subtract).then_inc(s_dns, 1)

        pool.wait_ge(s_plan, 1)
        pool.wait_ge(s_xst, 16 * LEAD + 16 * B)
        gather(0, 0, 0, early=True)
        gather(1, 1, 0, early=True)
        pool.wait_ge(s_wraw, 16 * 3 * NE)
        gather(2, 0, 1)
        split_down(0)
        with pool.Fori(0, (NTILE - 3) // 2) as pair:
            for i in range(2):
                gather(pair * 2 + i + 3, (i + 1) % 2, pair + (i + 3) // 2)
                split_down(pair * 2 + i + 1)
        for t in range(NTILE - 2, NTILE):
            split_down(t)
        for h in range(2):
            pool.wait_ge(s_yst[h], 16 * LEAD + 16 * NTILE)
        with pool.Fori(0, B) as b:
            for i in range(TT):
                wait_alone(pool, s_pcur, b * TT + i + 1, s_passed)
                for c in range(2):
                    G.indirect_dma_start(back[i][c][:, :], None, expert_rows,
                                         bass.IndirectOffsetOnAxis(ap=pcur[i][:, c:c + 1], axis=0),
                                         bounds_check=NTILE * ROWS - 1).then_inc(s_back[i], 16)

    @block.scalar
    def _(act):
        act.wait_ge(s_gates_in, 32)
        A.activation(gates[:, :], gates_raw[:, :], ACT.Tanh).then_inc(s_gates, 1)
        act.wait_ge(s_constb, 1)

        def ln_std(n):
            act.wait_ge(s_var, n + 1)
            A.activation(std[:, :], mv[:, :, 1], ACT.Sqrt, bias=eps_ln[:, :]).then_inc(s_std, 1)

        def a_std_of(b):
            act.wait_ge(s_avar, b + 1)
            A.activation(a_std[:, :], a_mv[:, :, 1], ACT.Sqrt, bias=eps_ln[:, :]).then_inc(s_astd, 1)

        def smooth_root(b, k):
            n = (DT, CT)[k]
            act.wait_ge(s_ratio, 2 * b + k + 1)
            A.activation(smooth[:, 0:n], ratio[:, 0:n], ACT.Sqrt).then_inc(s_sqrt, 1)

        def evict_row(b, k):
            act.wait_ge(s_rows, 2 * b + k + 1)
            if k == 0:
                A.activation(s_row[:, :], ps[:, 2, :], ACT.Copy).then_inc(s_srow, 1)
            else:
                A.activation(s_row[:, 0:DC], ps[:, 3, 0:DC], ACT.Copy).then_inc(s_srow, 1)

        def evict_x(b, k):
            act.wait_ge(s_qxT, 2 * b + k + 1)
            n = (DT, CT)[k]
            A.activation(qxT[:, 0:n, :].rearrange("p n s -> p (n s)"), psb[:, 2048:2048 + n * S], ACT.Copy).then_inc(s_qxE, 1)

        def evict_w(b, k):
            act.wait_ge(s_qwT, 2 * b + k + 1)
            n, c = (DT, CT)[k], (2048, 3072)[k]
            A.activation(qwT[:, 0:n, :].rearrange("p n s -> p (n s)"), psb[:, c:c + n * S], ACT.Copy).then_inc(s_qwE, 1)

        def evict_scale(b, k):
            act.wait_ge(s_bc, 2 * b + k + 1)
            A.activation(wsc_row[:, :], ps[:, 2, :], ACT.Copy).then_inc(s_bcE, 1)

        def a_silu(b):
            act.wait_ge(s_h, LEAD + 8 * b + TT)
            A.activation(hh[:, :, 0:IH], hh[:, :, 0:IH], ACT.Silu).then_inc(s_silu, 1)

        def normed(b):
            act.wait_ge(s_bnb, b + 1)
            for j in range(TT):
                ins = A.activation(xn[:, j, :], xt[:, bass.ds(b * TT + j, 1), :].rearrange("p o d -> p (o d)"),
                                   ACT.Identity, bias=b_shift[:, j:j + 1], scale=rstd[:, j:j + 1])
            ins.then_inc(s_bxn, 1)

        def turned_hi(b):
            for t in range(DT):
                act.wait_ge(s_bxt, b * DT + t + 1)
                A.activation(bxh[:, t, :], ps[:, t % 2, :], ACT.Copy).then_inc(s_bhi, 1)

        def squares(b, j):
            i, k = j % 2, b * HT + j
            act.wait_ge(s_hps, k + 1)
            A.activation(relu[i][:, :], ps[:, i, :], ACT.Relu, scale=h_scale[:, :]).then_inc(s_relu, 1)
            act.wait_ge(s_relu, LEAD + k + 1)
            if j >= 2:
                act.wait_ge(s_yuse, LEAD + k - 1)
            else:
                act.wait_ge(s_yuse, LEAD + b * HT)
            A.activation(sq[i][:, :], relu[i][:, :], ACT.Square).then_inc(s_sq, 1)
            act.wait_ge(s_sq, k + 1)
            A.activation(sqh[i][:, :], sq[i][:, :], ACT.Copy).then_inc(s_sqh, 1)

        def ternary_abs(m):
            act.wait_ge(s_tw_in, 16 * m + 16)
            if m:
                act.wait_ge(s_ternT, DT)
            A.activation(ternary_bf[:, :], ternary_raw[:, :], ACT.Abs, accum_out=wabs[:, m:m + 1]).then_inc(s_wabs, 1)

        def ternary_out(m):
            dst, n_in, n_out = ((t_fc, HT, DT), (t_pr, DT, HT))[m]
            for o in range(n_out):
                k = m * DT + o
                act.wait_ge(s_ternT, k + 1)
                A.activation(dst[:, o, :], psb[:, 4096 + 2048 * (k % 2):4096 + 2048 * (k % 2) + n_in * P], ACT.Copy).then_inc(s_ternE, 1)

        def next_hi(b, k, bank):
            act.wait_ge(s_ct, b * CN + k + 1)
            dst = xTh[:, b % 2, k, :] if k < DT else cTh[:, b % 2, k - DT, :]
            A.activation(dst, ps[:, bank, :], ACT.Copy).then_inc(s_ch, 1)

        def iteration(b, main, feed, ahead, tern=False, first_c=False):
            def slot(j):
                if first_c and j == 0:
                    ln_std(LN_C)
                if feed:
                    squares(b - 1, j)
                if first_c and j == 5:
                    ln_std(LN_C + 1)
                if first_c:
                    for g in FIRST.get(j, ()):
                        next_hi(g // CN, g % CN, FIRST_BANKS[g % 2])

            slot(0)
            if tern:
                ternary_abs(0)
            slot(1)
            if main:
                evict_x(b, 0)
            slot(2)
            if main:
                evict_w(b, 0)
                evict_scale(b, 0)
            slot(3)
            if main:
                a_silu(b)
            if tern:
                ternary_out(0)
            slot(4)
            if main:
                smooth_root(b, 1)
            if ahead:
                a_std_of(b + 1)
            if tern:
                ternary_abs(1)
            slot(5)
            slot(6)
            if main:
                evict_row(b, 1)
            slot(7)
            slot(8)
            if main:
                evict_x(b, 1)
                evict_w(b, 1)
                evict_scale(b, 1)
            slot(9)
            if ahead:
                smooth_root(b + 1, 0)
            if main:
                ln_std(LN_B + b)
            if ahead:
                evict_row(b + 1, 0)
            if main:
                normed(b)
                turned_hi(b)
            if tern:
                ternary_out(1)

        a_std_of(0)
        smooth_root(0, 0)
        evict_row(0, 0)
        iteration(0, True, False, True, tern=True)
        with act.Fori(1, B - 1) as b:
            iteration(b, True, True, True)
        iteration(B - 1, True, True, False)
        iteration(B, False, True, False, first_c=True)
        def exps(n, i, h):
            act.wait_ge(s_nb, n * TT + i + 1)
            A.activation(pr[h][:, i, :], sm[i][:, :], ACT.Exp, bias=nbias[h][:, i:i + 1], scale=SCALE,
                         accum_out=rsum[h][:, i:i + 1]).then_inc(s_exp[i], 1)

        def evict_k(m, bl):
            act.wait_ge(s_kv, 2 * m + 1)
            A.activation(kh[bl][:, :], ps[:, 6, :], ACT.Copy).then_inc(s_kh, 1)
            act.wait_ge(s_kv, 2 * m + 2)
            A.activation(vT[:, :], ps[:, 7, :], ACT.Copy).then_inc(s_vT, 1)

        def evict_v(m, bl):
            act.wait_ge(s_vt, m + 1)
            A.activation(vh[bl][:, :, :].rearrange("p n d -> p (n d)"), ps[:, 7, :], ACT.Copy).then_inc(s_vh, 1)

        def evict_q(n, h, bank=4):
            act.wait_ge(s_q, LEAD + n + 1)
            A.activation(qh[h][:, :], ps[:, bank, :], ACT.Copy).then_inc(s_qh, 1)

        def group(n0, m0, last, following=None):
            for u in range(4):
                n, h = n0 + u, u % 2
                steps = NEXT.get(u, {}) if following is not None else {}
                nb = None if following is None else following + u - 2
                if steps and u == 3:
                    ln_std(LN_C + nb)
                for i in range(TT):
                    act.wait_ge(s_pt, n * TT + i + 1)
                    A.activation(pTh[:, i, :], ps[:, 2 + i % 2, :], ACT.Copy).then_inc(s_pth, 1)
                    if not (last and u == 3):
                        exps(n + 1, i, 1 - h)
                    if steps and u == 2 and i == 1:
                        ln_std(LN_C + nb)
                    for k in steps.get(i, ()):
                        next_hi(nb, k, NEXT_BANKS[(nb * CN + k) % 3])
                more_q = not (last and u >= 2)
                if h == 0 and more_q:
                    evict_q(n + 2, h)
                    evict_k(m0 + u // 2 + 1, (u // 2 + 1) % 2)
                act.wait_ge(s_o, n + 1)
                A.activation(oh[h][:, :], ps[:, 5, :], ACT.Copy).then_inc(s_oh, 1)
                if h == 0 and more_q:
                    evict_v(m0 + u // 2 + 1, (u // 2 + 1) % 2)
                if h == 1 and more_q:
                    evict_q(n + 2, h)
                for k in steps.get(TT, ()):
                    next_hi(nb, k, NEXT_BANKS[(nb * CN + k) % 3])

        for bp in range(2):
            n0, m0 = bp * (4 * NG), bp * (2 * NG)
            evict_q(n0, 0, bank=0)
            evict_k(m0, 0)
            evict_v(m0, 0)
            for i in range(TT):
                exps(n0, i, 0)
            evict_q(n0 + 1, 1)
            with act.Fori(0, NG - 1) as g:
                group(n0 + g * 4, m0 + g * 2, False)
            group(n0 + 4 * (NG - 1), m0 + 2 * (NG - 1), True, following=2 if bp == 0 else None)
        def router_batch(b):
            for t in range(DT):
                act.wait_ge(s_dxt, LEAD + b * DT + t + 1)
                A.activation(dxh[:, t, :], ps[:, t, :], ACT.Copy).then_inc(s_dxh, 1)
            for i in range(TT):
                act.wait_ge(s_ssq, LEAD + b * TT + i)
                A.activation(ps[:, 6, :], dxn[:, bass.ds(b * TT + i, 1), :].rearrange("p o d -> p (o d)"), ACT.Square,
                             accum_out=ssq[:, bass.ds(b * TT + i, 1)]).then_inc(s_ssq, 1)
            act.wait_ge(s_lgT, b + 1)
            A.activation(lgT[:, :], ps[0:NE, 4, :], ACT.Copy).then_inc(s_lgTE, 1)

        ln_std(LN_D)
        with act.Fori(0, B - 1) as b:
            ln_std(LN_D + b + 1)
            router_batch(b)
        router_batch(B - 1)
        act.wait_ge(s_ssq, LEAD + B * TT)
        A.activation(rms[:, :], ssq[:, :], ACT.Sqrt, bias=eps_q[:, :], scale=1.0 / D).then_inc(s_rms, 1)
        act.wait_ge(s_lc, 1)
        A.activation(pe_[:, :, :], lg[:, :, :], ACT.Exp).then_inc(s_lexp, 1)

        def hi_gate_up(t, i, early=False):
            e = act.value_load(tile_e[0:1, bass.ds(t, 1)], min_val=0, max_val=NE - 1)
            if not early:
                act.wait_ge(s_gu, 2 * t - 2)
            for dst, src in ((gwh[i], g_raw), (uwh[i], u_raw)):
                A.activation(dst[:, :, :].rearrange("p n f -> p (n f)"),
                             src[:, bass.ds(e, 1), :, :].rearrange("p e n f -> p (e n f)"), ACT.Copy).then_inc(s_guhi, 1)

        def hi_down(t, early=False):
            e = act.value_load(tile_e[0:1, bass.ds(t, 1)], min_val=0, max_val=NE - 1)
            if not early:
                act.wait_ge(s_dy, 2 * t)
            A.activation(dwh[:, :, :].rearrange("p n d -> p (n d)"),
                         d_raw[:, bass.ds(e, 1), :, :].rearrange("p e n d -> p (e n d)"), ACT.Copy).then_inc(s_dhi, 1)

        def hi_rows(t):
            for k in range(2):
                act.wait_ge(s_gT, 2 * t + k + 1)
                A.activation(gxh[:, 2 * k:2 * k + 2, :].rearrange("p n r -> p (n r)"), ps[:, k, :], ACT.Copy).then_inc(s_gxh, 1)

        def silu(t, i):
            act.wait_ge(s_gu, 2 * t + 1)
            A.activation(sg[:, :], ps[:, 2 + 4 * i, :], ACT.Silu).then_inc(s_sg, 1)

        def hi_gated(t, i):
            act.wait_ge(s_au, t + 1)
            A.activation(auh[i][:, :, :].rearrange("p f r -> p (f r)"), au[:, :], ACT.Copy).then_inc(s_auh, 1)

        def rows_out(t):
            for h in range(2):
                act.wait_ge(s_dy, 2 * t + h + 1)
                act.wait_ge(s_yst[h], 16 * LEAD + 16 * t)
                A.activation(yrow[h][:, :], ps[:, 4 + h, :], ACT.Copy).then_inc(s_yrow[h], 1)

        act.wait_ge(s_plan, 1)
        act.wait_ge(s_xst, 16 * LEAD + 16 * B)
        act.wait_ge(s_wraw, 16 * 3 * NE)
        hi_gate_up(0, 0, early=True)
        hi_rows(0)
        hi_gate_up(1, 1, early=True)
        silu(0, 0)
        hi_rows(1)
        hi_gated(0, 0)
        hi_gate_up(2, 0)
        hi_down(0, early=True)

        def slot(t, i):
            silu(t + 1, 1 - i)
            hi_rows(t + 2)
            hi_gated(t + 1, 1 - i)
            hi_gate_up(t + 3, 1 - i)
            rows_out(t)
            hi_down(t + 1)

        with act.Fori(0, (NTILE - 3) // 2) as pair:
            for i in range(2):
                slot(pair * 2 + i, i)
        t = NTILE - 3
        silu(t + 1, 1)
        hi_rows(t + 2)
        hi_gated(t + 1, 1)
        rows_out(t)
        hi_down(t + 1)
        silu(t + 2, 0)
        hi_gated(t + 2, 0)
        rows_out(t + 1)
        hi_down(t + 2)
        rows_out(t + 2)

    @block.vector
    def _(dve):
        V.memset(eps_ln[:, :], LN_EPS)
        V.memset(eps_q[:, :], Q_EPS)
        dve.wait_ge(s_const, 1)
        V.tensor_copy(identb[:, :], ident[:, :]).then_inc(s_constb, 1)

        def norm_stats(ch, tile0, added=None):
            for j in range(TT):
                if added is not None:
                    wait_alone(dve, s_xadd, added + j + 1, s_passed)
                ins = V.bn_stats(stats[:, j, :], xt[:, bass.ds(tile0 + j, 1), :].rearrange("p o d -> p (o d)"))
            ch.link(ins, s_passed)
            for j in range(TT):
                ins = V.bn_aggr(mv[:, j, :], stats[:, j, :])
            ins.then_inc(s_var, 1)

        def norm_apply(ch, tile0, n, done, into=None):
            dve.wait_ge(s_std, n + 1)
            ch.link(V.reciprocal(rstd[:, :], std[:, :]))
            for j in range(TT):
                dst = xn[:, j, :] if into is None else into[:, bass.ds(tile0 + j, 1), :].rearrange("p o d -> p (o d)")
                ins = V.tensor_scalar(dst, xt[:, bass.ds(tile0 + j, 1), :].rearrange("p o d -> p (o d)"),
                                      mv[:, j, 0:1], rstd[:, j:j + 1], ALU.subtract, ALU.mult)
            ins.then_inc(done, 1)

        def norm_factors(ch, b):
            dve.wait_ge(s_std, LN_B + b + 1)
            ch.link(V.reciprocal(rstd[:, :], std[:, :]))
            V.scalar_tensor_tensor(b_shift[:, :], mv[:, :, 0], -1.0, rstd[:, :], ALU.mult, ALU.mult).then_inc(s_bnb, 1)

        def head_stats(ch, b):
            wait_alone(dve, s_xin, 16 * b + 16, s_passed)
            for j in range(TT):
                ins = V.bn_stats(a_stats[:, j, :], xt[:, bass.ds(b * TT + j, 1), :].rearrange("p o d -> p (o d)"))
            ch.link(ins, s_passed)
            for j in range(TT):
                ins = V.bn_aggr(a_mv[:, j, :], a_stats[:, j, :])
            ins.then_inc(s_avar, 1)

        def head_norm(ch, b):
            dve.wait_ge(s_astd, b + 1)
            ch.link(V.reciprocal(a_rstd[:, :], a_std[:, :]))
            ch.link(V.scalar_tensor_tensor(a_fine[:, :], a_mv[:, :, 1], LN_EPS, a_rstd[:, :], ALU.add, ALU.mult))
            ch.link(V.tensor_tensor(a_fine[:, :], a_fine[:, :], a_std[:, :], ALU.add))
            ch.link(V.tensor_scalar(a_fine[:, :], a_fine[:, :], 0.5, None, ALU.mult))
            ch.link(V.reciprocal(a_rstd[:, :], a_fine[:, :]))
            for j in range(TT):
                ins = V.tensor_scalar(xa[:, j, :], xt[:, bass.ds(b * TT + j, 1), :].rearrange("p o d -> p (o d)"),
                                      a_mv[:, j, 0:1], a_rstd[:, j:j + 1], ALU.subtract, ALU.mult)
            ch.link(ins)

        def head_colmax_w(b, first=False):
            if not first:
                dve.wait_ge(s_cmT, LEAD + 2 * b - 1)
            wait_alone(dve, s_w1in, 16 * b + 16, s_passed)
            V.tensor_reduce(cmax[:, 0:D], w1[:, :, :].rearrange("p n d -> p d n"), AX.X,
                            ALU.max, apply_absolute_value=True).then_inc(s_cm, 1)

        def down_colmax(b):
            wait_alone(dve, s_w2in, 16 * b + 16, s_passed)
            V.tensor_reduce(cmax2[:, 0:DC], w2[:, :, :].rearrange("p n d -> p d n"), AX.X,
                            ALU.max, apply_absolute_value=True)

        def head_colmax_x(ch, b):
            V.tensor_reduce(cmax[:, D:], xa[:, :, :].rearrange("p n d -> p d n"), AX.X,
                            ALU.max, apply_absolute_value=True).then_inc(s_cm, 1)

        def smooth_ratio(ch, b, k):
            n = (DT, CT)[k]
            dve.wait_ge(s_cmT, LEAD + 2 * b + k + 1)
            ch.link(V.tensor_reduce(amax[:, 0:2 * n], ps[:, 2:4, :].rearrange("p k (n c) -> p (k n) c", c=P)[:, 0:2 * n, :],
                                    AX.X, ALU.max, apply_absolute_value=True))
            ch.link(V.tensor_scalar(amax[:, 0:2 * n], amax[:, 0:2 * n], Q_EPS, None, ALU.max))
            ch.link(V.reciprocal(winv[:, 0:n], amax[:, 0:n]))
            V.tensor_tensor(ratio[:, 0:n], amax[:, n:2 * n], winv[:, 0:n], ALU.mult).then_inc(s_ratio, 1)

        def smooth_diagonals(ch, b, k):
            n = (DT, CT)[k]
            dve.wait_ge(s_sqrt, 2 * b + k + 1)
            ch.link(V.reciprocal(refine[:, 0:n], smooth[:, 0:n]))
            ch.link(V.tensor_tensor(refine[:, 0:n], refine[:, 0:n], ratio[:, 0:n], ALU.mult))
            ch.link(V.tensor_tensor(smooth[:, 0:n], smooth[:, 0:n], refine[:, 0:n], ALU.add))
            ch.link(V.tensor_scalar(smooth[:, 0:n], smooth[:, 0:n], 0.5, Q_EPS, ALU.mult, ALU.max))
            ch.link(V.reciprocal(smooth_inv[:, 0:n], smooth[:, 0:n]))
            eye = ident[:, None, :].broadcast_to([P, n, P])
            V.tensor_tensor(diag_s[:, 0:n, :], eye, smooth[:, 0:n, None].broadcast_to([P, n, P]), ALU.mult)
            V.tensor_tensor(diag_i[:, 0:n, :], eye, smooth_inv[:, 0:n, None].broadcast_to([P, n, P]),
                            ALU.mult).then_inc(s_dg, 1)

        def quantize_x(ch, b, k, x_):
            for j in range(TT):
                ins = V.tensor_scalar(x_[:, j, :], x_[:, j, :], xrq[:, j:j + 1], MAGIC, ALU.mult, ALU.add)
            ch.link(ins)

        def smooth_x(ch, b, k, x_):
            width = (D, DC)[k]
            inv_row = (ps[:, 3, None, :], ps[:, 2, None, 0:DC])[k]
            wait_alone(dve, s_rows, 2 * b + k + 1, s_passed)
            ch.link(V.tensor_tensor(x_, x_, inv_row.broadcast_to([P, TT, width]), ALU.mult))
            ch.link(V.tensor_reduce(rowmax[:, :], x_, AX.X, ALU.max, apply_absolute_value=True))
            ch.link(V.tensor_scalar(xsc[:, :], rowmax[:, :], Q_EPS, 1.0 / QMAX, ALU.max, ALU.mult))
            ch.link(V.reciprocal(xrq[:, :], xsc[:, :]))

        def integers_x(k, x_):
            V.tensor_scalar(qx[:, :, 0:(D, DC)[k]], x_, -MAGIC, QMAX, ALU.add, ALU.min).then_inc(s_qx, 1)

        def scale_w(ch, b, k):
            width = (D, DC)[k]
            wait_alone(dve, (s_ws1, s_ws2)[k], LEAD + b + 1, s_passed)
            ch.link(V.tensor_reduce(wrowmax[:, :], ws[:, :, 0:width], AX.X, ALU.max, apply_absolute_value=True))
            ch.link(V.tensor_scalar(wsc[:, :], wrowmax[:, :], Q_EPS, 1.0 / QMAX, ALU.max, ALU.mult))
            V.reciprocal(wrq[:, :], wsc[:, :]).then_inc(s_wrq, 1)

        def scale_diagonal():
            V.tensor_tensor(diag_w[:, :, :], ident[:, None, :].broadcast_to([P, TT, P]),
                            wsc[:, :, None].broadcast_to([P, TT, P]), ALU.mult)

        def quantize_w(b, k):
            width = (D, DC)[k]
            dve.wait_ge(s_wmg, 2 * b + k + 1)
            V.tensor_scalar(qw[:, :, 0:width], ws[:, :, 0:width], -MAGIC, QMAX, ALU.add, ALU.min).then_inc(s_qw, 1)

        def dequantize(b, k):
            dve.wait_ge(s_bcE, 2 * b + k + 1)
            for j in range(TT):
                dve.wait_ge(s_mm, 8 * b + k * TT + j + 1)
                V.scalar_tensor_tensor(hh[:, j, :], ps[:, 3 - j % 2, :], xsc[:, j:j + 1], wsc_row[:, :],
                                       ALU.mult, ALU.mult).then_inc(s_h, 1)

        def gated_product(ch, b):
            dve.wait_ge(s_silu, b + 1)
            ch.link(V.tensor_tensor(hh[:, :, 0:IH], hh[:, :, 0:IH], hh[:, :, IH:], ALU.mult))
            V.tensor_reduce(cmax2[:, DC:], hh[:, :, 0:IH].rearrange("p n d -> p d n"), AX.X,
                            ALU.max, apply_absolute_value=True).then_inc(s_cm2, 1)

        def turned_lo(b):
            for t in range(DT):
                dve.wait_ge(s_bhi, b * DT + t + 1)
                V.tensor_tensor(bxl[:, t, :], ps[:, t % 2, :], F32R_AS_F32(bxh[:, t, :]), ALU.subtract).then_inc(s_blo, 1)

        def add_feed(b):
            dve.wait_ge(s_by, b + 1)
            for j in range(TT):
                xj = xt[:, bass.ds(b * TT + j, 1), :].rearrange("p o d -> p (o d)")
                ins = V.scalar_tensor_tensor(xj, ps[:, 4 + j, :], y_scale[:, :], xj, ALU.mult, ALU.add)
            ins.then_inc(s_bdone, 1)

        def ternary_threshold(m):
            ch = Chain(dve, c_dve, m * 4)
            dve.wait_ge(s_wtot, m + 1)
            ch.link(V.tensor_scalar(wmean[:, m:m + 1], ps[:, 7, m:m + 1], 1.0 / (HF * D), 1e-5, ALU.mult, ALU.max))
            ch.link(V.tensor_scalar(wthr[:, m:m + 1], wmean[:, m:m + 1], 0.7, None, ALU.mult))
            ch.link(V.tensor_scalar(wnthr[:, m:m + 1], wthr[:, m:m + 1], -1.0, None, ALU.mult))

        def ternary(m):
            ch = Chain(dve, c_dve, m * 4 + 3)
            ch.link(V.tensor_scalar(ternary_bf[:, :], ternary_raw[:, :], wnthr[:, m:m + 1], None, ALU.is_lt))
            V.scalar_tensor_tensor(ternary_bf[:, :], ternary_raw[:, :], wthr[:, m:m + 1], ternary_bf[:, :],
                                   ALU.is_gt, ALU.subtract).then_inc(s_tern, 1)

        def iteration(b, main, feed, ahead, tern=False):
            if main:
                ch = Chain(dve, c_main, b * MAIN_LINKS)
                hd = Chain(dve, c_head, (b + 1) * HEAD_LINKS)
                ch.n = TAIL_LINKS
                integers_x(0, xa[:, :, :])
                if tern:
                    ternary_threshold(0)
                scale_diagonal()
                if ahead:
                    head_stats(hd, b + 1)
                quantize_w(b, 0)
                if ahead:
                    head_colmax_w(b + 1)
                if tern:
                    ternary(0)
                dequantize(b, 0)
                down_colmax(b)
                gated_product(ch, b)
                smooth_ratio(ch, b, 1)
                smooth_diagonals(ch, b, 1)
                if ahead:
                    head_norm(hd, b + 1)
                if tern:
                    ternary_threshold(1)
                smooth_x(ch, b, 1, hh[:, :, 0:DC])
                quantize_x(ch, b, 1, hh[:, :, 0:DC])
                scale_w(ch, b, 1)
                integers_x(1, hh[:, :, 0:DC])
                scale_diagonal()
                ch.link(V.tensor_scalar(xsc[:, :], xsc[:, :], gates[:, 0:1], None, ALU.mult))
                quantize_w(b, 1)
                if ahead:
                    head_colmax_x(hd, b + 1)
                dequantize(b, 1)
                if ahead:
                    smooth_ratio(hd, b + 1, 0)
                norm_stats(ch, b * TT, added=b * TT)
                if ahead:
                    smooth_diagonals(hd, b + 1, 0)
                    assert hd.n == HEAD_LINKS, hd.n
                norm_factors(ch, b)
                if tern:
                    ternary(1)
                    V.tensor_copy(h_scale[:, :], wmean[:, 0:1])
                    V.tensor_scalar(y_scale[:, :], wmean[:, 1:2], gates[:, 2:3], None, ALU.mult)
                assert ch.n == MAIN_LINKS, ch.n
                if ahead:
                    ch = Chain(dve, c_main, (b + 1) * MAIN_LINKS)
                    smooth_x(ch, b + 1, 0, xa[:, :, :])
                turned_lo(b)
                if ahead:
                    quantize_x(ch, b + 1, 0, xa[:, :, :])
                    scale_w(ch, b + 1, 0)
                    assert ch.n == TAIL_LINKS, ch.n
            if feed:
                add_feed(b - 1)

        C_BASE = 8

        def next_stats(b):
            norm_stats(Chain(dve, c_dve, C_BASE + 2 * b + 2 * (b // 2)), b * TT)

        def next_norm(b):
            if b:
                dve.wait_ge(s_ct, (b - 1) * CN + DT)
            norm_apply(Chain(dve, c_dve, C_BASE + 2 * b + 2 * (b // 2) + 1), b * TT, LN_C + b, s_cxn)

        def next_lo(b, k, bank):
            dve.wait_ge(s_ch, b * CN + k + 1)
            hi, lo = (t[:, b % 2, k, :] for t in (xTh, xTl)) if k < DT else (t[:, b % 2, k - DT, :] for t in (cTh, cTl))
            V.tensor_tensor(lo, ps[:, bank, :], F32R_AS_F32(hi), ALU.subtract).then_inc(s_cl, 1)

        def penalties(bp):
            ch = Chain(dve, c_dve, C_BASE + 4 * (bp + 1) + 2 * bp)
            dve.wait_ge(s_min, bp * 32 + 32)
            ch.link(V.tensor_scalar(pen[:, :, :], mask_u8[:, :, :], MASKED, -MASKED, ALU.mult, ALU.add))
            V.tensor_reduce(valid[:, :], mask_u8[:, :, :], AX.X, ALU.max).then_inc(s_pen, 1)
            dve.wait_ge(s_pen, bp + 1)
            ch.link(V.tensor_scalar(y_gate[:, :], valid[:, :], gates[:, 1:2], None, ALU.mult))

        dve.wait_ge(s_gates, 1)
        hd = Chain(dve, c_head, 0)
        head_stats(hd, 0)
        head_colmax_w(0, first=True)
        head_norm(hd, 0)
        head_colmax_x(hd, 0)
        smooth_ratio(hd, 0, 0)
        smooth_diagonals(hd, 0, 0)
        ch = Chain(dve, c_main, 0)
        smooth_x(ch, 0, 0, xa[:, :, :])
        quantize_x(ch, 0, 0, xa[:, :, :])
        scale_w(ch, 0, 0)
        iteration(0, True, False, True, tern=True)
        with dve.Fori(1, B - 1) as b:
            iteration(b, True, True, True)
        iteration(B - 1, True, True, False)
        for b in range(2):
            next_stats(b)
            next_norm(b)
            for k in range(CN):
                next_lo(b, k, FIRST_BANKS[(b * CN + k) % 2])
        penalties(0)
        iteration(B, False, True, False)
        dve.wait_ge(s_bdone, LEAD + B)
        base = C_BASE + 12

        def row_max(n, i, h, bl):
            dve.wait_ge(s_exp[i], LEAD + n)
            wait_alone(dve, s_s, n * TT + i + 1, s_passed)
            V.tensor_tensor_reduce(out=sm[i][:, :], in0=ps[:, i % 2, :], in1=pen[:, bl, :], scale=1.0,
                                   scalar=-3.0e38, op0=ALU.add, op1=ALU.max,
                                   accum_out=smax[h][:, i:i + 1]).then_inc(s_max[i % 2], 1)
            dve.wait_ge(s_max[i % 2], LEAD + n * 2 + i // 2 + 1)
            V.tensor_scalar(nbias[h][:, i:i + 1], smax[h][:, i:i + 1], -SCALE, None, ALU.mult).then_inc(s_nb, 1)

        def lo_k(m, bl):
            dve.wait_ge(s_kh, m + 1)
            V.tensor_tensor(kl[bl][:, :], ps[:, 6, :], F32R_AS_F32(kh[bl][:, :]), ALU.subtract).then_inc(s_kl, 1)

        def lo_v(m, bl):
            dve.wait_ge(s_vh, m + 1)
            V.tensor_tensor(vl[bl][:, :, :].rearrange("p n d -> p (n d)"), ps[:, 7, :],
                            F32R_AS_F32(vh[bl][:, :, :].rearrange("p n d -> p (n d)")), ALU.subtract).then_inc(s_vl, 1)

        def lo_q(n, h, bank=4):
            dve.wait_ge(s_qh, n + 1)
            V.tensor_tensor(ql[h][:, :], ps[:, bank, :], F32R_AS_F32(qh[h][:, :]), ALU.subtract).then_inc(s_ql, 1)

        def inverse_sum(n, i, h):
            dve.wait_ge(s_exp[i], LEAD + n + 1)
            V.reciprocal(rinv[h][:, i:i + 1], rsum[h][:, i:i + 1]).then_inc(s_rinv, 1)

        def group(bp, n0, m0, last, following=None):
            for u in range(4):
                n, bl, h = n0 + u, u // 2, u % 2
                more_s, more_q = not (last and u == 3), not (last and u >= 2)
                steps = NEXT.get(u, {}) if following is not None else {}
                nb = None if following is None else following + u - 2
                for i in range(TT):
                    if more_s:
                        row_max(n + 1, i, 1 - h, ((u + 1) // 2) % 2)
                    dve.wait_ge(s_pth, n * TT + i + 1)
                    V.tensor_tensor(pTl[:, i, :], ps[:, 2 + i % 2, :], F32R_AS_F32(pTh[:, i, :]),
                                    ALU.subtract).then_inc(s_ptl[i % 2], 1)
                    if more_s and i:
                        inverse_sum(n + 1, i - 1, 1 - h)
                    if steps and u == 2 and i == 0:
                        next_stats(nb)
                    if steps and i == (1 if u == 2 else 0):
                        next_norm(nb)
                    for k in steps.get(i, ()):
                        next_lo(nb, k, NEXT_BANKS[(nb * CN + k) % 3])
                if more_s:
                    inverse_sum(n + 1, TT - 1, 1 - h)
                if h == 0 and more_q:
                    lo_q(n + 2, h)
                    lo_k(m0 + u // 2 + 1, (u // 2 + 1) % 2)
                dve.wait_ge(s_oh, n + 1)
                V.tensor_tensor(ol[h][:, :], ps[:, 5, :], F32R_AS_F32(oh[h][:, :]), ALU.subtract).then_inc(s_ol, 1)
                if h == 0 and more_q:
                    lo_v(m0 + u // 2 + 1, (u // 2 + 1) % 2)
                if h == 1 and more_q:
                    lo_q(n + 2, h)
                for k in steps.get(TT, ()):
                    next_lo(nb, k, NEXT_BANKS[(nb * CN + k) % 3])
                if steps and u == 2:
                    next_stats(nb + 1)
                if h == 1:
                    m = m0 + bl
                    for j in range(TT):
                        dve.wait_ge(s_y, LEAD + m * TT + j + 1)
                        xj = xt[:, bass.ds((bp * 2 + bl) * TT + j, 1), :].rearrange("p o d -> p (o d)")
                        V.scalar_tensor_tensor(xj, ps[:, 6 + j % 2, :], y_gate[:, bl:bl + 1], xj,
                                               ALU.mult, ALU.add).then_inc(s_yadd[j % 2], 1)
                    dve.wait_ge(s_yadd[1], LEAD + m * 2 + 2)

        for bp in range(2):
            n0, m0 = bp * (4 * NG), bp * (2 * NG)
            if bp:
                penalties(1)
            lo_q(n0, 0, bank=0)
            lo_k(m0, 0)
            lo_v(m0, 0)
            for i in range(TT):
                row_max(n0, i, 0, 0)
            for i in range(TT):
                inverse_sum(n0, i, 0)
            lo_q(n0 + 1, 1)
            with dve.Fori(0, NG - 1) as g:
                group(bp, n0 + g * 4, m0 + g * 2, False)
            group(bp, n0 + 4 * (NG - 1), m0 + 2 * (NG - 1), True, following=2 if bp == 0 else None)

        ch = Chain(dve, c_dve, base)
        dve.wait_ge(s_din, 32)
        V.tensor_tensor(rw[:, :], rw_raw[:, :], nw_raw[:, :], ALU.mult).then_inc(s_rws, 1)
        dve.wait_ge(s_rwT, 1)
        rwT = ps[:, 5, 0:DT * NE].rearrange("p (n e) -> p n e", e=NE)
        ch.link(V.tensor_copy(rwh[:, :, :], rwT))
        V.tensor_tensor(rwl[:, :, :], rwT, F32R_AS_F32(rwh[:, :, :]), ALU.subtract).then_inc(s_rw, 1)
        base += 1
        dve.wait_ge(s_iota, 1)
        def router_lo(b):
            for t in range(DT):
                dve.wait_ge(s_dxh, b * DT + t + 1)
                V.tensor_tensor(dxl[:, t, :], ps[:, t, :], F32R_AS_F32(dxh[:, t, :]),
                                ALU.subtract).then_inc(s_dxl, 1)

        ch = Chain(dve, c_dve, base)
        norm_stats(ch, 0)
        norm_apply(ch, 0, LN_D, s_dxn, dxn)
        with dve.Fori(0, B - 1) as b:
            ch = Chain(dve, c_dve, base + (b + 1) * 2)
            norm_stats(ch, (b + 1) * TT)
            router_lo(b)
            norm_apply(ch, (b + 1) * TT, LN_D + b + 1, s_dxn, dxn)
        router_lo(B - 1)
        base += 2 * B
        NT = B * TT
        ch = Chain(dve, c_dve, base)
        dve.wait_ge(s_rms, 1)
        ch.link(V.reciprocal(rms_inv[:, :], rms[:, :]))
        dve.wait_ge(s_lg, B)
        ch.link(V.tensor_tensor(lg[:, :, :], ps[:, 5, 0:NT * NE].rearrange("p (n e) -> p n e", e=NE),
                                rms_inv[:, :, None].broadcast_to([P, NT, NE]), ALU.mult))
        ch.link(V.tensor_reduce(lmax[:, :], lg[:, :, :], AX.X, ALU.max))
        V.tensor_tensor(lg[:, :, :], lg[:, :, :], lmax[:, :, None].broadcast_to([P, NT, NE]),
                        ALU.subtract).then_inc(s_lc, 1)
        V.tensor_copy(iota_b[:, :], iota_l[:, :])
        wait_alone(dve, s_lexp, 1, s_passed)
        for i in range(NT):
            ins = V.max(top[:, i, :], pe_[:, i, :])
        ch.link(ins, s_passed)
        for i in range(NT):
            ins = V.max_index(topi[:, i, :], top[:, i, :], pe_[:, i, :])
        ch.link(V.tensor_tensor(den[:, :], top[:, :, 0], top[:, :, 1], ALU.add))
        ch.link(V.tensor_copy(topf[:, :, :], topi[:, :, :]))
        ch.link(V.reciprocal(den[:, :], den[:, :]))
        ch.link(V.tensor_tensor(topw[:, :, :], top[:, :, 0:2], den[:, :, None].broadcast_to([P, NT, 2]), ALU.mult))
        for c in range(2):
            ins = V.tensor_tensor(chosen[:, c, :, :], iota_e[:, None, :].broadcast_to([P, NT, NE]),
                                  topf[:, :, c:c + 1].broadcast_to([P, NT, NE]), ALU.is_equal)
        ins.then_inc(s_cw, 1)
        for c in range(2):
            V.tensor_scalar(combine[:, c, :], topw[:, :, c], gates[:, 3:4], MOE_SCALE, ALU.mult, ALU.mult)

        dve.wait_ge(s_cnt, 1)
        flat = lambda ap: ap.rearrange("p e k -> p (e k)")
        ch.link(V.tensor_copy(total[:, :, :], ps[:, 1, 0:NPC * NE].rearrange("p (k e) -> p e k", e=NE)))
        ch.link(V.tensor_tensor_scan(flat(scan[:, :, :]), flat(keep[:, :, :]), flat(total[:, :, :]), 0.0,
                                     ALU.mult, ALU.add))
        ch.link(V.tensor_scalar(tiles[:, :], scan[:, :, NPC - 1], 1.0 / ROWS, (ROWS - 1.0) / ROWS - 0.498,
                                ALU.mult, ALU.add))
        ch.link(V.tensor_scalar(tiles[:, :], tiles[:, :], MAGIC, -MAGIC, ALU.add, ALU.add))
        ch.link(V.tensor_tensor_scan(tiles_to[:, :], ones[:, 0:NE], tiles[:, :], 0.0, ALU.mult, ALU.add))
        ch.link(V.tensor_tensor(first[:, :], tiles_to[:, :], tiles[:, :], ALU.subtract))
        ch.link(V.tensor_scalar(first[:, :], first[:, :], float(ROWS), None, ALU.mult))
        ch.link(V.tensor_tensor(scan[:, :, :], scan[:, :, :], total[:, :, :], ALU.subtract))
        ch.link(V.tensor_tensor(scan[:, :, :], scan[:, :, :], first[:, :, None].broadcast_to([P, NE, NPC]), ALU.add))
        ch.link(V.tensor_tensor(posm[:, :, :], ps[:, 0, 0:NPC * NE].rearrange("p (k e) -> p k e", e=NE),
                                scan[:, :, :].rearrange("p e k -> p k e"), ALU.add))
        ch.link(V.tensor_tensor(posm[:, :, :], posm[:, :, :], chosen[:, :, :, :].rearrange("p c j e -> p (c j) e"),
                                ALU.mult))
        ch.link(V.tensor_reduce(pos[:, :], posm[:, :, :], AX.X, ALU.add))
        V.tensor_copy(pos_i[:, :, :].rearrange("p c j -> p (c j)"), pos[:, :])
        ch.link(V.tensor_scalar(posq[:, :], pos[:, :], 1.0 / P, -0.498, ALU.mult, ALU.add))
        ch.link(V.tensor_scalar(posq[:, :], posq[:, :], MAGIC, -MAGIC, ALU.add, ALU.add))
        V.tensor_copy(posqb[:, :], posq[:, :])
        ch.link(V.scalar_tensor_tensor(posrb[:, :], posq[:, :], -float(P), pos[:, :], ALU.mult, ALU.add))
        V.tensor_tensor(hot_r[:, :, :], iota_b[:, None, :].broadcast_to([P, NPC, P]),
                        posrb[:, :, None].broadcast_to([P, NPC, P]), ALU.is_equal)
        ch.link(V.tensor_tensor(hot_q[:, :, 0, :], iota_b[:, None, 0:2 * NTILE].broadcast_to([P, NPC, 2 * NTILE]),
                                posqb[:, :, None].broadcast_to([P, NPC, 2 * NTILE]), ALU.is_equal))
        ch.link(V.tensor_scalar(hot_q[:, :, 1, :], hot_q[:, :, 0, :], iota_p[:, :], None, ALU.mult))
        V.tensor_tensor(hot_q[:, :, 0, :], hot_q[:, :, 0, :],
                        iota_j[:, :, :].rearrange("p c j -> p (c j)")[:, :, None].broadcast_to([P, NPC, 2 * NTILE]),
                        ALU.mult).then_inc(s_hot, 1)
        ch.link(V.tensor_tensor(texp[:, :, :], tiles_to[0:1, None, :].broadcast_to([1, NTILE, NE]),
                                iota_l[0:1, 0:NTILE, None].broadcast_to([1, NTILE, NE]), ALU.is_le))
        ch.link(V.tensor_reduce(texf[:, :], texp[:, :, :], AX.X, ALU.add))
        V.tensor_scalar(tile_e[:, :], texf[:, :], NE - 1.0, None, ALU.min)
        dve.wait_ge(s_inverted, 1)
        ch.link(V.tensor_scalar(rtok[:, :], ps[:, 2, 0:2 * NTILE], float(P), None, ALU.mult))
        V.tensor_tensor(row_tok[:, :], rtok[:, :], ps[:, 2, 2 * NTILE:4 * NTILE], ALU.add).then_inc(s_plan, 1)
        dve.wait_ge(s_plan, 1)
        base += ch.n

        def lo_gate_up(t, i):
            e = dve.value_load(tile_e[0:1, bass.ds(t, 1)], min_val=0, max_val=NE - 1)
            for k, (hi, lo, src) in enumerate(((gwh[i], gwl[i], g_raw), (uwh[i], uwl[i], u_raw))):
                dve.wait_ge(s_guhi, 2 * t + k + 1)
                V.tensor_tensor(lo[:, :, :].rearrange("p n f -> p (n f)"),
                                src[:, bass.ds(e, 1), :, :].rearrange("p e n f -> p (e n f)"),
                                F32R_AS_F32(hi[:, :, :].rearrange("p n f -> p (n f)")), ALU.subtract).then_inc(s_gulo, 1)

        def lo_rows(t):
            for k in range(2):
                dve.wait_ge(s_gxh, 2 * t + k + 1)
                part = slice(2 * k, 2 * k + 2)
                V.tensor_tensor(gxl[:, part, :].rearrange("p n r -> p (n r)"), ps[:, k, :],
                                F32R_AS_F32(gxh[:, part, :].rearrange("p n r -> p (n r)")), ALU.subtract).then_inc(s_gxl, 1)

        def gated(t, i, first=False):
            if not first:
                dve.wait_ge(s_aul, t)
            dve.wait_ge(s_sg, t + 1)
            dve.wait_ge(s_gu, 2 * t + 2)
            V.tensor_tensor(au[:, :], ps[:, 3 + 4 * i, :], sg[:, :], ALU.mult).then_inc(s_au, 1)

        def lo_gated(t, i):
            dve.wait_ge(s_auh, t + 1)
            V.tensor_tensor(aul[i][:, :, :].rearrange("p f r -> p (f r)"), au[:, :],
                            F32R_AS_F32(auh[i][:, :, :].rearrange("p f r -> p (f r)")), ALU.subtract).then_inc(s_aul, 1)

        dve.wait_ge(s_xst, 16 * LEAD + 16 * B)
        lo_gate_up(0, 0)
        lo_rows(0)
        lo_gate_up(1, 1)
        gated(0, 0, first=True)
        lo_rows(1)
        lo_gated(0, 0)
        lo_gate_up(2, 0)
        with dve.Fori(0, (NTILE - 3) // 2) as pair:
            for i in range(2):
                t = pair * 2 + i
                gated(t + 1, 1 - i)
                lo_rows(t + 2)
                lo_gated(t + 1, 1 - i)
                lo_gate_up(t + 3, 1 - i)
        t = NTILE - 3
        gated(t + 1, 1)
        lo_rows(t + 2)
        lo_gated(t + 1, 1)
        gated(t + 2, 0)
        lo_gated(t + 2, 0)

        def back_index(b, i):
            V.tensor_copy(pcur[i][:, :], pos_i[:, :, bass.ds(b * TT + i, 1)].rearrange("p c j -> p (c j)")).then_inc(s_pcur, 1)

        def add_rows(b, i, base):
            dve.wait_ge(s_back[i], 32 * b + 32)
            xj = xt[:, bass.ds(b * TT + i, 1), :].rearrange("p o d -> p (o d)")
            for c in range(2):
                ins = V.scalar_tensor_tensor(xj, back[i][c][:, :], combine[:, c, bass.ds(b * TT + i, 1)], xj,
                                             ALU.mult, ALU.add)
                if c == 0:
                    ins.then_inc(c_dve, 1)
                    dve.wait_ge(c_dve, base + b * TT + i + 1)
            ins.then_inc(s_dadd, 1)

        for h in range(2):
            dve.wait_ge(s_yst[h], 16 * LEAD + 16 * NTILE)
        for i in range(TT):
            back_index(0, i)
        with dve.Fori(0, B - 1) as b:
            for i in range(TT):
                add_rows(b, i, base)
                back_index(b + 1, i)
        for i in range(TT):
            add_rows(B - 1, i, base)

    @block.tensor
    def _(pe):
        pe.wait_ge(s_constb, 1)
        pe.wait_ge(s_const, 1)

        def turn_colmax(b, k):
            pe.wait_ge((s_cm, s_cm2)[k], (2 * b + 2, b + 1)[k])
            if k == 0:
                pe.wait_ge(s_h, LEAD + 8 * b)
            for c in range((2 * DT, 2 * CT)[k]):
                src = (cmax, cmax2)[k]
                mm = T.transpose(ps[:, 2 + c // 4, (c % 4) * P:(c % 4 + 1) * P], src[:, c * P:(c + 1) * P], ident[:, :])
            mm.then_inc(s_cmT, 1)

        def smooth_rows(b, k):
            pe.wait_ge(s_dg, 2 * b + k + 1)
            n = (DT, CT)[k]
            T.matmul(ps[:, (2, 3)[k], 0:n * P], ones[:, :], diag_s[:, 0:n, :].rearrange("p n c -> p (n c)"), start=True, stop=True)
            T.matmul(ps[:, (3, 2)[k], 0:n * P], ones[:, :], diag_i[:, 0:n, :].rearrange("p n c -> p (n c)"),
                     start=True, stop=True).then_inc(s_rows, 1)

        def transpose_q(src, base_col, n_out, done):
            for o in range(n_out):
                for j in range(TT):
                    c = base_col + o * S + j * P
                    mm = T.transpose(psb[:, c:c + P], src[:, j, o * P:(o + 1) * P], identb[:, :])
            mm.then_inc(done, 1)

        def turn_qx(b, k):
            pe.wait_ge(s_qx, 2 * b + k + 1)
            pe.wait_ge(s_srow, 2 * b + k + 1)
            transpose_q(qx, 2048, (DT, CT)[k], s_qxT)

        def turn_qw(b, k):
            pe.wait_ge(s_qw, 2 * b + k + 1)
            if k == 0:
                pe.wait_ge(s_qxE, 2 * b + 1)
            transpose_q(qw, (2048, 3072)[k], (DT, CT)[k], s_qwT)

        def scale_row(b, k):
            pe.wait_ge(s_qwE if k == 0 else s_qxE, 2 * b + k + 1)
            T.matmul(ps[:, 2, :], ones[:, :], diag_w[:, :, :].rearrange("p n c -> p (n c)"), start=True, stop=True).then_inc(s_bc, 1)

        def product(b, k):
            pe.wait_ge(s_qwE, 2 * b + k + 1)
            for j in range(TT):
                if j == 1:
                    pe.wait_ge(s_bcE, 2 * b + k + 1)
                elif j >= 2:
                    pe.wait_ge(s_h, LEAD + 8 * b + k * TT + j - 1)
                n_in = (DT, CT)[k]
                for t in range(n_in):
                    mm = T.matmul(ps[:, 3 - j % 2, :], qxT[:, t, j * P:(j + 1) * P], qwT[:, t, :],
                                  start=(t == 0), stop=(t == n_in - 1))
                mm.then_inc(s_mm, 1)

        def ternary_total(m):
            pe.wait_ge(s_wabs, m + 1)
            T.matmul(ps[:, 7, m:m + 1], ones[:, :], wabs[:, m:m + 1], start=True, stop=True).then_inc(s_wtot, 1)

        def turn_ternary(m):
            pe.wait_ge(s_tern, m + 1)
            n_in, n_out = ((HT, DT), (DT, HT))[m]
            src = ternary_bf[:, :].rearrange("p (n d) -> p n d", n=n_in)
            for o in range(n_out):
                k = m * DT + o
                if k >= 2:
                    pe.wait_ge(s_ternE, k - 1)
                for j in range(n_in):
                    c = 4096 + 2048 * (k % 2) + j * P
                    mm = T.transpose(psb[:, c:c + P], src[:, j, o * P:(o + 1) * P], identb[:, :])
                mm.then_inc(s_ternT, 1)

        def three(bank, ah, al, bh, bl_, first, last):
            T.matmul(bank, ah, bh, start=first, stop=False)
            T.matmul(bank, ah, bl_, start=False, stop=False)
            return T.matmul(bank, al, bh, start=False, stop=last)

        def hidden(b, j):
            i = j % 2
            if j < 2:
                pe.wait_ge(s_blo, LEAD + b * DT + DT)
            else:
                pe.wait_ge(s_relu, LEAD + b * HT + j - 1)
            for t in range(DT):
                for part in (bxh, bxl):
                    mm = T.matmul(ps[:, i, :], t_fc[:, t, j * P:(j + 1) * P], part[:, t, :],
                                  start=(t == 0 and part is bxh), stop=(t == DT - 1 and part is bxl))
            mm.then_inc(s_hps, 1)

        def project(b, j):
            i = j % 2
            if j == 0:
                pe.wait_ge(s_bdone, LEAD + b)
            pe.wait_ge(s_sql, b * HT + j + 1)
            for k in range(TT):
                for part in (sqh[i], sql[i]):
                    mm = T.matmul(ps[:, 4 + k, :], part[:, k * P:(k + 1) * P], t_pr[:, j, :],
                                  start=(j == 0 and part is sqh[i]), stop=(j == HT - 1 and part is sql[i]))
            mm.then_inc(s_yuse, 1)

        def turn_normed(b):
            pe.wait_ge(s_bxn, b + 1)
            pe.wait_ge(s_relu, LEAD + b * HT)
            for t in range(DT):
                if t >= 2:
                    pe.wait_ge(s_blo, LEAD + b * DT + t - 1)
                for j in range(TT):
                    mm = T.transpose(ps[:, t % 2, j * P:(j + 1) * P], xn[:, j, t * P:(t + 1) * P], ident[:, :])
                mm.then_inc(s_bxt, 1)

        def next_turn(b, k, banks):
            g = b * CN + k
            if k == 0:
                pe.wait_ge(s_cxn, b + 1)
            if k == DT:
                pe.wait_ge(s_cin, 32 * (b // 2) + 32)
            if g >= len(banks):
                pe.wait_ge(s_cl, g - len(banks) + 1)
            bank = banks[g % len(banks)]
            for j in range(TT):
                src = xn[:, j, k * P:(k + 1) * P] if k < DT else ctx_raw[:, b % 2, j, (k - DT) * P:(k - DT + 1) * P]
                mm = T.transpose(ps[:, bank, j * P:(j + 1) * P], src, ident[:, :])
            mm.then_inc(s_ct, 1)

        def iteration(b, main, feed, ahead, tern=False, first_c=False):
            def slot(j):
                if feed:
                    if j >= 2:
                        project(b - 1, j - 2)
                    hidden(b - 1, j)
                if first_c:
                    for g in FIRST.get(j, ()):
                        next_turn(g // CN, g % CN, FIRST_BANKS)

            slot(0)
            if tern:
                ternary_total(0)
            slot(1)
            if main:
                turn_qx(b, 0)
            slot(2)
            if main:
                turn_qw(b, 0)
            slot(3)
            if main:
                scale_row(b, 0)
            if main:
                product(b, 0)
            if tern:
                turn_ternary(0)
            slot(4)
            if main:
                turn_colmax(b, 1)
            slot(5)
            slot(6)
            if main:
                smooth_rows(b, 1)
            if tern:
                ternary_total(1)
            slot(7)
            slot(8)
            if main:
                turn_qx(b, 1)
                turn_qw(b, 1)
                scale_row(b, 1)
            if main:
                product(b, 1)
            if feed:
                project(b - 1, HT - 3)
            if ahead:
                turn_colmax(b + 1, 0)
            if feed:
                hidden(b - 1, HT - 1)
                project(b - 1, HT - 2)
                project(b - 1, HT - 1)
                pe.wait_ge(s_yuse, LEAD + b * HT)
                pe.nop().then_inc(s_by, 1)
            if ahead:
                smooth_rows(b + 1, 0)
            if main:
                turn_normed(b)
            if tern:
                turn_ternary(1)

        turn_colmax(0, 0)
        smooth_rows(0, 0)
        iteration(0, True, False, True, tern=True)
        with pe.Fori(1, B - 1) as b:
            iteration(b, True, True, True)
        iteration(B - 1, True, True, False)
        iteration(B, False, True, False, first_c=True)

        def kv(grp, m, bl):
            pe.wait_ge(s_w1, LEAD + grp + 1)
            for t in range(CT):
                mm = three(ps[:, 6, :], wkh[:, t, :], wkl[:, t, :], cTh[:, bl, t, :], cTl[:, bl, t, :],
                           t == 0, t == CT - 1)
            mm.then_inc(s_kv, 1)
            for t in range(CT):
                mm = three(ps[:, 7, :], wvh[:, t, :], wvl[:, t, :], cTh[:, bl, t, :], cTl[:, bl, t, :],
                           t == 0, t == CT - 1)
            mm.then_inc(s_kv, 1)

        def v_turn(m):
            pe.wait_ge(s_vT, m + 1)
            for j in range(TT):
                mm = T.transpose(ps[:, 7, j * P:(j + 1) * P], vT[:, j * P:(j + 1) * P], ident[:, :])
            mm.then_inc(s_vt, 1)

        def query_part(n, t, h, bl, bank=4):
            if t == 0:
                pe.wait_ge(s_ql, LEAD + n)
            mm = three(ps[:, bank, :], wqh[:, t, h * DH:(h + 1) * DH], wql[:, t, h * DH:(h + 1) * DH],
                       xTh[:, bl, t, :], xTl[:, bl, t, :], t == 0, t == DT - 1)
            if t == DT - 1:
                mm.then_inc(s_q, 1)

        def query(n, h, bl, bank=4):
            for t in range(DT):
                query_part(n, t, h, bl, bank)

        def scores(n, i, h, bl):
            if i == 0:
                pe.wait_ge(s_ql, LEAD + n + 1)
            pe.wait_ge(s_max[i % 2], LEAD + n * 2 + i // 2)
            three(ps[:, i % 2, :], qh[h][:, i * P:(i + 1) * P], ql[h][:, i * P:(i + 1) * P],
                  kh[bl][:, :], kl[bl][:, :], True, True).then_inc(s_s, 1)

        def turn(n, i, h):
            pe.wait_ge(s_ptl[i % 2], LEAD + n * 2 + i // 2)
            for j in range(TT):
                mm = T.transpose(ps[:, 2 + i % 2, j * P:(j + 1) * P], pr[h][:, j, i * P:(i + 1) * P], ident[:, :])
            mm.then_inc(s_pt, 1)

        def attend_part(n, i, h, bl):
            if i == 0:
                pe.wait_ge(s_ol, LEAD + n)
            pe.wait_ge(s_ptl[i % 2], LEAD + n * 2 + i // 2 + 1)
            mm = three(ps[:, 5, :], vh[bl][:, i, :], vl[bl][:, i, :], pTh[:, i, :], pTl[:, i, :],
                       i == 0, i == TT - 1)
            if i == TT - 1:
                mm.then_inc(s_o, 1)

        def project_out(grp, n, m):
            pe.wait_ge(s_w2, LEAD + grp + 1)
            pe.wait_ge(s_ol, LEAD + n + 1)
            for j in range(TT):
                if j < 2:
                    pe.wait_ge(s_vl, m + 1)
                else:
                    pe.wait_ge(s_yadd[j % 2], LEAD + m * 2 + j // 2)
                for h in range(2):
                    mm = three(ps[:, 6 + j % 2, :], oh[h][:, j * P:(j + 1) * P], ol[h][:, j * P:(j + 1) * P],
                               woh[:, h, :], wol[:, h, :], h == 0, h == 1)
                mm.then_inc(s_y, 1)

        def group(grp, n0, m0, last, following=None):
            for u in range(4):
                n, bl, h = n0 + u, u // 2, u % 2
                pe.wait_ge(s_pn, n + 1)
                nbl = ((u + 1) // 2) % 2
                more_s, more_q = not (last and u == 3), not (last and u >= 2)
                steps = NEXT.get(u, {}) if following is not None else {}
                nb = None if following is None else following + u - 2
                if u == 2 and more_q:
                    pe.wait_ge(s_w1, LEAD + grp + 2)
                if h == 1 and more_s:
                    pe.wait_ge(s_kl, m0 + bl + 2)
                for i in range(TT):
                    if more_s:
                        scores(n + 1, i, 1 - h, nbl)
                    turn(n, i, h)
                    if h == 0 and more_q:
                        query_part(n + 2, i, h, 1 - bl)
                    if h == 1 and i >= 2:
                        attend_part(n, i - 2, h, bl)
                    for k in steps.get(i, ()):
                        next_turn(nb, k, NEXT_BANKS)
                if h == 0:
                    if more_q:
                        m = m0 + u // 2 + 1
                        pe.wait_ge(s_yadd[1], LEAD + m * 2 - 2)
                        kv(grp if u == 0 else grp + 1, m, (u // 2 + 1) % 2)
                    pe.wait_ge(s_vl, m0 + bl + 1)
                    for i in range(TT):
                        attend_part(n, i, h, bl)
                    if more_q:
                        v_turn(m)
                    for k in steps.get(TT, ()):
                        next_turn(nb, k, NEXT_BANKS)
                else:
                    attend_part(n, 2, h, bl)
                    attend_part(n, 3, h, bl)
                    if more_q:
                        query(n + 2, h, 1 - bl)
                    for k in steps.get(TT, ()):
                        next_turn(nb, k, NEXT_BANKS)
                    if steps:
                        pe.wait_ge(s_cl, (nb + 1) * CN)
                    project_out(grp, n, m0 + bl)

        for bp in range(2):
            grp, n0, m0 = bp * NG, bp * (4 * NG), bp * (2 * NG)
            pe.wait_ge(s_cl, (bp + 1) * 2 * CN)
            pe.wait_ge(s_w1, LEAD + grp + 1)
            pe.wait_ge(s_max[0], LEAD + n0 * 2)
            query(n0, 0, 0, bank=0)
            if bp == 0:
                pe.wait_ge(s_bdone, LEAD + B)
            else:
                pe.wait_ge(s_yadd[1], LEAD + m0 * 2)
            kv(grp, m0, 0)
            v_turn(m0)
            pe.wait_ge(s_kl, m0 + 1)
            for i in range(TT):
                scores(n0, i, 0, 0)
            query(n0 + 1, 1, 0)
            with pe.Fori(0, NG - 1) as g:
                group(grp + g, n0 + g * 4, m0 + g * 2, False)
            group(grp + (NG - 1), n0 + 4 * (NG - 1), m0 + 2 * (NG - 1), True, following=2 if bp == 0 else None)

        pe.wait_ge(s_rws, 1)
        for t in range(DT):
            mm = T.transpose(ps[:, 5, t * NE:(t + 1) * NE], rw[:, t * P:(t + 1) * P], ident[0:NE, 0:NE])
        mm.then_inc(s_rwT, 1)
        pe.wait_ge(s_rw, 1)
        for b in range(B):
            pe.wait_ge(s_dxn, b + 1)
            for t in range(DT):
                pe.wait_ge(s_dxl, LEAD + b * DT)
                for j in range(TT):
                    mm = T.transpose(ps[:, t, j * P:(j + 1) * P],
                                     dxn[:, b * TT + j, t * P:(t + 1) * P], ident[:, :])
                mm.then_inc(s_dxt, 1)
            pe.wait_ge(s_dxl, LEAD + b * DT + DT)
            for t in range(DT):
                mm = three(ps[0:NE, 4, :], rwh[:, t, :], rwl[:, t, :], dxh[:, t, :], dxl[:, t, :], t == 0, t == DT - 1)
            mm.then_inc(s_lgT, 1)
            pe.wait_ge(s_lgTE, b + 1)
            for j in range(TT):
                mm = T.transpose(ps[:, 5, (b * TT + j) * NE:(b * TT + j + 1) * NE], lgT[:, j * P:(j + 1) * P], ident[0:NE, 0:NE])
            mm.then_inc(s_lg, 1)

        pe.wait_ge(s_cw, 1)
        pe.wait_ge(s_iota, 1)
        picks = chosen[:, :, :, :].rearrange("p c j e -> p (c j e)")
        T.matmul(ps[:, 0, 0:NPC * NE], before[:, :], picks, start=True, stop=True)
        T.matmul(ps[:, 1, 0:NPC * NE], onesb[:, :], picks, start=True, stop=True).then_inc(s_cnt, 1)
        pe.wait_ge(s_hot, 1)
        for k in range(NPC):
            mm = T.matmul(ps[:, 2, 0:4 * NTILE], hot_r[:, k, :], hot_q[:, k, :, :].rearrange("p c q -> p (c q)"),
                          start=(k == 0), stop=(k == NPC - 1))
        mm.then_inc(s_inverted, 1)

        def turn_rows(t, i, k, early=False):
            pe.wait_ge(s_gat[i], 32 * k + 32)
            if not early:
                pe.wait_ge(s_gxl, 2 * t)
            for d in range(DT):
                for h in range(2):
                    mm = T.transpose(ps[:, d // 2, (d % 2) * ROWS + h * P:(d % 2) * ROWS + (h + 1) * P],
                                     xg[:, i, h, d * P:(d + 1) * P], ident[:, :])
                if d % 2:
                    mm.then_inc(s_gT, 1)

        def gate_up(t, i):
            pe.wait_ge(s_gxl, 2 * t + 2)
            for k, (hi, lo) in enumerate(((gwh[i], gwl[i]), (uwh[i], uwl[i]))):
                pe.wait_ge(s_gulo, 2 * t + k + 1)
                for f in range(FT):
                    for d in range(DT):
                        mm = three(ps[:, 2 + 4 * i + k, f * ROWS:(f + 1) * ROWS], hi[:, d, f * P:(f + 1) * P],
                                   lo[:, d, f * P:(f + 1) * P], gxh[:, d, :], gxl[:, d, :], d == 0, d == DT - 1)
                mm.then_inc(s_gu, 1)

        def down(t, i):
            pe.wait_ge(s_aul, t + 1)
            pe.wait_ge(s_dns, t + 1)
            for h in range(2):
                pe.wait_ge(s_yrow[h], LEAD + t)
                for f in range(FT):
                    mm = three(ps[:, 4 + h, :], auh[i][:, f, h * P:(h + 1) * P], aul[i][:, f, h * P:(h + 1) * P],
                               dwh[:, f, :], dwl[:, f, :], f == 0, f == FT - 1)
                mm.then_inc(s_dy, 1)

        turn_rows(0, 0, 0, early=True)
        gate_up(0, 0)
        turn_rows(1, 1, 0)
        with pe.Fori(0, (NTILE - 3) // 2) as pair:
            for i in range(2):
                t = pair * 2 + i
                gate_up(t + 1, 1 - i)
                turn_rows(t + 2, i, pair + 1)
                down(t, i)
        t = NTILE - 3
        gate_up(t + 1, 1)
        turn_rows(t + 2, 0, (t + 2) // 2)
        down(t, 0)
        gate_up(t + 2, 0)
        down(t + 1, 1)
        down(t + 2, 0)

    persistent.close()
    sems.close()


_INS = ['x', 'fside_BxS2xS2_0', 'ctx_1024', 'mask_BxS2_bf1', 'g_xattn', 'g_ffn', 'L0_ffn_w_fc', 'L0_ffn_w_proj',
        'L1_xattn_Wq', 'L1_xattn_Wk', 'L1_xattn_Wv', 'L1_xattn_Wo', 'L1_ffn_router_w', 'L1_ffn_norm_w',
        'L1_ffn_gate_w', 'L1_ffn_up_w', 'L1_ffn_down_w']


def kernel(**inputs):
    import numpy as _np
    import concourse.bacc as _bacc
    from concourse import mybir as _mybir
    from concourse.bass_utils import run_bass_kernel_spmd as _run

    nc = _bacc.Bacc("TRN2", target_bir_lowering=False, num_devices=1)
    arrays, args = {}, []
    for name in _INS:
        a = _np.ascontiguousarray(inputs[name])
        if a.dtype == _np.bool_:
            a = a.view(_np.uint8)
        arrays[f"in_{name}"] = a
        args.append(nc.dram_tensor(f"in_{name}", a.shape, _mybir.dt.from_np(a.dtype), kind="ExternalInput").ap())
    args.append(nc.dram_tensor("out_y", (B, S, D), FP32, kind="ExternalOutput").ap())
    flamingo_gated_kernel(nc, *args)
    r = _run(nc, [arrays], core_ids=[0])
    return r.results[0]["out_y"]
```
